# Optimizing a Trainium2 kernel written in Bass

```python
import numpy as np
import jax
import jax.numpy as jnp

def _softmax(x, axis=-1):
    return jax.nn.softmax(x, axis=axis)

def _gelu(x):
    return jax.nn.gelu(x, approximate=True)

def _silu(x):
    return jax.nn.silu(x)

def _sigmoid(x):
    return jax.nn.sigmoid(x)

def _layernorm(x, axis=-1, eps=1e-05):
    m = jnp.mean(x, axis=axis, keepdims=True)
    v = jnp.var(x, axis=axis, keepdims=True)
    return (x - m) / jnp.sqrt(v + eps)

def _scatter_add(tgt, idx, src, axis=0):
    return tgt.at[idx].add(src)

def _segment_sum(src, seg, n):
    return jax.ops.segment_sum(src, seg, n)
kernel_name = 'mk_lm_tower_d2_tok_ids512_r4_52d6c5'

def setup_inputs(seed: int=0):
    np.random.seed(seed)
    _w = jnp.asarray

    def _rec_inputs():
        import jax
        import jax.numpy as jnp
        _rk = jax.random.key(seed)
        x = jax.random.randint(jax.random.fold_in(_rk, 1), (4, 1024), 0, 31993, jnp.int32)
        mask_BS_i1_0 = jnp.where(jnp.ones((4, 1024), dtype=bool), 1, 0).astype(jnp.int32)
        return (x, mask_BS_i1_0)
    x, mask_BS_i1_0 = _rec_inputs()

    def _L0_tok_setup():
        import jax, jax.numpy as jnp
        import numpy as np
        L = 2
        E = 128
        H = 8
        D = E // H
        T = 1024
        V = 8000
        WIN = 16
        FF = 4 * E
        EPS = 1e-05

        def layer_norm(x, g, b):
            m = jnp.mean(x, axis=-1, keepdims=True)
            v = jnp.mean(jnp.square(x - m), axis=-1, keepdims=True)
            return (x - m) * jax.lax.rsqrt(v + EPS) * g + b

        def sliding_window_attn(x, mask, Wq, Wk, Wv, Wo, bo):
            B, Tt, _ = x.shape
            q = (x @ Wq).reshape(B, Tt, H, D)
            k = (x @ Wk).reshape(B, Tt, H, D)
            v = (x @ Wv).reshape(B, Tt, H, D)
            idx = jnp.arange(Tt)[:, None] + jnp.arange(-WIN, WIN + 1)[None, :]
            valid = (idx >= 0) & (idx < Tt)
            idxc = jnp.clip(idx, 0, Tt - 1)
            kg = k[:, idxc]
            vg = v[:, idxc]
            scores = jnp.einsum('bthd,btwhd->bhtw', q, kg) / jnp.sqrt(jnp.asarray(D, x.dtype))
            mvalid = valid[None, :, :] & (mask[:, idxc] > 0)
            scores = jnp.where(mvalid[:, None, :, :], scores, jnp.asarray(-1000000000.0, x.dtype))
            a = jax.nn.softmax(scores, axis=-1)
            out = jnp.einsum('bhtw,btwhd->bthd', a, vg).reshape(B, Tt, E)
            return out @ Wo + bo
        key = jax.random.key(seed)
        ks = jax.random.split(key, 12)
        s = 0.02
        return {'tokens': jax.random.randint(ks[0], (2, T), 0, V, dtype=jnp.int32), 'attention_mask': jnp.ones((2, T), dtype=jnp.int32), 'tok_emb': jax.random.normal(ks[1], (V, E), jnp.float32) * s, 'pos_emb': jax.random.normal(ks[2], (T, E), jnp.float32) * s, 'Wq': jax.random.normal(ks[3], (L, E, E), jnp.float32) * s, 'Wk': jax.random.normal(ks[4], (L, E, E), jnp.float32) * s, 'Wv': jax.random.normal(ks[5], (L, E, E), jnp.float32) * s, 'Wo': jax.random.normal(ks[6], (L, E, E), jnp.float32) * s, 'bo': jnp.zeros((L, E), jnp.float32), 'ln1_g': jnp.ones((L, E), jnp.float32), 'ln1_b': jnp.zeros((L, E), jnp.float32), 'ln2_g': jnp.ones((L, E), jnp.float32), 'ln2_b': jnp.zeros((L, E), jnp.float32), 'W1': jax.random.normal(ks[7], (L, E, FF), jnp.float32) * s, 'b1': jnp.zeros((L, FF), jnp.float32), 'W2': jax.random.normal(ks[8], (L, FF, E), jnp.float32) * s, 'b2': jnp.zeros((L, E), jnp.float32)}
    _L0_tok_all = _L0_tok_setup()
    _L0_tok_in = {k: v for k, v in _L0_tok_all.items() if k in ('tok_emb', 'pos_emb', 'Wq', 'Wk', 'Wv', 'Wo', 'bo', 'ln1_g', 'ln1_b', 'ln2_g', 'ln2_b', 'W1', 'b1', 'W2', 'b2')}
    del _L0_tok_all

    def _L0_attn_setup():
        import jax, jax.numpy as jnp
        import numpy as np
        B, L, C, H = (4, 512, 128, 8)
        CH = C // H
        EPS = 1e-05
        key = jax.random.key(seed)
        k1, k2, k3 = jax.random.split(key, 3)
        return {'input_x': jax.random.normal(k1, (B, L, C), dtype=jnp.float32), 'gamma': jnp.ones((C,), dtype=jnp.float32), 'beta': jnp.zeros((C,), dtype=jnp.float32), 'w_xyz': jax.random.normal(k2, (C, 3 * C), dtype=jnp.float32) * 0.02, 'b_xyz': jnp.zeros((3 * C,), dtype=jnp.float32), 'w_end': jax.random.normal(k3, (C, C), dtype=jnp.float32) * 0.02, 'b_end': jnp.zeros((C,), dtype=jnp.float32)}
    _L0_attn_all = _L0_attn_setup()
    _L0_attn_in = {k: v for k, v in _L0_attn_all.items() if k in ('gamma', 'beta', 'w_xyz', 'b_xyz', 'w_end', 'b_end')}
    del _L0_attn_all

    def _L0_ffn_setup():
        import jax, jax.numpy as jnp
        import numpy as np
        DIM = 128
        FF_DIM = 512
        NUM_EXPERTS = 8
        TOP_K = 2
        B, T = (8, 1024)
        key = jax.random.key(seed)
        k_x, k_r, k_w1, k_w2 = jax.random.split(key, 4)
        x = jax.random.normal(k_x, (B, T, DIM), dtype=jnp.float32)
        Wr = jax.random.normal(k_r, (NUM_EXPERTS, DIM), dtype=jnp.float32) * DIM ** (-0.5)
        W1 = jax.random.normal(k_w1, (NUM_EXPERTS, FF_DIM, DIM), dtype=jnp.float32) * DIM ** (-0.5)
        W2 = jax.random.normal(k_w2, (NUM_EXPERTS, DIM, FF_DIM), dtype=jnp.float32) * FF_DIM ** (-0.5)
        return {'x': x, 'Wr': Wr, 'W1': W1, 'W2': W2}
    _L0_ffn_all = _L0_ffn_setup()
    _L0_ffn_in = {k: v for k, v in _L0_ffn_all.items() if k in ('Wr', 'W1', 'W2')}
    del _L0_ffn_all

    def _L1_attn_setup():
        import jax, jax.numpy as jnp
        import numpy as np
        N_HEADS = 8
        N_GROUPS = 4
        B, T, D = (16, 256, 128)
        GH = D // N_HEADS * N_GROUPS

        def _rope_tables(t, d):
            i = np.arange(d // 2, dtype=np.float64)
            theta = 10000.0 ** (-(2.0 * (i - 1.0))) / d
            ang = np.arange(t, dtype=np.float64)[:, None] * theta[None, :]
            return (jnp.asarray(np.cos(ang), jnp.float32), jnp.asarray(np.sin(ang), jnp.float32))

        def _apply_rope(x, cos, sin):
            xe, xo = (x[..., 0::2], x[..., 1::2])
            oe = xe * cos + xo * sin
            oo = -xe * sin + xo * cos
            return jnp.stack([oe, oo], axis=-1).reshape(x.shape)
        key = jax.random.key(seed)
        k1, k2, k3, k4 = jax.random.split(key, 4)
        x = jax.random.normal(k1, (B, T, D), dtype=jnp.float32)
        Wq = jax.random.normal(k2, (D, D), dtype=jnp.float32) * D ** (-0.5)
        Wk = jax.random.normal(k3, (D, GH), dtype=jnp.float32) * D ** (-0.5)
        Wv = jax.random.normal(k4, (D, GH), dtype=jnp.float32) * D ** (-0.5)
        return {'x': x, 'Wq': Wq, 'Wk': Wk, 'Wv': Wv}
    _L1_attn_all = _L1_attn_setup()
    _L1_attn_in = {k: v for k, v in _L1_attn_all.items() if k in ('Wq', 'Wk', 'Wv')}
    del _L1_attn_all

    def _L1_ffn_setup():
        import jax, jax.numpy as jnp
        import numpy as np
        B, S, D = (4, 512, 128)
        I = 96
        E = 16
        K = 2

        def _inv_softplus(v):
            return float(np.log(np.expm1(v)))

        def swiglu5(h, alpha, gate_scale, up_shift, gate_clamp_raw, up_clamp_raw):
            gate_clamp = jax.nn.softplus(gate_clamp_raw)
            up_clamp = jax.nn.softplus(up_clamp_raw)
            g = jnp.clip(h[..., ::2], -gate_clamp, gate_clamp)
            u = jnp.clip(h[..., 1::2], -up_clamp, up_clamp)
            return g * jax.nn.sigmoid(g * alpha) * gate_scale * (u + up_shift)
        key = jax.random.key(seed)
        ks = jax.random.split(key, 10)
        std = 0.02
        raw = _inv_softplus(7.0)
        act = jnp.array([1.702, 1.0, 1.0, raw, raw], dtype=jnp.float32)
        return {'x': jax.random.normal(ks[0], (B, S, D), dtype=jnp.float32), 'gate_w': jax.random.normal(ks[1], (D, E), dtype=jnp.float32) * 0.01, 'gate_b': jnp.zeros((E,), dtype=jnp.float32), 'shared_w1': jax.random.normal(ks[2], (D, 2 * I), dtype=jnp.float32) * std, 'shared_b1': jnp.zeros((2 * I,), dtype=jnp.float32), 'shared_w2': jax.random.normal(ks[3], (I, D), dtype=jnp.float32) * std, 'shared_b2': jnp.zeros((D,), dtype=jnp.float32), 'shared_act': act, 'expert_w1': jax.random.normal(ks[4], (E, D, 2 * I), dtype=jnp.float32) * std, 'expert_b1': jnp.zeros((E, 2 * I), dtype=jnp.float32), 'expert_w2': jax.random.normal(ks[5], (E, I, D), dtype=jnp.float32) * std, 'expert_b2': jnp.zeros((E, D), dtype=jnp.float32), 'expert_act': jnp.tile(act[None, :], (E, 1))}
    _L1_ffn_all = _L1_ffn_setup()
    _L1_ffn_in = {k: v for k, v in _L1_ffn_all.items() if k in ('gate_w', 'gate_b', 'shared_w1', 'shared_b1', 'shared_w2', 'shared_b2', 'shared_act', 'expert_w1', 'expert_b1', 'expert_w2', 'expert_b2', 'expert_act')}
    del _L1_ffn_all
    return {'x': x, 'mask_BS_i1_0': mask_BS_i1_0, 'L0_tok_tok_emb': _L0_tok_in['tok_emb'], 'L0_tok_pos_emb': _L0_tok_in['pos_emb'], 'L0_tok_Wq': _L0_tok_in['Wq'], 'L0_tok_Wk': _L0_tok_in['Wk'], 'L0_tok_Wv': _L0_tok_in['Wv'], 'L0_tok_Wo': _L0_tok_in['Wo'], 'L0_tok_bo': _L0_tok_in['bo'], 'L0_tok_ln1_g': _L0_tok_in['ln1_g'], 'L0_tok_ln1_b': _L0_tok_in['ln1_b'], 'L0_tok_ln2_g': _L0_tok_in['ln2_g'], 'L0_tok_ln2_b': _L0_tok_in['ln2_b'], 'L0_tok_W1': _L0_tok_in['W1'], 'L0_tok_b1': _L0_tok_in['b1'], 'L0_tok_W2': _L0_tok_in['W2'], 'L0_tok_b2': _L0_tok_in['b2'], 'L0_attn_gamma': _L0_attn_in['gamma'], 'L0_attn_beta': _L0_attn_in['beta'], 'L0_attn_w_xyz': _L0_attn_in['w_xyz'], 'L0_attn_b_xyz': _L0_attn_in['b_xyz'], 'L0_attn_w_end': _L0_attn_in['w_end'], 'L0_attn_b_end': _L0_attn_in['b_end'], 'L0_ffn_Wr': _L0_ffn_in['Wr'], 'L0_ffn_W1': _L0_ffn_in['W1'], 'L0_ffn_W2': _L0_ffn_in['W2'], 'L1_attn_Wq': _L1_attn_in['Wq'], 'L1_attn_Wk': _L1_attn_in['Wk'], 'L1_attn_Wv': _L1_attn_in['Wv'], 'L1_ffn_gate_w': _L1_ffn_in['gate_w'], 'L1_ffn_gate_b': _L1_ffn_in['gate_b'], 'L1_ffn_shared_w1': _L1_ffn_in['shared_w1'], 'L1_ffn_shared_b1': _L1_ffn_in['shared_b1'], 'L1_ffn_shared_w2': _L1_ffn_in['shared_w2'], 'L1_ffn_shared_b2': _L1_ffn_in['shared_b2'], 'L1_ffn_shared_act': _L1_ffn_in['shared_act'], 'L1_ffn_expert_w1': _L1_ffn_in['expert_w1'], 'L1_ffn_expert_b1': _L1_ffn_in['expert_b1'], 'L1_ffn_expert_w2': _L1_ffn_in['expert_w2'], 'L1_ffn_expert_b2': _L1_ffn_in['expert_b2'], 'L1_ffn_expert_act': _L1_ffn_in['expert_act']}

def reference(x, mask_BS_i1_0, L0_tok_tok_emb, L0_tok_pos_emb, L0_tok_Wq, L0_tok_Wk, L0_tok_Wv, L0_tok_Wo, L0_tok_bo, L0_tok_ln1_g, L0_tok_ln1_b, L0_tok_ln2_g, L0_tok_ln2_b, L0_tok_W1, L0_tok_b1, L0_tok_W2, L0_tok_b2, L0_attn_gamma, L0_attn_beta, L0_attn_w_xyz, L0_attn_b_xyz, L0_attn_w_end, L0_attn_b_end, L0_ffn_Wr, L0_ffn_W1, L0_ffn_W2, L1_attn_Wq, L1_attn_Wk, L1_attn_Wv, L1_ffn_gate_w, L1_ffn_gate_b, L1_ffn_shared_w1, L1_ffn_shared_b1, L1_ffn_shared_w2, L1_ffn_shared_b2, L1_ffn_shared_act, L1_ffn_expert_w1, L1_ffn_expert_b1, L1_ffn_expert_w2, L1_ffn_expert_b2, L1_ffn_expert_act):
    import jax
    import jax.numpy as jnp

    def _L0_tok_ref(tokens, attention_mask, tok_emb, pos_emb, Wq, Wk, Wv, Wo, bo, ln1_g, ln1_b, ln2_g, ln2_b, W1, b1, W2, b2):
        import jax, jax.numpy as jnp
        import numpy as np
        L = 2
        E = 128
        H = 8
        D = E // H
        T = 1024
        V = 8000
        WIN = 16
        FF = 4 * E
        EPS = 1e-05

        def layer_norm(x, g, b):
            m = jnp.mean(x, axis=-1, keepdims=True)
            v = jnp.mean(jnp.square(x - m), axis=-1, keepdims=True)
            return (x - m) * jax.lax.rsqrt(v + EPS) * g + b

        def sliding_window_attn(x, mask, Wq, Wk, Wv, Wo, bo):
            B, Tt, _ = x.shape
            q = (x @ Wq).reshape(B, Tt, H, D)
            k = (x @ Wk).reshape(B, Tt, H, D)
            v = (x @ Wv).reshape(B, Tt, H, D)
            idx = jnp.arange(Tt)[:, None] + jnp.arange(-WIN, WIN + 1)[None, :]
            valid = (idx >= 0) & (idx < Tt)
            idxc = jnp.clip(idx, 0, Tt - 1)
            kg = k[:, idxc]
            vg = v[:, idxc]
            scores = jnp.einsum('bthd,btwhd->bhtw', q, kg) / jnp.sqrt(jnp.asarray(D, x.dtype))
            mvalid = valid[None, :, :] & (mask[:, idxc] > 0)
            scores = jnp.where(mvalid[:, None, :, :], scores, jnp.asarray(-1000000000.0, x.dtype))
            a = jax.nn.softmax(scores, axis=-1)
            out = jnp.einsum('bhtw,btwhd->bthd', a, vg).reshape(B, Tt, E)
            return out @ Wo + bo
        x = tok_emb[tokens] + pos_emb[None, :, :]
        for l in range(L):
            h = layer_norm(x, ln1_g[l], ln1_b[l])
            x = x + sliding_window_attn(h, attention_mask, Wq[l], Wk[l], Wv[l], Wo[l], bo[l])
            h = layer_norm(x, ln2_g[l], ln2_b[l])
            x = x + (jax.nn.relu(h @ W1[l] + b1[l]) @ W2[l] + b2[l])
        return x

    def _L0_attn_ref(input_x, gamma, beta, w_xyz, b_xyz, w_end, b_end):
        import jax, jax.numpy as jnp
        import numpy as np
        B, L, C, H = (4, 512, 128, 8)
        CH = C // H
        EPS = 1e-05
        b, l, c = input_x.shape
        h = H
        ch = c // h
        scale = 1.0 / np.sqrt(ch).astype(np.float32)
        mu = jnp.mean(input_x, axis=-1, keepdims=True)
        var = jnp.var(input_x, axis=-1, keepdims=True)
        xn = (input_x - mu) / jnp.sqrt(var + EPS) * gamma + beta
        xyz = (xn @ w_xyz + b_xyz).reshape(b, l, 3, h, ch).transpose(2, 0, 3, 1, 4)
        q, k, v = (xyz[0], xyz[1], xyz[2])
        scores = jnp.einsum('bhqc,bhkc->bhqk', q * scale, k)
        attn = jax.nn.softmax(scores, axis=-1)
        z = jnp.einsum('bhqk,bhkc->bhqc', attn, v).transpose(0, 2, 1, 3).reshape(b, l, c)
        z = z @ w_end + b_end
        return input_x + z

    def _L0_ffn_ref(x, Wr, W1, W2):
        import jax, jax.numpy as jnp
        import numpy as np
        DIM = 128
        FF_DIM = 512
        NUM_EXPERTS = 8
        TOP_K = 2
        B, T = (8, 1024)
        Bc, Tc, D = x.shape
        N = Bc * Tc
        xf = x.reshape(N, D)
        logits = xf @ Wr.T
        topk_w, topk_i = jax.lax.top_k(logits, TOP_K)
        gates_k = jax.nn.softmax(topk_w.astype(jnp.float32), axis=-1).astype(x.dtype)
        gates = jnp.zeros((N, NUM_EXPERTS), dtype=x.dtype)
        gates = gates.at[jnp.arange(N)[:, None], topk_i].add(gates_k)
        out = jnp.zeros((N, D), dtype=x.dtype)
        for e in range(NUM_EXPERTS):
            h = jax.nn.gelu(xf @ W1[e].T, approximate=False)
            out = out + gates[:, e:e + 1] * (h @ W2[e].T)
        return out.reshape(Bc, Tc, D)

    def _L1_attn_ref(x, Wq, Wk, Wv):
        import jax, jax.numpy as jnp
        import numpy as np
        N_HEADS = 8
        N_GROUPS = 4
        B, T, D = (16, 256, 128)
        GH = D // N_HEADS * N_GROUPS

        def _rope_tables(t, d):
            i = np.arange(d // 2, dtype=np.float64)
            theta = 10000.0 ** (-(2.0 * (i - 1.0))) / d
            ang = np.arange(t, dtype=np.float64)[:, None] * theta[None, :]
            return (jnp.asarray(np.cos(ang), jnp.float32), jnp.asarray(np.sin(ang), jnp.float32))

        def _apply_rope(x, cos, sin):
            xe, xo = (x[..., 0::2], x[..., 1::2])
            oe = xe * cos + xo * sin
            oo = -xe * sin + xo * cos
            return jnp.stack([oe, oo], axis=-1).reshape(x.shape)
        b, t, c = x.shape
        n, ng = (N_HEADS, N_GROUPS)
        h = c // n
        npg = n // ng
        gh = h * ng
        cq, sq = _rope_tables(t, c)
        ck, sk = _rope_tables(t, gh)
        q = _apply_rope(x @ Wq, cq, sq)
        k = _apply_rope(x @ Wk, ck, sk)
        v = x @ Wv
        q = q.reshape(b, t, ng, npg, h)
        k = k.reshape(b, t, ng, h)
        v = v.reshape(b, t, ng, h)
        att = jnp.einsum('bigph,bjgh->bgpij', q, k) / h ** 0.5
        causal = jnp.tril(jnp.ones((t, t), dtype=bool))
        att = jnp.where(causal, att, -jnp.inf)
        att = jax.nn.softmax(att, axis=-1)
        out = jnp.einsum('bgpij,bjgh->bgpih', att, v)
        return jnp.transpose(out, (0, 2, 1, 3, 4)).reshape(b, t, c)

    def _L1_ffn_ref(x, gate_w, gate_b, shared_w1, shared_b1, shared_w2, shared_b2, shared_act, expert_w1, expert_b1, expert_w2, expert_b2, expert_act):
        import jax, jax.numpy as jnp
        import numpy as np
        B, S, D = (4, 512, 128)
        I = 96
        E = 16
        K = 2

        def _inv_softplus(v):
            return float(np.log(np.expm1(v)))

        def swiglu5(h, alpha, gate_scale, up_shift, gate_clamp_raw, up_clamp_raw):
            gate_clamp = jax.nn.softplus(gate_clamp_raw)
            up_clamp = jax.nn.softplus(up_clamp_raw)
            g = jnp.clip(h[..., ::2], -gate_clamp, gate_clamp)
            u = jnp.clip(h[..., 1::2], -up_clamp, up_clamp)
            return g * jax.nn.sigmoid(g * alpha) * gate_scale * (u + up_shift)
        shape = x.shape
        xf = x.reshape(-1, shape[-1])
        h = xf @ shared_w1 + shared_b1
        t = swiglu5(h, shared_act[0], shared_act[1], shared_act[2], shared_act[3], shared_act[4])
        z = t @ shared_w2 + shared_b2
        gate_logits = xf @ gate_w + gate_b
        gate_probs = jax.nn.softmax(gate_logits, -1)
        w, idx = jax.lax.top_k(gate_probs, K)
        w = w / jnp.sum(w, axis=-1, keepdims=True)
        cw = jnp.sum(jax.nn.one_hot(idx, E, dtype=xf.dtype) * w[..., None], axis=1)
        he = jnp.einsum('nd,edh->enh', xf, expert_w1) + expert_b1[:, None, :]
        a = expert_act
        te = swiglu5(he, a[:, 0, None, None], a[:, 1, None, None], a[:, 2, None, None], a[:, 3, None, None], a[:, 4, None, None])
        oe = jnp.einsum('enh,ehd->end', te, expert_w2) + expert_b2[:, None, :]
        y = jnp.einsum('ne,end->nd', cw, oe)
        return (y + z).reshape(shape)
    h = _L0_tok_ref(x, mask_BS_i1_0, L0_tok_tok_emb, L0_tok_pos_emb, L0_tok_Wq, L0_tok_Wk, L0_tok_Wv, L0_tok_Wo, L0_tok_bo, L0_tok_ln1_g, L0_tok_ln1_b, L0_tok_ln2_g, L0_tok_ln2_b, L0_tok_W1, L0_tok_b1, L0_tok_W2, L0_tok_b2)
    h = h + _L0_attn_ref(_layernorm(h, axis=-1), L0_attn_gamma, L0_attn_beta, L0_attn_w_xyz, L0_attn_b_xyz, L0_attn_w_end, L0_attn_b_end)
    h = h + _L0_ffn_ref(_layernorm(h, axis=-1), L0_ffn_Wr, L0_ffn_W1, L0_ffn_W2)
    h = h + _L1_attn_ref(_layernorm(h, axis=-1), L1_attn_Wq, L1_attn_Wk, L1_attn_Wv)
    h = h + _L1_ffn_ref(_layernorm(h, axis=-1), L1_ffn_gate_w, L1_ffn_gate_b, L1_ffn_shared_w1, L1_ffn_shared_b1, L1_ffn_shared_w2, L1_ffn_shared_b2, L1_ffn_shared_act, L1_ffn_expert_w1, L1_ffn_expert_b1, L1_ffn_expert_w2, L1_ffn_expert_b2, L1_ffn_expert_act)
    return h

_drawn_inputs = setup_inputs


def setup_inputs(seed=0):
    import zlib

    import numpy as np

    out = dict(_drawn_inputs(seed))
    spreads = {'L0_tok_bo': (0.0, 0.1),
     'L0_tok_ln1_g': (1.0, 0.2),
     'L0_tok_ln1_b': (0.0, 0.1),
     'L0_tok_ln2_g': (1.0, 0.2),
     'L0_tok_ln2_b': (0.0, 0.1),
     'L0_tok_b1': (0.0, 0.1),
     'L0_tok_b2': (0.0, 0.1),
     'L0_attn_gamma': (1.0, 0.6),
     'L0_attn_beta': (0.0, 0.404),
     'L0_attn_b_xyz': (0.0, 0.1),
     'L0_attn_b_end': (0.0, 0.1),
     'L1_ffn_gate_b': (0.0, 0.1),
     'L1_ffn_shared_b1': (0.0, 0.8),
     'L1_ffn_shared_b2': (0.0, 0.1),
     'L1_ffn_expert_b1': (0.0, 0.8),
     'L1_ffn_expert_b2': (0.0, 0.27)}
    factors = {'L0_tok_Wq': 5.631,
     'L0_tok_Wk': 5.141,
     'L1_attn_Wq': 8.0,
     'L1_attn_Wk': 8.0,
     'L1_ffn_shared_w1': 3.888,
     'L1_ffn_shared_w2': 3.403,
     'L1_ffn_expert_w1': 5.638,
     'L1_ffn_expert_w2': 4.972}
    for name, (base, spread) in spreads.items():
        noise = np.random.default_rng([zlib.crc32(name.encode()), seed]).standard_normal(out[name].shape)
        drawn = base * np.exp(spread * noise) if base else spread * noise
        out[name] = jnp.asarray(drawn.astype(out[name].dtype))
    for name, factor in factors.items():
        out[name] = (out[name] * factor).astype(out[name].dtype)
    return out
```

```python
from contextlib import ExitStack

import numpy as np

import concourse.bass as bass
from concourse import mybir

F32 = mybir.dt.float32
BF16 = mybir.dt.bfloat16
I32 = mybir.dt.int32
ALU = mybir.AluOpType
ACT = mybir.ActivationFunctionType
AX_X = mybir.AxisListType.X

P = 128
B, T = 4, 1024
N = B * T
CH = 512
NCH = N // CH
H, HD = 8, 16
U = B * H
VOCAB = 8000
LAYERS = 2
FF = 512
FB = FF // P
E0 = 8
E1 = 16
I1 = 96
WIN = 16
EPS = 1e-5
CREDIT = 4
SLOTS = 4
BIG = 3.0e38
OUTSIDE = -1.0e30
MASKED = -4.0e9
MASK_PARTS = (-3992977408.0, -7012352.0, -10240.0)
SCALE = 0.25
Q_PARTS = (0, 0, 1, 1, 0, 2)
K_PARTS = (0, 1, 0, 1, 2, 0)
STACK = 16 * len(Q_PARTS)


def geometry(mode):
    if mode == "window":
        qt, nt, pad = P - 2 * WIN, 12, WIN
        return dict(mode=mode, qt=qt, nt=nt, pad=pad, nq=qt * nt, nk=qt * (nt - 1) + P,
                               q_chunks=[(0, 384), (384, 384), (768, 384)],
                               k_chunks=[(0, 400), (400, 400), (800, 384)],
                               score_rows=STACK + 3, steps=3)
    return dict(mode=mode, qt=P, nt=T // P, pad=0, nq=T, nk=T,
                           q_chunks=[(0, CH), (CH, CH)], k_chunks=[(0, CH), (CH, CH)],
                           score_rows=STACK, steps=T // P)


def geometries():
    out = {}
    before = dict(calls=0, mx=0, red=0, sc=0, items=0, qk=0, chain=0)
    for mode, calls in (("window", LAYERS), ("full", 1), ("causal", 1)):
        g = geometry(mode)
        g["before"] = dict(before)
        n_qk = len(g["q_chunks"]) + len(g["k_chunks"])
        g["splits"] = [4 + (3 if mode == "causal" else 1 if mode == "window" and k >= len(g["q_chunks"]) else 0)
                    for k in range(n_qk)]
        g["links"] = sum(g["splits"]) + (6 if mode == "window" else 0)
        before["calls"] += calls
        before["mx"] += calls * U * len(max_steps(g))
        before["red"] += calls * U * (len(max_steps(g)) + 1)
        before["sc"] += calls * U * g["steps"]
        before["items"] += calls * B * (n_qk + g["nt"] // 4)
        before["qk"] += calls * B * n_qk
        before["chain"] += calls * B * g["links"]
        out[mode] = g
    return out


def max_steps(g):
    if g["mode"] == "window":
        return [(4 * s, 0, CH) for s in range(3)]
    out = []
    for t in range(g["nt"]):
        end = (t + 1) * P if g["mode"] == "causal" else T
        out += [(t, k0, min(CH, end - k0)) for k0 in range(0, end, CH)]
    return out


def at(n, step=1):
    return (n + CREDIT) * step


def build(nc, A):
    with ExitStack() as ctx:
        def sb(name, shape, dt=F32):
            return ctx.enter_context(nc.sbuf_tensor(name, shape, dt))

        credited = []

        def sem(name):
            return ctx.enter_context(nc.semaphore(name))

        def sems(prefix, names, dma=()):
            made = {}
            for n in list(names) + list(dma):
                made[n] = sem(f"{prefix}_{n}")
                credited.append((made[n], 16 if n in dma else 1))
            return made

        def scratch(name, shape, dt=F32):
            return nc.dram_tensor(name, shape, dt, kind="Internal").ap()

        q_stack = scratch("q_stack", (U, STACK, 1152), BF16)
        k_stack = scratch("k_stack", (U, STACK + 3, 1184), BF16)
        v_scr = scratch("v_scr", (B, H, P, 12 * HD))
        num_scr = scratch("num_scr", (U, HD, T))
        den_scr = scratch("den_scr", (U, HD, T))
        g0_scr = scratch("g0_scr", (N // P, E0, P))
        g1_scr = scratch("g1_scr", (N // P, E1, P))

        xT = sb("xT", [P, N])
        hT = sb("hT", [P, N])
        ident = sb("ident", [P, P])
        identb = sb("identb", [P, P], BF16)
        mean_w = sb("mean_w", [P, P])
        band_q = sb("band_q", [P, 4, P], BF16)
        band_k = sb("band_k", [P, 4, P - 2 * WIN], BF16)
        causal_q = sb("causal_q", [P, P], BF16)
        causal_k = sb("causal_k", [P, P], BF16)
        eps_t = sb("eps_t", [P, 1])
        one_t = sb("one_t", [P, 1])
        ones_row = sb("ones_row", [1, P])
        w_tok = sb("w_tok", [P, 4, P])
        w_tok1 = sb("w_tok1", [P, FF])
        w_tok2 = sb("w_tok2", [P, FB, P])
        vec_tok = sb("vec_tok", [P, 6])
        b1_tok = sb("b1_tok", [P, FB])
        w_a0 = sb("w_a0", [P, 4, P])
        vec_a0 = sb("vec_a0", [P, 5])
        bv_a0 = sb("bv_a0", [1, P])
        w_a1 = sb("w_a1", [P, 5, P])
        wr0 = sb("wr0", [P, E0])
        wr1 = sb("wr1", [P, E1])
        br1 = sb("br1", [E1, 1])
        w_e1 = sb("w_e1", [P, E0, FF])
        w_e2 = sb("w_e2", [P, E0, FB, P])

        WORK = 20 * 1024 - 256
        work = sb("work", [P, WORK])

        def area():
            used = [0]

            def take(shape, dt=F32, parts=P):
                n = int(np.prod(shape))
                words = n if dt in (F32, I32) else (n + 1) // 2
                v = work[0:parts, used[0]:used[0] + words]
                used[0] += words
                assert used[0] <= WORK, used[0]
                if dt != F32:
                    v = v.bitcast(dt)
                if len(shape) == 2:
                    v = v.rearrange("p (a b) -> p a b", a=shape[0])
                if len(shape) == 3:
                    v = v.rearrange("p (a b c) -> p a b c", a=shape[0], b=shape[1])
                return v

            return take

        bank = ctx.enter_context(nc.psum_tensor("bank", [P, 8, CH], F32))

        s_const = sem("const_ready")
        s_w = sem("weights_in")
        s_wl = sem("layer_weights_in")
        s_credit = sem("credit_given")
        s_pool = sem("masks_built")
        s_phase = sem("phase_end")
        s_settled = sem("settled")
        GEO = geometries()

        layer_phases = ("ln1", "qkv", "attn", "out", "ln2", "ffn")
        late_phases = ("ln3", "res", "ln4", "qkv0", "attn0", "out0", "ln5", "gate0", "moe",
                       "ln6", "qkv1", "attn1", "out1", "ln7", "gate1", "swi")

        def settled(eng):
            eng.sem_inc(s_settled, 1)

        def phase_end(eng, name, l=0):
            if name == "em":
                k = 1
            elif name in layer_phases:
                k = l * len(layer_phases) + (2 + layer_phases.index(name))
            else:
                k = 2 + LAYERS * len(layer_phases) + late_phases.index(name)
            settled(eng)
            eng.drain().then_inc(s_phase, 1)
            eng.wait_ge(s_phase, 5 * k)
            settled(eng)

        EM = sems("em", ["idx_f", "idx_T", "idx", "posed", "turned", "copied", "chain"], ["misc"])
        gathered = [sem("gathered0"), sem("gathered1")]
        take = area()
        em_tok = take([P], I32, 32)
        em_f = take([P], F32, 32)
        em_neg = take([P], F32, 32)
        em_idx = take([N // P], I32)
        em_cur = [take([1], I32) for _ in range(2)]
        em_row = [take([P]) for _ in range(2)]
        em_sum = [take([P]) for _ in range(2)]
        em_pos = take([T // P, P])

        def em_sp(sp):
            sp.dma_start(em_tok, A["x"].rearrange("b (t p) -> (b t) p", p=P)).then_inc(EM["misc"], 16)
            sp.dma_start(em_pos, A["pos"].rearrange("(t p) d -> p t d", p=P)).then_inc(EM["misc"], 16)

        def em_pool(pool):
            pool.wait_ge(EM["idx"], at(1))
            with pool.Fori(0, B) as b:
                for t in range(T // P):
                    g, n = t % 2, b * (T // P) + t
                    pool.wait_ge(EM["posed"], at(n + 1 - 2))
                    settled(pool)
                    pool.tensor_copy(em_cur[g], em_idx[:, bass.ds(n, 1)]).then_inc(EM["chain"], 1)
                    pool.wait_ge(EM["chain"], at(n + 1))
                    settled(pool)
                    pool.indirect_dma_start(out=em_row[g], out_offset=None, in_=A["tok"],
                                            in_offset=bass.IndirectOffsetOnAxis(ap=em_cur[g], axis=0),
                                            ).then_inc(gathered[g], 16)

        def em_pe(pe):
            pe.wait_ge(EM["idx_f"], at(5))
            pe.transpose(bank[:, 7, 0:32], em_f, ident[0:32, 0:32]).then_inc(EM["idx_T"], 1)
            with pe.Fori(0, B) as b:
                for t in range(T // P):
                    g, n = t % 2, b * (T // P) + t
                    pe.wait_ge(EM["posed"], at(n + 1))
                    pe.wait_ge(EM["copied"], at(n + 1 - 2))
                    pe.transpose(bank[:, g, 0:P], em_sum[g], ident[:, :]).then_inc(EM["turned"], 1)

        def em_dve(v):
            v.wait_ge(EM["misc"], at(2, 16))
            v.tensor_copy(em_f, em_tok).then_inc(EM["idx_f"], 1)
            v.wait_ge(EM["idx_f"], at(1))
            v.tensor_scalar(em_neg, em_f, 0.0, float(VOCAB), ALU.is_lt, ALU.mult).then_inc(EM["idx_f"], 1)
            v.wait_ge(EM["idx_f"], at(2))
            v.tensor_tensor(em_f, em_f, em_neg, ALU.add).then_inc(EM["idx_f"], 1)
            v.wait_ge(EM["idx_f"], at(3))
            v.tensor_scalar(em_f, em_f, 0.0, float(VOCAB - 1), ALU.max, ALU.min).then_inc(EM["idx_f"], 2)
            v.wait_ge(EM["idx_T"], at(1))
            v.tensor_copy(em_idx, bank[:, 7, 0:32]).then_inc(EM["idx"], 1)
            with v.Fori(0, B) as b:
                for t in range(T // P):
                    g, n = t % 2, b * (T // P) + t
                    v.wait_ge(gathered[g], (b * (T // P // 2) + t // 2 + 1) * 16)
                    v.wait_ge(EM["turned"], at(n + 1 - 2))
                    v.tensor_tensor(em_sum[g], em_row[g], em_pos[:, t, :], ALU.add).then_inc(EM["posed"], 1)

        def em_act(act):
            with act.Fori(0, B) as b:
                for t in range(T // P):
                    g, n = t % 2, b * (T // P) + t
                    act.wait_ge(EM["turned"], at(n + 1))
                    act.activation(xT[:, bass.ds(n * P, P)], bank[:, g, 0:P], ACT.Copy).then_inc(EM["copied"], 1)

        take = area()
        ln_c = take([2, CH])
        ln_sq = take([2, CH])
        ln_sd = take([2, CH])
        ln_n = take([2, CH])
        LN_NAMES = ["mean", "cent", "sq", "var", "sd", "rstd", "norm", "done"]

        def ln_pe(pe, S, base, src):
            def mean(n, g, c):
                pe.wait_ge(S["cent"], at(n + 1 - 2))
                pe.matmul(bank[:, g, :], mean_w[:, :], src[:, bass.ds(c * CH, CH)],
                          start=True, stop=True).then_inc(S["mean"], 1)

            def var(n, g):
                pe.wait_ge(S["sq"], at(n + 1))
                pe.wait_ge(S["sd"], at(n + 1 - 2))
                pe.matmul(bank[:, 2 + g, :], mean_w[:, :], ln_sq[:, g, :],
                          start=True, stop=True).then_inc(S["var"], 1)

            with pe.Fori(0, NCH // 2) as i:
                n = base + 2 * i
                mean(n, 0, 2 * i)
                mean(n + 1, 1, 2 * i + 1)
                var(n, 0)
                var(n + 1, 1)

        def ln_dve(v, S, base, src, gained=None):
            def centre(n, g, c):
                v.wait_ge(S["mean"], at(n + 1))
                v.wait_ge(S["norm"], at(n + 1 - 2))
                v.wait_ge(S["sq"], at(n + 1 - 2))
                v.tensor_tensor(ln_c[:, g, :], src[:, bass.ds(c * CH, CH)], bank[:, g, :],
                                ALU.subtract).then_inc(S["cent"], 1)

            def scale(n, g, c):
                v.wait_ge(S["sd"], at(n + 1))
                v.reciprocal(ln_sd[:, g, :], ln_sd[:, g, :]).then_inc(S["rstd"], 1)
                v.wait_ge(S["rstd"], at(n + 1))
                if gained is None:
                    v.tensor_tensor(hT[:, bass.ds(c * CH, CH)], ln_c[:, g, :], ln_sd[:, g, :],
                                    ALU.mult).then_inc(S["norm"], 1)
                else:
                    v.wait_ge(S["done"], at(gained + c + 1 - 2))
                    v.tensor_tensor(ln_n[:, g, :], ln_c[:, g, :], ln_sd[:, g, :],
                                    ALU.mult).then_inc(S["norm"], 1)

            with v.Fori(0, NCH // 2) as i:
                n = base + 2 * i
                centre(n, 0, 2 * i)
                centre(n + 1, 1, 2 * i + 1)
                scale(n, 0, 2 * i)
                scale(n + 1, 1, 2 * i + 1)

        def ln_act(act, S, base, gain):
            with act.Fori(0, NCH // 2) as i:
                n = base + 2 * i
                for g in range(2):
                    act.wait_ge(S["cent"], at(n + g + 1))
                    act.wait_ge(S["var"], at(n + g + 1 - 2))
                    act.activation(ln_sq[:, g, :], ln_c[:, g, :], ACT.Square).then_inc(S["sq"], 1)
                for g in range(2):
                    act.wait_ge(S["var"], at(n + g + 1))
                    act.wait_ge(S["norm"], at(n + g + 1 - 2))
                    act.activation(ln_sd[:, g, :], bank[:, 2 + g, :], ACT.Sqrt,
                                   bias=eps_t[:, 0:1]).then_inc(S["sd"], 1)
                if gain is not None:
                    for g in range(2):
                        act.wait_ge(S["norm"], at(n + g + 1))
                        act.activation(hT[:, bass.ds((2 * i + g) * CH, CH)], ln_n[:, g, :], ACT.Identity,
                                       bias=gain[1], scale=gain[0]).then_inc(S["done"], 1)

        def qkv_buffers(g):
            take = area()
            r = dict()
            r["h"] = take([1184])
            r["f"] = take([3, CH])
            r["f2"] = take([3, CH]) if g["mode"] == "causal" else None
            r["qp"] = take([3, 1152], BF16)
            r["kp"] = take([3, 1184], BF16)
            r["v"] = take([H, 12, HD])
            if g["mode"] == "window":
                r["mi"] = take([T], I32)
                r["m"] = take([1184])
                r["mr"] = take([3, 1184], BF16)
            if g["mode"] == "causal":
                r["cos"] = take([2, T])
                r["sin"] = take([2, T])
            return r

        QB = {m: qkv_buffers(GEO[m]) for m in GEO}
        QK_NAMES = ["h", "mm", "evac", "q", "k", "chain", "m"]
        QK_DMA = ["stored", "mask", "mrows", "rope"]

        def qkv_items(g):
            items = [("q", c, w) for c, w in g["q_chunks"]] + [("k", c, w) for c, w in g["k_chunks"]]
            return items + [("v", t, 4) for t in range(0, g["nt"], 4)]

        def qkv_pool(pool, S, l, g):
            R = QB[g["mode"]]
            with pool.Fori(0, B) as b:
                n = l * B + b
                pool.wait_ge(S["mm"], at(g["before"]["items"] + n * len(qkv_items(g))))
                settled(pool)
                main = pool.tensor_copy(R["h"][:, g["pad"]:g["pad"] + T], hT[:, bass.ds(b * T, T)])
                if g["pad"]:
                    main.then_inc(S["h"], 1)
                    pool.tensor_copy(R["h"][:, 0:g["pad"]],
                                     hT[:, bass.ds(b * T, 1)].broadcast_to([P, g["pad"]])).then_inc(S["h"], 1)
                    pool.tensor_copy(R["h"][:, g["pad"] + T:g["nk"]],
                                     hT[:, bass.ds(b * T + T - 1, 1)].broadcast_to([P, g["nk"] - g["pad"] - T])
                                     ).then_inc(S["h"], 1)
                else:
                    main.then_inc(S["h"], 3)

        def qkv_pe(pe, S, l, g, wq, wk, wv, wq2=None, wk2=None, bv=None):
            R = QB[g["mode"]]
            items = qkv_items(g)
            with pe.Fori(0, B) as b:
                for n, (kind, c, w) in enumerate(items):
                    s = 2 * (n % 3)
                    m = g["before"]["items"] + (l * B + b) * len(items) + n
                    if n == 0:
                        pe.wait_ge(S["h"], at(3 * (g["before"]["calls"] * B + l * B + b + 1)))
                    pe.wait_ge(S["evac"], at(m + 1 - 3))
                    if kind == "v":
                        for t in range(4):
                            hs = R["h"][:, (c + t) * g["qt"]:(c + t) * g["qt"] + P]
                            last = pe.matmul(bank[:, s, t * P:(t + 1) * P], hs, wv,
                                             start=True, stop=bv is None)
                            if bv is not None:
                                last = pe.matmul(bank[:, s, t * P:(t + 1) * P], ones_row[:, :], bv,
                                                 start=False, stop=True)
                    else:
                        c0 = c + (g["pad"] if kind == "q" else 0)
                        last = pe.matmul(bank[:, s, 0:w], wq if kind == "q" else wk, R["h"][:, c0:c0 + w],
                                         start=True, stop=True)
                        if wq2 is not None:
                            last = pe.matmul(bank[:, s + 1, 0:w], wq2 if kind == "q" else wk2,
                                             R["h"][:, c0:c0 + w], start=True, stop=True)
                    last.then_inc(S["mm"], 1)

        def qkv_act(act, S, l, g, bq=0.0, bk=0.0):
            R = QB[g["mode"]]
            items = qkv_items(g)
            with act.Fori(0, B) as b:
                for n, (kind, c, w) in enumerate(items):
                    s = n % 3
                    m = g["before"]["items"] + (l * B + b) * len(items) + n
                    act.wait_ge(S["mm"], at(m + 1))
                    if kind == "v":
                        if c == 0:
                            act.wait_ge(S["stored"], at(13 * (g["before"]["calls"] * B + l * B + b), 16))
                        act.activation(R["v"][:, :, c:c + 4, :],
                                       bank[:, 2 * s, :].rearrange("p (t h d) -> p h t d", t=4, h=H),
                                       ACT.Copy).then_inc(S["evac"], 1)
                    else:
                        n_qk = len(g["q_chunks"]) + len(g["k_chunks"])
                        act.wait_ge(S["q"], at(g["before"]["qk"] + (l * B + b) * n_qk + (n + 1 - 3 if n >= 3 else 0)))
                        last = act.activation(R["f"][:, s, 0:w], bank[:, 2 * s, 0:w], ACT.Identity,
                                              bias=bq if kind == "q" else bk)
                        if g["mode"] == "causal":
                            last = act.activation(R["f2"][:, s, 0:w], bank[:, 2 * s + 1, 0:w], ACT.Copy)
                        last.then_inc(S["evac"], 1)

        def qkv_dve(v, S, l, g):
            R = QB[g["mode"]]
            items = qkv_items(g)
            n_qk = len(g["q_chunks"]) + len(g["k_chunks"])
            if g["mode"] == "causal":
                v.wait_ge(S["rope"], at(2, 16))
            with v.Fori(0, B) as b:
                count = [0]
                base = g["before"]["chain"] + (l * B + b) * g["links"]

                def link(ins):
                    ins.then_inc(S["chain"], 1)
                    count[0] += 1
                    v.wait_ge(S["chain"], at(base + count[0]))

                v.wait_ge(S["stored"], at(13 * (g["before"]["calls"] * B + l * B + b), 16))
                if g["mode"] == "window":
                    v.wait_ge(S["mask"], at(l * B + b + 1, 16))
                    v.wait_ge(S["mrows"], at(H * (l * B + b), 16))
                    link(v.memset(R["m"][:, 0:WIN], 0.0))
                    link(v.memset(R["m"][:, WIN + T:g["nk"]], 0.0))
                    link(v.tensor_scalar(R["m"][:, WIN:WIN + T], R["mi"], 0.0, None, ALU.is_gt))
                    for j in range(3):
                        link(v.tensor_scalar(R["mr"][:, j, :], R["m"], -MASK_PARTS[j], MASK_PARTS[j],
                                             ALU.mult, ALU.add))
                    v.sem_inc(S["m"], 1)
                for n, (kind, c, w) in enumerate(items[:n_qk]):
                    s = n % 3
                    f = R["f"][:, s, 0:w]
                    parts = R["qp"] if kind == "q" else R["kp"]
                    v.wait_ge(S["evac"], at(g["before"]["items"] + (l * B + b) * len(items) + n + 1))
                    if g["mode"] == "causal":
                        f2 = R["f2"][:, s, 0:w]
                        of = 0 if kind == "q" else 1
                        link(v.tensor_tensor(f, f, R["cos"][:, of, c:c + w], ALU.mult))
                        link(v.tensor_tensor(f2, f2, R["sin"][:, of, c:c + w], ALU.mult))
                        link(v.tensor_tensor(f, f, f2, ALU.add))
                    if g["mode"] == "window" and kind == "k":
                        link(v.tensor_tensor(f, f, R["m"][:, c:c + w], ALU.mult))
                    link(v.tensor_copy(parts[:, 0, c:c + w], f))
                    link(v.tensor_tensor(f, f, parts[:, 0, c:c + w], ALU.subtract))
                    link(v.tensor_copy(parts[:, 1, c:c + w], f))
                    link(v.tensor_tensor(parts[:, 2, c:c + w], f, parts[:, 1, c:c + w], ALU.subtract))
                    v.sem_inc(S["q"], 1)

        def qkv_sp(sp, S, l, g):
            R = QB[g["mode"]]
            items = qkv_items(g)
            n_q, n_k = len(g["q_chunks"]), len(g["k_chunks"])
            if g["mode"] == "causal":
                sp.dma_start(R["cos"], A["cos"].rearrange("a p t -> p a t")).then_inc(S["rope"], 16)
                sp.dma_start(R["sin"], A["sin"].rearrange("a p t -> p a t")).then_inc(S["rope"], 16)
            with sp.Fori(0, B) as b:
                n = l * B + b
                if g["mode"] == "window":
                    sp.wait_ge(S["m"], at(n))
                    sp.dma_start(R["mi"], A["mask"][bass.ds(b, 1), :].broadcast_to([P, T])
                                 ).then_inc(S["mask"], 16)
                sp.wait_ge(S["q"], at(g["before"]["qk"] + n * (n_q + n_k) + n_q))
                for j, part in enumerate(Q_PARTS):
                    sp.dma_start(q_stack[bass.ds(b * H, H), j * HD:(j + 1) * HD, 0:g["nq"]],
                                 R["qp"][:, part, 0:g["nq"]]).then_inc(S["stored"], 16)
                sp.wait_ge(S["q"], at(g["before"]["qk"] + (n + 1) * (n_q + n_k)))
                for j, part in enumerate(K_PARTS):
                    sp.dma_start(k_stack[bass.ds(b * H, H), j * HD:(j + 1) * HD, 0:g["nk"]],
                                 R["kp"][:, part, 0:g["nk"]]).then_inc(S["stored"], 16)
                if g["mode"] == "window":
                    for h in range(H):
                        sp.dma_start(k_stack[bass.ds(b * H + h, 1), STACK:STACK + 3, 0:g["nk"]],
                                     R["mr"][0:1, :, 0:g["nk"]]).then_inc(S["mrows"], 16)
                sp.wait_ge(S["evac"], at(g["before"]["items"] + (n + 1) * len(items)))
                sp.dma_start(v_scr[bass.ds(b, 1), :, :, 0:g["nt"] * HD].rearrange("b h p x -> p (b h) x"),
                             R["v"][:, :, 0:g["nt"], :].rearrange("p h t d -> p h (t d)")).then_inc(S["stored"], 16)
            sp.wait_ge(S["stored"], at(13 * (g["before"]["calls"] * B + l * B + B), 16))
            if g["mode"] == "window":
                sp.wait_ge(S["mrows"], at(H * (l * B + B), 16))

        def first(g, l):
            return (g["before"]["calls"] + l) * U

        def attn_buffers(g):
            take = area()
            r = dict()
            r["q"] = take([SLOTS, 1184], BF16)
            r["k"] = take([SLOTS, 1184], BF16)
            r["vc"] = take([SLOTS, 12, HD])
            r["vp"] = take([SLOTS, 12, 3 * HD])
            r["p"] = take([3, 384]) if g["mode"] == "window" else take([4, T])
            r["mh"] = take([SLOTS, 8, 2])
            r["m"] = take([SLOTS, 12])
            r["a"] = take([SLOTS, P])
            r["ap"] = take([SLOTS, 3, P], BF16)
            r["z"] = take([2, 1152])
            return r

        AB = {m: attn_buffers(GEO[m]) for m in GEO}
        AT_NAMES = ["init", "vpad", "mx", "red", "neg", "mt", "split", "sc", "exp", "pv", "oev", "chain"]
        AT_DMA = ["load0", "load1", "load2", "load3", "row0", "row1", "row2", "row3", "z0", "z1"]

        def slot_sem(S, kind, j):
            return {"load": [S["load0"], S["load1"], S["load2"], S["load3"]], "row": [S["row0"], S["row1"], S["row2"], S["row3"]],
                    "z": [S["z0"], S["z1"]]}[kind][j]

        def scrambled(scr):
            return scr.rearrange("u d t -> u (d t)").rearrange("u (s h r) -> u s h r", s=8, h=HD)

        def attn_sp(sp, S, l, g):
            R = AB[g["mode"]]

            def load(i, j):
                u, s = 4 * i + j, slot_sem(S, "load", j)
                rows = g["score_rows"]
                sp.dma_start(R["q"][0:STACK, j, 0:g["nq"]],
                             q_stack[bass.ds(u, 1), :, 0:g["nq"]].rearrange("u r t -> (u r) t")).then_inc(s, 16)
                sp.dma_start(R["k"][0:rows, j, 0:g["nk"]],
                             k_stack[bass.ds(u, 1), 0:rows, 0:g["nk"]].rearrange("u r t -> (u r) t")).then_inc(s, 16)
                sp.dma_start(R["vc"][:, j, 0:g["nt"], :].rearrange("p t d -> p (t d)"),
                             v_flat[bass.ds(u, 1), :, 0:g["nt"] * HD].rearrange("u p x -> (u p) x")).then_inc(s, 16)

            def row(i, j):
                s = slot_sem(S, "row", j)
                sp.wait_ge(S["split"], at(first(g, l) + 4 * i + j + 1))
                for x in range(3):
                    sp.dma_start(R["q"][g["score_rows"] + x:g["score_rows"] + x + 1, j, 0:g["nq"]],
                                 R["ap"][0:g["nt"], j, x, 0:g["qt"]]).then_inc(s, 16)

            def store(i, j):
                u = 4 * i + j
                sp.wait_ge(S["oev"], at(first(g, l) + u + 1))
                for x, dst in ((0, num_scr), (32, den_scr)):
                    if g["mode"] == "causal":
                        sp.dma_start(scrambled(dst)[bass.ds(u, 1), :, :, :].rearrange("u s h r -> (u h) s r"),
                                     R["z"][x:x + HD, j % 2, 0:T].rearrange("p (s r) -> p s r", s=8)
                                     ).then_inc(slot_sem(S, "z", j % 2), 16)
                        continue
                    sp.dma_start(dst[bass.ds(u, 1), :, :].rearrange("u d t -> (u d) t"),
                                 R["z"][x:x + HD, j % 2, 0:T]).then_inc(slot_sem(S, "z", j % 2), 16)

            sp.wait_ge(S["init"], at(5 * (g["before"]["calls"] + l + 1)))
            for j in range(SLOTS):
                load(0, j)
            row(0, 0)
            row(0, 1)
            with sp.Fori(0, U // SLOTS - 1) as i:
                for j in range(SLOTS):
                    row(i + (j + 2) // 4, (j + 2) % 4)
                    store(i, j)
                    sp.wait_ge(S["pv"], at(g["before"]["sc"] + (l * U + 4 * i + j + 1) * g["steps"]))
                    load(i + 1, j)
            i = U // SLOTS - 1
            for j in range(SLOTS):
                if j < 2:
                    row(i, j + 2)
                store(i, j)
            for x in range(2):
                sp.wait_ge(slot_sem(S, "z", x), at(2 * ((g["before"]["calls"] + l) * (U // 2) + U // 2), 16))

        def attn_pool(pool, S, l, g):
            R = AB[g["mode"]]
            fills = ((R["vp"][:, :, :, HD:2 * HD], 0.0), (R["vp"][:, :, :, 2 * HD:3 * HD], 1.0), (R["mh"], -BIG),
                     (R["q"][STACK:STACK + 6, :, :], 1.0), (R["k"][STACK:STACK + 6, :, :], 1.0))
            for x, (tile, value) in enumerate(fills):
                pool.memset(tile, value).then_inc(S["init"], 1)
                pool.wait_ge(S["init"], at(5 * (g["before"]["calls"] + l) + x + 1))
                settled(pool)
            with pool.Fori(0, U // SLOTS) as i:
                for j in range(SLOTS):
                    u = first(g, l) + 4 * i + j
                    pool.wait_ge(slot_sem(S, "load", j), at(3 * ((g["before"]["calls"] + l) * (U // SLOTS) + i + 1), 16))
                    settled(pool)
                    pool.tensor_copy(R["vp"][:, j, 0:g["nt"], 0:HD], R["vc"][:, j, 0:g["nt"], :]).then_inc(S["vpad"], 1)

        def attn_pe(pe, S, l, g):
            R = AB[g["mode"]]
            MS = max_steps(g)
            NS = len(MS) + 1
            sr, er = g["score_rows"], g["score_rows"] + 3
            e_ring = 3 if g["mode"] == "window" else 2

            def max_step(i, j, s):
                u = first(g, l) + 4 * i + j
                if s == 0:
                    pe.wait_ge(slot_sem(S, "load", j), at(3 * ((g["before"]["calls"] + l) * (U // SLOTS) + i + 1), 16))
                pe.wait_ge(S["red"], at(g["before"]["red"] + (l * U + 4 * i + j) * NS + s + 1 - 2))
                t, k0, w = MS[s]
                o = bank[:, (j * NS + s) % 2, :]
                if g["mode"] == "window":
                    pe.matmul(o[0:g["qt"], :], identb[0:g["qt"], 0:g["qt"]], band_q[0:g["qt"], :, :],
                              start=True, stop=False, skip_group_check=True)
                    for x in range(4):
                        c = (t + x) * g["qt"]
                        last = pe.matmul(o[0:g["qt"], x * P:(x + 1) * P], R["q"][0:sr, j, c:c + g["qt"]],
                                         R["k"][0:sr, j, c:c + P], start=False, stop=(x == 3),
                                         skip_group_check=True)
                else:
                    diagonal = g["mode"] == "causal" and k0 + w == (t + 1) * P
                    last = pe.matmul(o[:, 0:w], R["q"][0:sr, j, t * P:(t + 1) * P], R["k"][0:sr, j, k0:k0 + w],
                                     start=True, stop=True)
                    if diagonal:
                        last = pe.matmul(o[:, w - P:w], identb[:, :], causal_q[:, :], start=False, stop=True,
                                         skip_group_check=True)
                last.then_inc(S["mx"], 1)

            def turn_max(i, j):
                u = first(g, l) + 4 * i + j
                pe.wait_ge(S["neg"], at(u + 1))
                pe.wait_ge(S["red"], at(g["before"]["red"] + (l * U + 4 * i + j) * NS + NS - 2))
                pe.transpose(bank[0:g["nt"], (j * NS + NS - 1) % 2, 0:g["qt"]], R["m"][0:g["qt"], j, 0:g["nt"]],
                             ident[0:g["qt"], 0:g["qt"]]).then_inc(S["mt"], 1)

            def score_step(i, j, t):
                u = first(g, l) + 4 * i + j
                m = g["before"]["sc"] + (l * U + 4 * i + j) * g["steps"] + t
                if t == 0:
                    pe.wait_ge(slot_sem(S, "row", j), at(3 * ((g["before"]["calls"] + l) * (U // SLOTS) + i + 1), 16))
                pe.wait_ge(S["exp"], at(m + 1 - e_ring))
                if g["mode"] == "window":
                    o = bank[:, 2 + t, 0:4 * g["qt"]]
                    pe.matmul(o, identb[:, :], band_k[:, :, :], start=True, stop=False, skip_group_check=True)
                    for x in range(4):
                        c = (4 * t + x) * g["qt"]
                        last = pe.matmul(o[:, x * g["qt"]:(x + 1) * g["qt"]], R["k"][0:er, j, c:c + P],
                                         R["q"][0:er, j, c:c + g["qt"]], start=False, stop=(x == 3),
                                         skip_group_check=True)
                else:
                    lo = t * P if g["mode"] == "causal" else 0
                    for half in range(2):
                        c0, c1 = max(lo, half * CH), (half + 1) * CH
                        if c0 >= c1:
                            continue
                        diagonal = g["mode"] == "causal" and c0 == lo
                        o = bank[:, 2 + 2 * (t % 2) + half, :]
                        last = pe.matmul(o[:, c0 - half * CH:CH], R["k"][0:er, j, t * P:(t + 1) * P],
                                         R["q"][0:er, j, c0:c1], start=True, stop=True)
                        if diagonal:
                            last = pe.matmul(o[:, c0 - half * CH:c0 - half * CH + P], identb[:, :],
                                             causal_k[:, :], start=False, stop=True, skip_group_check=True)
                last.then_inc(S["sc"], 1)

            def value_step(i, j, t):
                u = first(g, l) + 4 * i + j
                if t == 0:
                    pe.wait_ge(S["vpad"], at(u + 1))
                    pe.wait_ge(S["oev"], at(u))
                pe.wait_ge(S["exp"], at(g["before"]["sc"] + (l * U + 4 * i + j) * g["steps"] + t + 1))
                if g["mode"] == "window":
                    for x in range(4):
                        last = pe.matmul(bank[0:3 * HD, 5 + t, x * g["qt"]:(x + 1) * g["qt"]],
                                         R["vp"][:, j, 4 * t + x, :], R["p"][:, t, x * g["qt"]:(x + 1) * g["qt"]],
                                         start=True, stop=True)
                else:
                    lo = t * P if g["mode"] == "causal" else 0
                    for half in range(2):
                        c0, c1 = max(lo, half * CH), (half + 1) * CH
                        if c0 >= c1:
                            continue
                        last = pe.matmul(bank[0:3 * HD, 6 + half, c0 - half * CH:CH], R["vp"][:, j, t, :],
                                         R["p"][:, t % 4, c0:c1], start=(t == 0),
                                         stop=(g["mode"] == "causal" or t == g["steps"] - 1),
                                         skip_group_check=True)
                last.then_inc(S["pv"], 1)

            per_step = -(-len(MS) // (g["steps"] - 2)) if g["mode"] != "window" else 2

            def unit(i, j, ahead):
                i2, j2 = i + (j + 2) // 4, (j + 2) % 4
                turn_at = -(-len(MS) // per_step)
                for t in range(g["steps"]):
                    if ahead:
                        for s in range(t * per_step, min((t + 1) * per_step, len(MS))):
                            max_step(i2, j2, s)
                    score_step(i, j, t)
                    if t:
                        value_step(i, j, t - 1)
                    if ahead and t == turn_at:
                        turn_max(i2, j2)
                value_step(i, j, g["steps"] - 1)

            for j in range(2):
                for s in range(len(MS)):
                    max_step(0, j, s)
                turn_max(0, j)
            with pe.Fori(0, U // SLOTS - 1) as i:
                for j in range(SLOTS):
                    unit(i, j, True)
            for j in range(SLOTS):
                unit(U // SLOTS - 1, j, j < 2)

        def attn_act(act, S, l, g):
            R = AB[g["mode"]]
            ring = 3 if g["mode"] == "window" else 4
            with act.Fori(0, U // SLOTS) as i:
                for j in range(SLOTS):
                    for t in range(g["steps"]):
                        m = g["before"]["sc"] + (l * U + 4 * i + j) * g["steps"] + t
                        act.wait_ge(S["sc"], at(m + 1))
                        act.wait_ge(S["pv"], at(m + 1 - ring))
                        if g["mode"] == "window":
                            o, x = R["p"][:, t, :], bank[:, 2 + t, 0:4 * g["qt"]]
                        else:
                            lo = t * P if g["mode"] == "causal" else 0
                            o = R["p"][:, t % 4, lo:T]
                            b0 = 2 + 2 * (t % 2)
                            x = bank[:, b0:b0 + 2, :].rearrange("p a b -> p (a b)")[:, lo:T]
                        act.activation(o, x, ACT.Exp, scale=SCALE).then_inc(S["exp"], 1)

        def attn_dve(v, S, l, g):
            R = AB[g["mode"]]
            MS = max_steps(g)
            NS = len(MS) + 1

            def maxima(i, j):
                u = first(g, l) + 4 * i + j
                for s, (t, k0, w) in enumerate(MS):
                    v.wait_ge(S["mx"], at(g["before"]["mx"] + (l * U + 4 * i + j) * len(MS) + s + 1))
                    o = bank[:, (j * NS + s) % 2, :]
                    if g["mode"] == "window":
                        ins = v.tensor_reduce(R["m"][0:g["qt"], j, t:t + 4],
                                              o[0:g["qt"], :].rearrange("p (t k) -> p t k", t=4), AX_X, ALU.max)
                    else:
                        ins = v.tensor_reduce(R["mh"][:, j, t, k0 // CH:k0 // CH + 1], o[:, 0:w], AX_X, ALU.max)
                    ins.then_inc(S["red"], 1)
                v.wait_ge(S["red"], at(g["before"]["red"] + (l * U + 4 * i + j) * NS + NS - 1))
                if g["mode"] == "window":
                    v.sem_inc(S["neg"], 1)
                else:
                    v.tensor_reduce(R["m"][:, j, 0:g["nt"]], R["mh"][:, j, :, :], AX_X, ALU.max).then_inc(S["neg"], 1)
                v.wait_ge(S["mt"], at(u + 1))
                mt = bank[0:g["nt"], (j * NS + NS - 1) % 2, 0:g["qt"]]
                rest = R["a"][0:g["nt"], j, 0:g["qt"]]
                part = [R["ap"][0:g["nt"], j, x, 0:g["qt"]] for x in range(3)]
                v.tensor_scalar(part[0], mt, -1.0, None, ALU.mult).then_inc(S["chain"], 1)
                v.wait_ge(S["chain"], at(3 * u + 1))
                v.scalar_tensor_tensor(out=rest, in0=mt, scalar=-1.0, in1=part[0], op0=ALU.mult,
                                       op1=ALU.subtract).then_inc(S["red"], 1)
                v.wait_ge(S["red"], at(g["before"]["red"] + (l * U + 4 * i + j) * NS + NS))
                v.tensor_copy(part[1], rest).then_inc(S["chain"], 1)
                v.wait_ge(S["chain"], at(3 * u + 2))
                v.tensor_tensor(part[2], rest, part[1], ALU.subtract).then_inc(S["chain"], 1)
                v.wait_ge(S["chain"], at(3 * u + 3))
                v.sem_inc(S["split"], 1)

            def sums(i, j):
                u = first(g, l) + 4 * i + j
                v.wait_ge(S["pv"], at(g["before"]["sc"] + (l * U + 4 * i + j + 1) * g["steps"]))
                v.wait_ge(slot_sem(S, "z", j % 2), at(2 * ((g["before"]["calls"] + l) * (U // 2) + 2 * i + j // 2), 16))
                if g["mode"] == "window":
                    v.tensor_copy(R["z"][0:3 * HD, j % 2, :].rearrange("p (a b) -> p a b", a=3),
                                  bank[0:3 * HD, 5:8, 0:4 * g["qt"]]).then_inc(S["oev"], 1)
                elif g["mode"] == "causal":
                    v.tensor_copy(R["z"][0:3 * HD, j % 2, 0:T].rearrange("p (s r) -> p s r", s=8),
                                  bank[0:3 * HD, 6:8, :].rearrange("p a b -> p (a b)").rearrange(
                                      "p (r s) -> p s r", s=8)).then_inc(S["oev"], 1)
                else:
                    v.tensor_copy(R["z"][0:3 * HD, j % 2, 0:T],
                                  bank[0:3 * HD, 6:8, :].rearrange("p a b -> p (a b)")).then_inc(S["oev"], 1)

            maxima(0, 0)
            maxima(0, 1)
            with v.Fori(0, U // SLOTS - 1) as i:
                for j in range(SLOTS):
                    maxima(i + (j + 2) // 4, (j + 2) % 4)
                    sums(i, j)
            for j in range(SLOTS):
                if j < 2:
                    maxima(U // SLOTS - 1, j + 2)
                sums(U // SLOTS - 1, j)

        take = area()
        ou_n = take([2, CH])
        ou_d = take([2, CH])
        ou_z = take([2, CH])
        OU_NAMES = ["rec", "z", "mm", "x"]
        OU_DMA = ["in0", "in1"]

        def out_sp(sp, S, l, scramble=False):
            with sp.Fori(0, B) as b:
                for g in range(2):
                    n = l * NCH + 2 * b + g
                    sp.wait_ge(S["z"], at(n + 1 - 2))
                    for buf, src in ((ou_n, num_scr), (ou_d, den_scr)):
                        if scramble:
                            rows = scrambled(src).rearrange("u s h r -> u (s h) r").rearrange(
                                "(b k m) p r -> b m p k r", k=H // 2, m=2)
                            sp.dma_start(buf[:, g, :].rearrange("p (k r) -> p k r", r=P),
                                         rows[bass.ds(b, 1), g, :, :, :].rearrange("b p k r -> (b p) k r")
                                         ).then_inc(S["in0"] if g == 0 else S["in1"], 16)
                            continue
                        sp.dma_start(buf[:, g, :], src[bass.ds(b * H, H), :, g * CH:(g + 1) * CH].rearrange(
                            "u d t -> (u d) t")).then_inc(S["in0"] if g == 0 else S["in1"], 16)

        def out_dve(v, S, l, bias, project=True):
            def z(n, g, c):
                v.wait_ge(S["in0"] if g == 0 else S["in1"], at(2 * (l * (NCH // 2) + c // 2 + 1) if isinstance(c, int)
                                                        else 2 * (l * (NCH // 2) + c + 1), 16))
                v.reciprocal(ou_d[:, g, :], ou_d[:, g, :]).then_inc(S["rec"], 1)
                v.wait_ge(S["rec"], at(n + 1))
                v.wait_ge(S["mm"], at(n + 1 - 2))
                v.tensor_tensor(ou_z[:, g, :], ou_n[:, g, :], ou_d[:, g, :], ALU.mult).then_inc(S["z"], 1)

            def add(n, g, c):
                x = xT[:, bass.ds(c * CH, CH)]
                if project:
                    v.wait_ge(S["mm"], at(n + 1))
                    v.scalar_tensor_tensor(out=x, in0=bank[:, g, :], scalar=bias, in1=x, op0=ALU.add,
                                           op1=ALU.add).then_inc(S["x"], 1)
                else:
                    v.wait_ge(S["z"], at(n + 1))
                    v.tensor_tensor(x, x, ou_z[:, g, :], ALU.add).then_inc(S["mm"], 1)

            with v.Fori(0, B) as b:
                n = l * NCH + 2 * b
                z(n, 0, b)
                z(n + 1, 1, b)
                add(n, 0, 2 * b)
                add(n + 1, 1, 2 * b + 1)

        def out_pe(pe, S, l, wo):
            with pe.Fori(0, B) as b:
                for g in range(2):
                    n = l * NCH + 2 * b + g
                    pe.wait_ge(S["z"], at(n + 1))
                    pe.wait_ge(S["x"], at(n + 1 - 2))
                    pe.matmul(bank[:, g, :], wo, ou_z[:, g, :], start=True, stop=True).then_inc(S["mm"], 1)

        take = area()
        ff_r = take([2, FB, CH])
        FF_NAMES = ["up", "act", "down", "x"]

        def ffn_pe(pe, S, l):
            def up(c, g):
                for k in range(FB):
                    pe.wait_ge(S["act"], at((l * NCH + c) * FB + k + 1 - 4))
                    pe.matmul(bank[:, k, :], w_tok1[:, k * P:(k + 1) * P], hT[:, bass.ds(c * CH, CH)],
                              start=True, stop=True).then_inc(S["up"], 1)

            def down(c, g):
                pe.wait_ge(S["x"], at(l * NCH + c + 1 - 2))
                for k in range(FB):
                    pe.wait_ge(S["act"], at((l * NCH + c) * FB + k + 1))
                    last = pe.matmul(bank[:, 4 + g, :], w_tok2[:, k, :], ff_r[:, g, k, :],
                                     start=(k == 0), stop=(k == FB - 1))
                last.then_inc(S["down"], 1)

            up(0, 0)
            with pe.Fori(0, NCH // 2 - 1) as i:
                up(2 * i + 1, 1)
                down(2 * i, 0)
                up(2 * i + 2, 0)
                down(2 * i + 1, 1)
            up(NCH - 1, 1)
            down(NCH - 2, 0)
            down(NCH - 1, 1)

        def ffn_act(act, S, l):
            with act.Fori(0, NCH // 2) as i:
                for g in range(2):
                    c = l * NCH + 2 * i + g
                    act.wait_ge(S["down"], at(c + 1 - 2))
                    for k in range(FB):
                        act.wait_ge(S["up"], at(c * FB + k + 1))
                        act.activation(ff_r[:, g, k, :], bank[:, k, :], ACT.Relu,
                                       bias=b1_tok[:, k:k + 1]).then_inc(S["act"], 1)

        def ffn_dve(v, S, l):
            with v.Fori(0, NCH // 2) as i:
                for g in range(2):
                    v.wait_ge(S["down"], at(l * NCH + 2 * i + g + 1))
                    x = xT[:, bass.ds((2 * i + g) * CH, CH)]
                    v.scalar_tensor_tensor(out=x, in0=bank[:, 4 + g, :], scalar=vec_tok[:, 5:6], in1=x,
                                           op0=ALU.add, op1=ALU.add).then_inc(S["x"], 1)

        NT_ = N // P
        take = area()
        ga_l = take([2, CH])
        ga_buf = [take([NT_ * E1]) for _ in range(6)]
        ga_m = [take([NT_]) for _ in range(4)]
        ga_out = take([4, P])
        GA_NAMES = ["mm", "lg", "turn", "tok", "chain", "shift", "exp", "gates", "rows", "copied"]
        GA_DMA = ["out"]

        def gate_views(E):
            return [x[:, 0:NT_ * E].rearrange("p (t e) -> p t e", e=E) for x in ga_buf]

        def gate_pe(pe, S, E, wr):
            with pe.Fori(0, NCH // 2) as i:
                for g in range(2):
                    n = 2 * i + g
                    pe.wait_ge(S["lg"], at(n + 1 - 2))
                    pe.matmul(bank[0:E, g, :], wr, hT[:, bass.ds(n * CH, CH)], start=True, stop=True
                              ).then_inc(S["mm"], 1)
                    pe.wait_ge(S["lg"], at(n + 1))
                    pe.wait_ge(S["tok"], at(n + 1 - 2))
                    settled(pe)
                    for t in range(4):
                        last = pe.transpose(bank[:, 2 + g, t * E:(t + 1) * E], ga_l[0:E, g, t * P:(t + 1) * P],
                                            ident[0:E, 0:E])
                    last.then_inc(S["turn"], 1)
            pe.wait_ge(S["gates"], at(1))
            for x in range(NT_ * E // P):
                last = pe.transpose(bank[:, 4, x * P:(x + 1) * P], ga_buf[5][:, x * P:(x + 1) * P], ident[:, :])
            last.then_inc(S["rows"], 1)

        def gate_act(act, S, E, bias):
            with act.Fori(0, NCH // 2) as i:
                for g in range(2):
                    n = 2 * i + g
                    act.wait_ge(S["mm"], at(n + 1))
                    act.wait_ge(S["turn"], at(n + 1 - 2))
                    act.activation(ga_l[0:E, g, :], bank[0:E, g, :], ACT.Identity, bias=bias).then_inc(S["lg"], 1)
            key = gate_views(E)[1]
            act.wait_ge(S["shift"], at(1))
            act.activation(key, key, ACT.Exp).then_inc(S["exp"], 1)

        def gate_dve(v, S, E):
            lt, key, order, first, second, w = gate_views(E)
            count = [0]

            def link(ins):
                ins.then_inc(S["chain"], 1)
                count[0] += 1
                v.wait_ge(S["chain"], at(count[0]))

            def wide(x):
                return x.unsqueeze(2).broadcast_to([P, NT_, E])

            def pick(one, source, top):
                link(v.tensor_reduce(top, source, AX_X, ALU.max))
                link(v.tensor_tensor(key, source, wide(top), ALU.is_equal))
                link(v.tensor_tensor(key, key, order, ALU.mult))
                link(v.tensor_reduce(ga_m[2], key, AX_X, ALU.max))
                link(v.tensor_tensor(one, order, wide(ga_m[2]), ALU.is_equal))

            for e in range(E):
                link(v.memset(order[:, :, e:e + 1], float(E - e)))
            with v.Fori(0, NCH // 2) as i:
                for g in range(2):
                    n = 2 * i + g
                    v.wait_ge(S["turn"], at(n + 1))
                    v.tensor_copy(ga_buf[0][:, bass.ds(n * 4 * E, 4 * E)], bank[:, 2 + g, 0:4 * E]
                                  ).then_inc(S["tok"], 1)
            v.wait_ge(S["tok"], at(NCH))
            pick(first, lt, ga_m[0])
            link(v.tensor_scalar(w, first, -1.0, 1.0, ALU.mult, ALU.add))
            link(v.tensor_tensor(w, w, lt, ALU.mult))
            link(v.scalar_tensor_tensor(out=w, in0=first, scalar=-BIG, in1=w, op0=ALU.mult, op1=ALU.add))
            pick(second, w, ga_m[1])
            link(v.tensor_tensor(w, first, second, ALU.add))
            link(v.tensor_tensor(key, lt, wide(ga_m[0]), ALU.subtract))
            v.sem_inc(S["shift"], 1)
            v.wait_ge(S["exp"], at(1))
            link(v.tensor_tensor(key, key, w, ALU.mult))
            link(v.tensor_reduce(ga_m[2], key, AX_X, ALU.add))
            link(v.reciprocal(ga_m[3], ga_m[2]))
            v.tensor_tensor(w, key, wide(ga_m[3]), ALU.mult).then_inc(S["gates"], 1)
            v.wait_ge(S["rows"], at(1))
            n = NT_ * E // P
            v.tensor_copy(ga_out[:, 0:n, :], bank[:, 4, 0:n * P].rearrange("p (a b) -> p a b", a=n)
                          ).then_inc(S["copied"], 1)

        def gate_sp(sp, S, E, scr):
            sp.wait_ge(S["copied"], at(1))
            sp.dma_start(scr.rearrange("t e p -> (t e) p").rearrange("(x r) p -> r x p", r=P),
                         ga_out[:, 0:NT_ * E // P, :]).then_inc(S["out"], 16)
            sp.wait_ge(S["out"], at(1, 16))

        take = area()
        mo_r = take([2, FB, CH])
        mo_g = take([4, CH])
        mo_t = take([2, CH])
        MO_NAMES = ["up", "act", "down", "t", "x"]
        MO_DMA = ["g0", "g1", "g2", "g3"]

        def moe_sp(sp, S):
            with sp.Fori(0, NCH) as c:
                for e in range(E0):
                    sp.wait_ge(S["t"], at(c * E0 + e + 1 - 4))
                    sp.dma_start(mo_g[:, e % 4, :].rearrange("p (t q) -> p t q", t=4),
                                 g0_scr[bass.ds(c * 4, 4), e, :].partition_broadcast(P)
                                 ).then_inc([S["g0"], S["g1"], S["g2"], S["g3"]][e % 4], 16)

        def moe_pe(pe, S):
            def up(c, e):
                for k in range(FB):
                    pe.wait_ge(S["act"], at((c * E0 + e) * FB + k + 1 - 4))
                    pe.matmul(bank[:, k, :], w_e1[:, e, k * P:(k + 1) * P], hT[:, bass.ds(c * CH, CH)],
                              start=True, stop=True).then_inc(S["up"], 1)

            def down(c, e):
                n = c * E0 + e
                pe.wait_ge(S["t"], at(n + 1 - 2))
                for k in range(FB):
                    pe.wait_ge(S["act"], at(n * FB + k + 1))
                    last = pe.matmul(bank[:, 4 + e % 2, :], w_e2[:, e, k, :], mo_r[:, e % 2, k, :],
                                     start=(k == 0), stop=(k == FB - 1))
                last.then_inc(S["down"], 1)

            up(0, 0)
            with pe.Fori(0, NCH - 1) as c:
                for e in range(E0):
                    if e < E0 - 1:
                        up(c, e + 1)
                    else:
                        up(c + 1, 0)
                    down(c, e)
            for e in range(E0):
                if e < E0 - 1:
                    up(NCH - 1, e + 1)
                down(NCH - 1, e)

        def moe_act(act, S):
            with act.Fori(0, NCH) as c:
                for e in range(E0):
                    n = c * E0 + e
                    act.wait_ge(S["down"], at(n + 1 - 2))
                    for k in range(FB):
                        act.wait_ge(S["up"], at(n * FB + k + 1))
                        act.activation(mo_r[:, e % 2, k, :], bank[:, k, :], ACT.Gelu).then_inc(S["act"], 1)

        def moe_dve(v, S):
            with v.Fori(0, NCH) as c:
                for e in range(E0):
                    n = c * E0 + e
                    v.wait_ge(S["down"], at(n + 1))
                    v.wait_ge([S["g0"], S["g1"], S["g2"], S["g3"]][e % 4], at(c * 2 + e // 4 + 1, 16))
                    v.wait_ge(S["x"], at(n + 1 - 2))
                    v.tensor_tensor(mo_t[:, e % 2, :], bank[:, 4 + e % 2, :], mo_g[:, e % 4, :],
                                    ALU.mult).then_inc(S["t"], 1)
                    v.wait_ge(S["t"], at(n + 1))
                    x = xT[:, bass.ds(c * CH, CH)]
                    v.tensor_tensor(x, x, mo_t[:, e % 2, :], ALU.add).then_inc(S["x"], 1)

        E2 = E1 + 1
        take = area()
        sw_w = take([E2, 2 * I1])
        sw_w2 = take([E2, P])
        sw_b = take([2, E2])
        sw_p = take([5, E2])
        sw_c = take([2, E2])
        sw_n = take([2, E2])
        sw_eb = take([P])
        sw_cw = take([CH])
        sw_g = take([4, CH])
        sw_gt = take([2, CH])
        sw_gg = take([3, CH])
        sw_sg = take([2, CH])
        sw_ut = take([2, CH])
        sw_u = take([3, CH])
        sw_t = take([2, CH])
        sw_o = take([3, CH])
        SW_NAMES = ["prep", "ones", "hg", "hu", "gt", "ut", "gg", "clip", "u", "used", "sg", "t", "o", "down",
                    "x"]
        SW_DMA = ["w", "g0", "g1", "g2", "g3", "cw"]

        def ring(c, e, r):
            if e >= r:
                return at(c * E2 + e + 1 - r)
            last = max(x for x in range(E2) if x % r == e)
            return at(c * E2 + last + 1 - E2)

        def swi_sp(sp, S):
            for dst, src in ((sw_w, A["sw1"]), (sw_w2[0:I1], A["sw2"]), (sw_b[0:I1], A["sb1"]),
                             (sw_p[0:I1], A["sact"].partition_broadcast(I1)), (sw_eb[0:E2], A["sb2"])):
                sp.dma_start(dst, src).then_inc(S["w"], 16)
            sp.wait_ge(S["ones"], at(1))
            with sp.Fori(0, NCH) as c:
                sp.wait_ge(S["down"], at(c * E2))
                sp.dma_start(sw_cw[0:E1, :].rearrange("e (t q) -> e t q", t=4),
                             g1_scr[bass.ds(c * 4, 4), :, :].rearrange("t e q -> e t q")).then_inc(S["cw"], 16)
                for e in range(E1):
                    sp.wait_ge(S["used"], at(c * E1 + e + 1 - 4))
                    sp.dma_start(sw_g[0:I1, e % 4, :].rearrange("p (t q) -> p t q", t=4),
                                 g1_scr[bass.ds(c * 4, 4), e, :].partition_broadcast(I1)
                                 ).then_inc([S["g0"], S["g1"], S["g2"], S["g3"]][e % 4], 16)

        def swi_pool(pool, S):
            pool.memset(sw_cw[0:E2, :], 1.0).then_inc(S["ones"], 1)
            pool.wait_ge(S["prep"], at(5))
            with pool.Fori(0, NCH) as c:
                for e in range(E2):
                    n = c * E2 + e
                    pool.wait_ge(S["gt"], at(n + 1))
                    pool.wait_ge(S["t"], ring(c, e, 3))
                    settled(pool)
                    pool.tensor_scalar(sw_gg[0:I1, e % 3, :], sw_gt[0:I1, e % 2, :], sw_n[0:I1, 0, e:e + 1],
                                       None, ALU.max).then_inc(S["gg"], 1)
                    pool.wait_ge(S["ut"], at(n + 1))
                    pool.wait_ge(S["o"], ring(c, e, 3))
                    settled(pool)
                    clip = pool.tensor_scalar(sw_u[0:I1, e % 3, :], sw_ut[0:I1, e % 2, :],
                                              sw_n[0:I1, 1, e:e + 1], sw_p[0:I1, 2, e:e + 1], ALU.max, ALU.add)
                    clip.then_inc(S["clip"], 1)
                    pool.wait_ge(S["clip"], at(n + 1))
                    if e < E1:
                        pool.wait_ge([S["g0"], S["g1"], S["g2"], S["g3"]][e % 4], at(c * 4 + e // 4 + 1, 16))
                        pool.tensor_tensor(sw_u[0:I1, e % 3, :], sw_u[0:I1, e % 3, :], sw_g[0:I1, e % 4, :],
                                           ALU.mult).then_inc(S["u"], 1)
                        pool.wait_ge(S["u"], at(n + 1))
                        pool.sem_inc(S["used"], 1)
                    else:
                        pool.sem_inc(S["u"], 1)

        def swi_pe(pe, S):
            def hidden(c, e):
                n = c * E2 + e
                for x, (done, read) in enumerate(((S["hg"], S["gt"]), (S["hu"], S["ut"]))):
                    pe.wait_ge(read, ring(c, e, 2))
                    pe.matmul(bank[0:I1, 2 * x + e % 2, :], sw_w[:, e, x * I1:(x + 1) * I1],
                              hT[:, bass.ds(c * CH, CH)], start=True, stop=True).then_inc(done, 1)
                del n

            def down(c, e):
                if e == 0:
                    pe.wait_ge(S["x"], at(c))
                    pe.wait_ge(S["cw"], at(c + 1, 16))
                    pe.matmul(bank[:, 4, :], sw_eb[0:E2, :], sw_cw[0:E2, :], start=True, stop=False)
                pe.wait_ge(S["o"], at(c * E2 + e + 1))
                last = pe.matmul(bank[:, 4, :], sw_w2[0:I1, e, :], sw_o[0:I1, e % 3, :],
                                 start=False, stop=(e == E2 - 1))
                last.then_inc(S["down"], 1)

            def chunk(c, more):
                for e in range(E2):
                    if e + 2 < E2:
                        hidden(c, e + 2)
                    elif more:
                        hidden(c + 1, e + 2 - E2)
                    down(c, e)

            pe.wait_ge(S["w"], at(5, 16))
            hidden(0, 0)
            hidden(0, 1)
            with pe.Fori(0, NCH - 1) as c:
                chunk(c, True)
            chunk(NCH - 1, False)

        def swi_act(act, S):
            raw = sw_p[0:I1, 3:5, :]
            act.wait_ge(S["prep"], at(1))
            act.activation(sw_c[0:I1], sw_c[0:I1], ACT.Exp, scale=-1.0).then_inc(S["prep"], 1)
            act.wait_ge(S["prep"], at(2))
            act.activation(sw_c[0:I1], sw_c[0:I1], ACT.Ln, bias=one_t[0:I1, 0:1]).then_inc(S["prep"], 1)
            del raw
            with act.Fori(0, NCH) as c:
                for e in range(E2):
                    act.wait_ge(S["gg"], at(c * E2 + e + 1))
                    act.wait_ge(S["t"], ring(c, e, 2))
                    act.activation(sw_sg[0:I1, e % 2, :], sw_gg[0:I1, e % 3, :], ACT.Sigmoid,
                                   scale=sw_p[0:I1, 0, e:e + 1]).then_inc(S["sg"], 1)

        def swi_dve(v, S):
            raw = sw_p[0:I1, 3:5, :]
            v.wait_ge(S["w"], at(5, 16))
            v.scalar_tensor_tensor(out=sw_c[0:I1], in0=raw, scalar=-1.0, in1=raw, op0=ALU.mult,
                                   op1=ALU.max).then_inc(S["prep"], 1)
            v.wait_ge(S["prep"], at(3))
            v.scalar_tensor_tensor(out=sw_c[0:I1], in0=raw, scalar=0.0, in1=sw_c[0:I1], op0=ALU.max,
                                   op1=ALU.add).then_inc(S["prep"], 1)
            v.wait_ge(S["prep"], at(4))
            v.tensor_scalar(sw_n[0:I1], sw_c[0:I1], -1.0, None, ALU.mult).then_inc(S["prep"], 1)

            def clip_above(c, e):
                n = c * E2 + e
                for x, (ready, done, read, dst) in enumerate(((S["hg"], S["gt"], S["gg"], sw_gt),
                                                              (S["hu"], S["ut"], S["clip"], sw_ut))):
                    v.wait_ge(ready, at(n + 1))
                    v.wait_ge(read, ring(c, e, 2))
                    v.tensor_scalar(dst[0:I1, e % 2, :], bank[0:I1, 2 * x + e % 2, :], sw_b[0:I1, x, e:e + 1],
                                    sw_c[0:I1, x, e:e + 1], ALU.add, ALU.min).then_inc(done, 1)

            def product(c, e):
                n = c * E2 + e
                v.wait_ge(S["sg"], at(n + 1))
                v.scalar_tensor_tensor(out=sw_t[0:I1, e % 2, :], in0=sw_sg[0:I1, e % 2, :],
                                       scalar=sw_p[0:I1, 1, e:e + 1], in1=sw_gg[0:I1, e % 3, :],
                                       op0=ALU.mult, op1=ALU.mult).then_inc(S["t"], 1)
                v.wait_ge(S["t"], at(n + 1))
                v.wait_ge(S["u"], at(n + 1))
                v.wait_ge(S["down"], ring(c, e, 3))
                v.tensor_tensor(sw_o[0:I1, e % 3, :], sw_t[0:I1, e % 2, :], sw_u[0:I1, e % 3, :],
                                ALU.mult).then_inc(S["o"], 1)

            def chunk(c, more):
                for e in range(E2):
                    if e + 1 < E2:
                        clip_above(c, e + 1)
                    elif more:
                        clip_above(c + 1, 0)
                    product(c, e)
                v.wait_ge(S["down"], at((c + 1) * E2))
                x = xT[:, bass.ds(c * CH, CH)]
                v.tensor_tensor(x, x, bank[:, 4, :], ALU.add).then_inc(S["x"], 1)

            clip_above(0, 0)
            with v.Fori(0, NCH - 1) as c:
                chunk(c, True)
            chunk(NCH - 1, False)

        take = area()
        fi_s = take([2, CH])
        fi_o = take([2, CH])
        FI = sems("fi", ["staged", "turned", "copied"], ["out0", "out1"])

        def fin_dve(v):
            with v.Fori(0, NCH // 2) as i:
                for g in range(2):
                    v.wait_ge(FI["turned"], at(2 * i + g + 1 - 2))
                    v.tensor_copy(fi_s[:, g, :], xT[:, bass.ds((2 * i + g) * CH, CH)]).then_inc(FI["staged"], 1)

        def fin_pe(pe):
            with pe.Fori(0, NCH // 2) as i:
                for g in range(2):
                    pe.wait_ge(FI["staged"], at(2 * i + g + 1))
                    pe.wait_ge(FI["copied"], at(2 * i + g + 1 - 2))
                    for t in range(4):
                        last = pe.transpose(bank[:, g, t * P:(t + 1) * P], fi_s[:, g, t * P:(t + 1) * P], ident[:, :])
                    last.then_inc(FI["turned"], 1)

        def fin_act(act):
            with act.Fori(0, NCH // 2) as i:
                for g in range(2):
                    act.wait_ge(FI["turned"], at(2 * i + g + 1))
                    act.wait_ge(FI["out0"] if g == 0 else FI["out1"], at(i, 16))
                    act.activation(fi_o[:, g, :], bank[:, g, :], ACT.Copy).then_inc(FI["copied"], 1)

        def fin_sp(sp):
            with sp.Fori(0, NCH // 2) as i:
                for g in range(2):
                    sp.wait_ge(FI["copied"], at(2 * i + g + 1))
                    sp.dma_start(A["out"][bass.ds((2 * i + g) * CH, CH), :].rearrange("(t q) d -> q t d", q=P),
                                 fi_o[:, g, :].rearrange("p (t d) -> p t d", t=4)
                                 ).then_inc(FI["out0"] if g == 0 else FI["out1"], 16)
            sp.wait_ge(FI["out0"], at(NCH // 2, 16))
            sp.wait_ge(FI["out1"], at(NCH // 2, 16))

        win, full, causal = (GEO[m] for m in ("window", "full", "causal"))
        LN = sems("ln", LN_NAMES)
        QKV = sems("qkv", QK_NAMES, QK_DMA)
        AT = sems("attn", AT_NAMES, AT_DMA)
        OT, O0, O1 = (sems(x, OU_NAMES, OU_DMA) for x in ("out_tok", "out_a0", "out_a1"))
        FT = sems("ffn_tok", FF_NAMES)
        G0, G1 = (sems(x, GA_NAMES, GA_DMA) for x in ("gate0", "gate1"))
        MO = sems("moe", MO_NAMES, MO_DMA)
        SW = sems("swi", SW_NAMES, SW_DMA)
        RE = sems("res", ["x"])
        v_flat = v_scr.rearrange("b h p x -> (b h) p x")
        N_W = 11
        ln_at = lambda k: NCH * k

        def vt(i):
            return vec_tok[:, i:i + 1]

        def va(i):
            return vec_a0[:, i:i + 1]

        def started(eng):
            eng.wait_ge(s_credit, 1)
            eng.wait_ge(s_const, 2)

        block = ctx.enter_context(nc.Block())

        @block.sync
        def _(sp):
            started(sp)
            em_sp(sp)
            for dst, src in ((w_a0, A["a0_w"]), (vec_a0, A["a0_v"]), (bv_a0, A["a0_bv"]), (w_a1, A["a1_w"]),
                             (wr0, A["wr0"]), (wr1, A["wr1"]), (br1, A["br1"]), (w_e1, A["e1"]), (w_e2, A["e2"])):
                sp.dma_start(dst[:], src).then_inc(s_w, 16)
            phase_end(sp, "em")
            with sp.Fori(0, LAYERS) as l:
                for dst, src in ((w_tok, A["tok_w"]), (w_tok1, A["tok_w1"]), (w_tok2, A["tok_w2"]),
                                 (vec_tok, A["tok_v"]), (b1_tok, A["tok_b1"])):
                    shape = "o p a b -> (o p) a b" if len(dst.shape) == 3 else "o p a -> (o p) a"
                    s = src[bass.ds(l, 1)]
                    sp.dma_start(dst[:], s.rearrange(shape)).then_inc(s_wl, 16)
                phase_end(sp, "ln1", l)
                qkv_sp(sp, QKV, l, win)
                phase_end(sp, "qkv", l)
                attn_sp(sp, AT, l, win)
                phase_end(sp, "attn", l)
                out_sp(sp, OT, l)
                phase_end(sp, "out", l)
                phase_end(sp, "ln2", l)
                phase_end(sp, "ffn", l)
            phase_end(sp, "ln3")
            phase_end(sp, "res")
            phase_end(sp, "ln4")
            qkv_sp(sp, QKV, 0, full)
            phase_end(sp, "qkv0")
            attn_sp(sp, AT, 0, full)
            phase_end(sp, "attn0")
            out_sp(sp, O0, 0)
            phase_end(sp, "out0")
            phase_end(sp, "ln5")
            gate_sp(sp, G0, E0, g0_scr)
            phase_end(sp, "gate0")
            moe_sp(sp, MO)
            phase_end(sp, "moe")
            phase_end(sp, "ln6")
            qkv_sp(sp, QKV, 0, causal)
            phase_end(sp, "qkv1")
            attn_sp(sp, AT, 0, causal)
            phase_end(sp, "attn1")
            out_sp(sp, O1, 0, scramble=True)
            phase_end(sp, "out1")
            phase_end(sp, "ln7")
            gate_sp(sp, G1, E1, g1_scr)
            phase_end(sp, "gate1")
            swi_sp(sp, SW)
            phase_end(sp, "swi")
            fin_sp(sp)

        @block.gpsimd
        def _(pool):
            for s, step in credited:
                pool.sem_inc(s, CREDIT * step)
            pool.sem_inc(s_credit, 1)
            pool.memset(ident[:, :], 0.0)
            pool.memset(identb[:, :], 0.0)
            pool.memset(mean_w[:, :], 1.0 / P)
            pool.memset(eps_t[:, :], EPS)
            pool.memset(one_t[:, :], 1.0)
            pool.memset(ones_row[:, :], 1.0)
            pool.memset(band_q[:, :, :], 0.0)
            pool.memset(band_k[:, :, :], 0.0)
            pool.memset(causal_q[:, :], 0.0)
            pool.memset(causal_k[:, :], 0.0).then_inc(s_const, 1)
            pool.wait_ge(s_const, 1)

            def keep(m, pattern, base, mult):
                return pool.affine_select(out=m, in_=m, compare_op=ALU.is_ge, fill=OUTSIDE, base=base,
                                          pattern=pattern, channel_multiplier=mult)

            qt = P - 2 * WIN
            order = [0]

            def link(ins):
                ins.then_inc(s_pool, 1)
                order[0] += 1
                pool.wait_ge(s_pool, order[0])

            link(pool.affine_select(out=ident[:, :], in_=ident[:, :], compare_op=ALU.not_equal, fill=1.0,
                                    base=0, pattern=[[-1, P]], channel_multiplier=1))
            link(pool.affine_select(out=identb[:, :], in_=identb[:, :], compare_op=ALU.not_equal, fill=1.0,
                                    base=0, pattern=[[-1, P]], channel_multiplier=1))
            link(keep(band_q[:, :, :], [[0, 4], [1, P]], 0, -1))
            link(keep(band_q[:, :, :], [[0, 4], [-1, P]], 2 * WIN, 1))
            link(keep(band_k[:, :, :], [[0, 4], [-1, qt]], 0, 1))
            link(keep(band_k[:, :, :], [[0, 4], [1, qt]], 2 * WIN, -1))
            link(keep(causal_q[:, :], [[-1, P]], 0, 1))
            link(keep(causal_k[:, :], [[1, P]], 0, -1))
            pool.sem_inc(s_const, 1)
            em_pool(pool)
            phase_end(pool, "em")
            with pool.Fori(0, LAYERS) as l:
                phase_end(pool, "ln1", l)
                qkv_pool(pool, QKV, l, win)
                phase_end(pool, "qkv", l)
                attn_pool(pool, AT, l, win)
                phase_end(pool, "attn", l)
                phase_end(pool, "out", l)
                phase_end(pool, "ln2", l)
                phase_end(pool, "ffn", l)
            phase_end(pool, "ln3")
            phase_end(pool, "res")
            phase_end(pool, "ln4")
            qkv_pool(pool, QKV, 0, full)
            phase_end(pool, "qkv0")
            attn_pool(pool, AT, 0, full)
            phase_end(pool, "attn0")
            phase_end(pool, "out0")
            phase_end(pool, "ln5")
            phase_end(pool, "gate0")
            phase_end(pool, "moe")
            phase_end(pool, "ln6")
            qkv_pool(pool, QKV, 0, causal)
            phase_end(pool, "qkv1")
            attn_pool(pool, AT, 0, causal)
            phase_end(pool, "attn1")
            phase_end(pool, "out1")
            phase_end(pool, "ln7")
            phase_end(pool, "gate1")
            swi_pool(pool, SW)
            phase_end(pool, "swi")

        @block.tensor
        def _(pe):
            started(pe)
            em_pe(pe)
            phase_end(pe, "em")
            with pe.Fori(0, LAYERS) as l:
                pe.wait_ge(s_wl, (l + 1) * 5 * 16)
                settled(pe)
                ln_pe(pe, LN, l * (2 * NCH), xT)
                phase_end(pe, "ln1", l)
                qkv_pe(pe, QKV, l, win, w_tok[:, 0, :], w_tok[:, 1, :], w_tok[:, 2, :])
                phase_end(pe, "qkv", l)
                attn_pe(pe, AT, l, win)
                phase_end(pe, "attn", l)
                out_pe(pe, OT, l, w_tok[:, 3, :])
                phase_end(pe, "out", l)
                ln_pe(pe, LN, l * (2 * NCH) + NCH, xT)
                phase_end(pe, "ln2", l)
                ffn_pe(pe, FT, l)
                phase_end(pe, "ffn", l)
            pe.wait_ge(s_w, 16 * 9)
            ln_pe(pe, LN, ln_at(4), xT)
            phase_end(pe, "ln3")
            phase_end(pe, "res")
            ln_pe(pe, LN, ln_at(5), hT)
            phase_end(pe, "ln4")
            qkv_pe(pe, QKV, 0, full, w_a0[:, 0, :], w_a0[:, 1, :], w_a0[:, 2, :], bv=bv_a0[:, :])
            phase_end(pe, "qkv0")
            attn_pe(pe, AT, 0, full)
            phase_end(pe, "attn0")
            out_pe(pe, O0, 0, w_a0[:, 3, :])
            phase_end(pe, "out0")
            ln_pe(pe, LN, ln_at(6), xT)
            phase_end(pe, "ln5")
            gate_pe(pe, G0, E0, wr0[:, :])
            phase_end(pe, "gate0")
            moe_pe(pe, MO)
            phase_end(pe, "moe")
            ln_pe(pe, LN, ln_at(7), xT)
            phase_end(pe, "ln6")
            qkv_pe(pe, QKV, 0, causal, w_a1[:, 0, :], w_a1[:, 2, :], w_a1[:, 4, :],
                   wq2=w_a1[:, 1, :], wk2=w_a1[:, 3, :])
            phase_end(pe, "qkv1")
            attn_pe(pe, AT, 0, causal)
            phase_end(pe, "attn1")
            phase_end(pe, "out1")
            ln_pe(pe, LN, ln_at(8), xT)
            phase_end(pe, "ln7")
            gate_pe(pe, G1, E1, wr1[:, :])
            phase_end(pe, "gate1")
            swi_pe(pe, SW)
            phase_end(pe, "swi")
            fin_pe(pe)

        @block.vector
        def _(v):
            started(v)
            em_dve(v)
            phase_end(v, "em")
            with v.Fori(0, LAYERS) as l:
                ln_dve(v, LN, l * (2 * NCH), xT, l * (2 * NCH))
                phase_end(v, "ln1", l)
                qkv_dve(v, QKV, l, win)
                phase_end(v, "qkv", l)
                attn_dve(v, AT, l, win)
                phase_end(v, "attn", l)
                out_dve(v, OT, l, vt(4))
                phase_end(v, "out", l)
                ln_dve(v, LN, l * (2 * NCH) + NCH, xT, l * (2 * NCH) + NCH)
                phase_end(v, "ln2", l)
                ffn_dve(v, FT, l)
                phase_end(v, "ffn", l)
            v.wait_ge(s_w, 16 * 9)
            ln_dve(v, LN, ln_at(4), xT)
            phase_end(v, "ln3")
            with v.Fori(0, NCH) as c:
                x = xT[:, bass.ds(c * CH, CH)]
                v.tensor_tensor(x, x, hT[:, bass.ds(c * CH, CH)], ALU.add).then_inc(RE["x"], 1)
            v.wait_ge(RE["x"], at(NCH))
            phase_end(v, "res")
            ln_dve(v, LN, ln_at(5), hT, ln_at(4))
            phase_end(v, "ln4")
            qkv_dve(v, QKV, 0, full)
            phase_end(v, "qkv0")
            attn_dve(v, AT, 0, full)
            phase_end(v, "attn0")
            out_dve(v, O0, 0, va(4))
            phase_end(v, "out0")
            ln_dve(v, LN, ln_at(6), xT)
            phase_end(v, "ln5")
            gate_dve(v, G0, E0)
            phase_end(v, "gate0")
            moe_dve(v, MO)
            phase_end(v, "moe")
            ln_dve(v, LN, ln_at(7), xT)
            phase_end(v, "ln6")
            qkv_dve(v, QKV, 0, causal)
            phase_end(v, "qkv1")
            attn_dve(v, AT, 0, causal)
            phase_end(v, "attn1")
            out_dve(v, O1, 0, None, project=False)
            phase_end(v, "out1")
            ln_dve(v, LN, ln_at(8), xT)
            phase_end(v, "ln7")
            gate_dve(v, G1, E1)
            phase_end(v, "gate1")
            swi_dve(v, SW)
            phase_end(v, "swi")
            fin_dve(v)

        @block.scalar
        def _(act):
            started(act)
            em_act(act)
            phase_end(act, "em")
            with act.Fori(0, LAYERS) as l:
                act.wait_ge(s_wl, (l + 1) * 5 * 16)
                ln_act(act, LN, l * (2 * NCH), (vt(0), vt(1)))
                phase_end(act, "ln1", l)
                qkv_act(act, QKV, l, win)
                phase_end(act, "qkv", l)
                attn_act(act, AT, l, win)
                phase_end(act, "attn", l)
                phase_end(act, "out", l)
                ln_act(act, LN, l * (2 * NCH) + NCH, (vt(2), vt(3)))
                phase_end(act, "ln2", l)
                ffn_act(act, FT, l)
                phase_end(act, "ffn", l)
            act.wait_ge(s_w, 16 * 9)
            ln_act(act, LN, ln_at(4), None)
            phase_end(act, "ln3")
            phase_end(act, "res")
            ln_act(act, LN, ln_at(5), (va(0), va(1)))
            phase_end(act, "ln4")
            qkv_act(act, QKV, 0, full, bq=va(2), bk=va(3))
            phase_end(act, "qkv0")
            attn_act(act, AT, 0, full)
            phase_end(act, "attn0")
            phase_end(act, "out0")
            ln_act(act, LN, ln_at(6), None)
            phase_end(act, "ln5")
            gate_act(act, G0, E0, 0.0)
            phase_end(act, "gate0")
            moe_act(act, MO)
            phase_end(act, "moe")
            ln_act(act, LN, ln_at(7), None)
            phase_end(act, "ln6")
            qkv_act(act, QKV, 0, causal)
            phase_end(act, "qkv1")
            attn_act(act, AT, 0, causal)
            phase_end(act, "attn1")
            phase_end(act, "out1")
            ln_act(act, LN, ln_at(8), None)
            phase_end(act, "ln7")
            gate_act(act, G1, E1, br1[:, 0:1])
            phase_end(act, "gate1")
            swi_act(act, SW)
            phase_end(act, "swi")
            fin_act(act)


def rope_tables():
    t = np.arange(T, dtype=np.float64)
    out = []
    for d in (P, P // 2):
        i = np.arange(d // 2, dtype=np.float64)
        theta = 10000.0 ** (-(2.0 * (i - 1.0))) / d
        ang = t[:, None] * theta[None, :]
        cos, sin = np.cos(ang).astype(np.float32), np.sin(ang).astype(np.float32)
        c = np.repeat(cos, 2, axis=1).T
        s = np.stack([sin, -sin], axis=-1).reshape(T, d).T
        out.append((c, s))
    return out


def kernel(**inputs):
    import concourse.bacc as _bacc
    from concourse import mybir as _mybir
    from concourse.bass_utils import run_bass_kernel_spmd as _run

    x = {k: np.asarray(v) for k, v in inputs.items()}

    def pack(*arrays):
        return np.ascontiguousarray(np.stack(arrays, axis=-1))

    def columns(w, order):
        return w[:, order]

    swap = np.arange(P) ^ 1
    twice = np.concatenate([np.arange(HD) + HD * (h // 2) for h in range(H)])
    twice_swap = np.concatenate([(np.arange(HD) ^ 1) + HD * (h // 2) for h in range(H)])
    t = "L0_tok_"
    a, f, g, m = "L0_attn_", "L0_ffn_", "L1_attn_", "L1_ffn_"
    (cq, sq), (ck, sk) = rope_tables()
    wx, bx = x[a + "w_xyz"], x[a + "b_xyz"]
    w1 = np.concatenate([x[m + "expert_w1"], x[m + "shared_w1"][None]])
    w1 = np.concatenate([w1[..., 0::2], w1[..., 1::2]], axis=-1)
    b1 = np.concatenate([x[m + "expert_b1"], x[m + "shared_b1"][None]])
    w2 = np.concatenate([x[m + "expert_w2"], x[m + "shared_w2"][None]])
    arrays = {
        "x": x["x"], "mask": x["mask_BS_i1_0"], "tok": x[t + "tok_emb"], "pos": x[t + "pos_emb"],
        "tok_w": np.stack([x[t + "Wq"], x[t + "Wk"], x[t + "Wv"], x[t + "Wo"]], axis=2),
        "tok_w1": x[t + "W1"],
        "tok_w2": x[t + "W2"].reshape(LAYERS, FB, P, P).transpose(0, 2, 1, 3),
        "tok_v": pack(x[t + "ln1_g"], x[t + "ln1_b"], x[t + "ln2_g"], x[t + "ln2_b"], x[t + "bo"], x[t + "b2"]),
        "tok_b1": x[t + "b1"].reshape(LAYERS, FB, P).transpose(0, 2, 1),
        "a0_w": np.stack([wx[:, 0:P], wx[:, P:2 * P], wx[:, 2 * P:], x[a + "w_end"]], axis=1),
        "a0_v": pack(x[a + "gamma"], x[a + "beta"], bx[0:P], bx[P:2 * P], x[a + "b_end"]),
        "a0_bv": bx[None, 2 * P:],
        "a1_w": np.stack([x[g + "Wq"], columns(x[g + "Wq"], swap), columns(x[g + "Wk"], twice),
                          columns(x[g + "Wk"], twice_swap), columns(x[g + "Wv"], twice)], axis=1),
        "cos": np.stack([cq, ck[twice]]), "sin": np.stack([sq, sk[twice]]),
        "wr0": x[f + "Wr"].T, "wr1": x[m + "gate_w"], "br1": x[m + "gate_b"][:, None],
        "e1": x[f + "W1"].transpose(2, 0, 1),
        "e2": x[f + "W2"].reshape(E0, P, FB, P).transpose(3, 0, 2, 1),
        "sw1": w1.transpose(1, 0, 2), "sw2": w2.transpose(1, 0, 2),
        "sb1": np.stack([b1[:, 0::2].T, b1[:, 1::2].T], axis=1),
        "sb2": np.concatenate([x[m + "expert_b2"], x[m + "shared_b2"][None]]),
        "sact": np.concatenate([x[m + "expert_act"], x[m + "shared_act"][None]]).T,
    }
    nc = _bacc.Bacc("TRN2", target_bir_lowering=False, num_devices=1)
    sent, aps = {}, {}
    for name, v in arrays.items():
        v = np.ascontiguousarray(v)
        sent[f"in_{name}"] = v
        aps[name] = nc.dram_tensor(f"in_{name}", v.shape, _mybir.dt.from_np(v.dtype), kind="ExternalInput").ap()
    aps["out"] = nc.dram_tensor("out", (N, P), _mybir.dt.float32, kind="ExternalOutput").ap()
    build(nc, aps)
    r = _run(nc, [sent], core_ids=[0])
    return r.results[0]["out"].reshape(B, T, P)
```

```python
from contextlib import ExitStack

import numpy as np

import concourse.bass as bass
from concourse import mybir

F32 = mybir.dt.float32
BF16 = mybir.dt.bfloat16
F32R = mybir.dt.float32r
I32 = mybir.dt.int32
ALU = mybir.AluOpType
ACT = mybir.ActivationFunctionType
AX_X = mybir.AxisListType.X

P = 128
B, T = 4, 1024
N = B * T
CH = 512
NCH = N // CH
H, HD = 8, 16
U = B * H
VOCAB = 8000
LAYERS = 2
FF = 512
FB = FF // P
E0 = 8
E1 = 16
I1 = 96
WIN = 16
EPS = 1e-5
CREDIT = 4
SLOTS = 4
REST_FULL = "vpvpvpvp"
REST_CAUSAL = "vpvpvpvp"
BIG = 3.0e38
OUTSIDE = -1.0e30
MASKED = -4.0e9
MASK_PARTS = (-3992977408.0, -7012352.0, -10240.0)
SCALE = 0.25
Q_PARTS = (0, 0, 1, 1, 0, 2)
K_PARTS = (0, 1, 0, 1, 2, 0)
STACK = 16 * len(Q_PARTS)
Z_ROWS = 4 * HD


def geometry(mode):
    if mode == "window":
        qt, nt, pad = P - 2 * WIN, 12, WIN
        return dict(mode=mode, qt=qt, nt=nt, pad=pad, nq=qt * nt, nk=qt * (nt - 1) + P,
                               q_chunks=[(0, 384), (384, 384), (768, 384)],
                               k_chunks=[(0, 400), (400, 400), (800, 384)],
                               score_rows=STACK + 3, steps=3)
    return dict(mode=mode, qt=P, nt=T // P, pad=0, nq=T, nk=T,
                           q_chunks=[(0, CH), (CH, CH)], k_chunks=[(0, CH), (CH, CH)],
                           score_rows=STACK, steps=T // P)


def geometries():
    out = {}
    before = dict(calls=0, mx=0, red=0, sc=0, items=0, qk=0, chain=0, init=0, oev=0, stores=0, z=0, rest_v=0, rest_p=0, rest_n=0)
    for mode, calls in (("window", LAYERS), ("full", 1), ("causal", 1)):
        g = geometry(mode)
        g["before"] = dict(before)
        n_qk = len(g["q_chunks"]) + len(g["k_chunks"])
        g["splits"] = [2 + (3 if mode == "causal" else 1 if mode == "window" and k >= len(g["q_chunks"]) else 0)
                    for k in range(n_qk)]
        g["links"] = sum(g["splits"])
        g["stores"] = 13 + (H if mode == "window" else 0)
        g["rest"] = {"window": "nnn", "full": REST_FULL, "causal": REST_CAUSAL}[mode]
        g["z_parts"] = (0, 3) if mode == "window" else (0, 1, 2, 3)
        g["ahead"] = 1 if mode == "window" else 3
        g["evacs"] = 3 if mode == "window" else 1
        g["slots"] = 2 * SLOTS if mode == "window" else SLOTS
        g["late"], g["turn"] = mode == "full", {"window": 1, "full": 0, "causal": 6}[mode]
        g["fills"] = 5 if mode == "window" else 4
        before["calls"] += calls
        before["init"] += calls * g["fills"]
        before["stores"] += calls * (B // 2) * g["stores"]
        before["oev"] += calls * U * g["evacs"]
        before["z"] += calls * (U // 2) * len(g["z_parts"])
        for who in "vpn":
            before["rest_" + who] += calls * U * g["rest"].count(who)
        before["mx"] += calls * U * len(max_steps(g))
        before["red"] += calls * U * (len(max_steps(g)) + 1)
        before["sc"] += calls * U * g["steps"]
        before["items"] += calls * B * (n_qk + g["nt"] // 4)
        before["qk"] += calls * B * n_qk
        before["chain"] += calls * B * g["links"]
        out[mode] = g
    return out


def max_steps(g):
    if g["mode"] == "window":
        return [(4 * s, 0, CH) for s in range(3)]
    out = []
    for t in range(g["nt"]):
        end = (t + 1) * P if g["mode"] == "causal" else T
        out += [(t, k0, min(CH, end - k0)) for k0 in range(0, end, CH)]
    return out


def at(n, step=1):
    return (n + CREDIT) * step


def build(nc, A):
    with ExitStack() as ctx:
        def sb(name, shape, dt=F32):
            return ctx.enter_context(nc.sbuf_tensor(name, shape, dt))

        credited = []

        def sem(name):
            return ctx.enter_context(nc.semaphore(name))

        def sems(prefix, names, dma=()):
            made = {}
            for n in list(names) + list(dma):
                made[n] = sem(f"{prefix}_{n}")
                credited.append((made[n], 16 if n in dma else 1))
            return made

        def scratch(name, shape, dt=F32):
            return nc.dram_tensor(name, shape, dt, kind="Internal").ap()

        q_stack = scratch("q_stack", (U, STACK, 1152), BF16)
        k_stack = scratch("k_stack", (U, STACK + 3, 1184), BF16)
        v_scr = scratch("v_scr", (B, H, P, 12 * HD))
        z_scr = [scratch(f"z_scr{x}", (U, HD, T)) for x in range(4)]
        g0_scr = scratch("g0_scr", (N // P, E0, P))
        g1_scr = scratch("g1_scr", (N // P, E1, P))

        xT = sb("xT", [P, N])
        hT = sb("hT", [P, N])
        ident = sb("ident", [P, P])
        identb = sb("identb", [P, P], BF16)
        mean_w = sb("mean_w", [P, P])
        band_q = sb("band_q", [P, 4, P], BF16)
        band_k = sb("band_k", [P, 4, P - 2 * WIN], BF16)
        causal_q = sb("causal_q", [P, P], BF16)
        causal_k = sb("causal_k", [P, P], BF16)
        eps_t = sb("eps_t", [P, 1])
        one_t = sb("one_t", [P, 1])
        ones_row = sb("ones_row", [1, P])
        w_tok = sb("w_tok", [P, 4, P])
        w_tok1 = sb("w_tok1", [P, FF])
        w_tok2 = sb("w_tok2", [P, FB, P])
        vec_tok = sb("vec_tok", [P, 6])
        b1_tok = sb("b1_tok", [P, FB])
        w_a0 = sb("w_a0", [P, 4, P])
        vec_a0 = sb("vec_a0", [P, 5])
        bv_a0 = sb("bv_a0", [1, P])
        w_a1 = sb("w_a1", [P, 5, P])
        wr0 = sb("wr0", [P, E0])
        wr1 = sb("wr1", [P, E1])
        br1 = sb("br1", [E1, 1])
        w_e1 = sb("w_e1", [P, E0, FF])
        w_e2 = sb("w_e2", [P, E0, FB, P])

        vr_all = sb("vr_all", [P, SLOTS, T // P, Z_ROWS], F32R)
        rest_all = sb("rest_all", [P, 4, T], F32R)

        WORK = 24 * 1024 - 128
        work = sb("work", [P, WORK])

        def area():
            used = [0]

            def take(shape, dt=F32, parts=P):
                n = int(np.prod(shape))
                words = n if dt in (F32, I32) else (n + 1) // 2
                v = work[0:parts, used[0]:used[0] + words]
                used[0] += words
                assert used[0] <= WORK, used[0]
                if dt != F32:
                    v = v.bitcast(dt)
                if len(shape) == 2:
                    v = v.rearrange("p (a b) -> p a b", a=shape[0])
                if len(shape) == 3:
                    v = v.rearrange("p (a b c) -> p a b c", a=shape[0], b=shape[1])
                return v

            return take

        bank = ctx.enter_context(nc.psum_tensor("bank", [P, 8, CH], F32))

        s_const = sem("const_ready")
        s_w = sem("weights_in")
        s_wl = sem("layer_weights_in")
        s_credit = sem("credit_given")
        s_pool = sem("masks_built")
        s_phase = sem("phase_end")
        s_settled = sem("settled")
        GEO = geometries()

        layer_phases = ("ln1", "qkv", "attn", "out", "ln2", "ffn")
        late_phases = ("ln3", "res", "ln4", "qkv0", "attn0", "out0", "ln5", "gate0", "moe",
                       "ln6", "qkv1", "attn1", "out1", "ln7", "gate1", "swi")

        def settled(eng):
            eng.sem_inc(s_settled, 1)

        def phase_end(eng, name, l=0):
            if name == "em":
                k = 1
            elif name in layer_phases:
                k = l * len(layer_phases) + (2 + layer_phases.index(name))
            else:
                k = 2 + LAYERS * len(layer_phases) + late_phases.index(name)
            settled(eng)
            eng.drain().then_inc(s_phase, 1)
            eng.wait_ge(s_phase, 5 * k)
            settled(eng)

        EM = sems("em", ["idx_f", "idx_T", "idx", "posed", "turned", "copied", "chain"], ["misc"])
        gathered = [sem("gathered0"), sem("gathered1")]
        take = area()
        em_tok = take([P], I32, 32)
        em_f = take([P], F32, 32)
        em_neg = take([P], F32, 32)
        em_idx = take([N // P], I32)
        em_cur = [take([1], I32) for _ in range(2)]
        em_row = [take([P]) for _ in range(2)]
        em_sum = [take([P]) for _ in range(2)]
        em_pos = take([T // P, P])

        def em_sp(sp):
            sp.dma_start(em_tok, A["x"].rearrange("b (t p) -> (b t) p", p=P)).then_inc(EM["misc"], 16)
            sp.dma_start(em_pos, A["pos"].rearrange("(t p) d -> p t d", p=P)).then_inc(EM["misc"], 16)

        def em_pool(pool):
            pool.wait_ge(EM["idx"], at(1))
            with pool.Fori(0, B) as b:
                for t in range(T // P):
                    g, n = t % 2, b * (T // P) + t
                    pool.wait_ge(EM["posed"], at(n + 1 - 2))
                    settled(pool)
                    pool.tensor_copy(em_cur[g], em_idx[:, bass.ds(n, 1)]).then_inc(EM["chain"], 1)
                    pool.wait_ge(EM["chain"], at(n + 1))
                    settled(pool)
                    pool.indirect_dma_start(out=em_row[g], out_offset=None, in_=A["tok"],
                                            in_offset=bass.IndirectOffsetOnAxis(ap=em_cur[g], axis=0),
                                            ).then_inc(gathered[g], 16)

        def em_pe(pe):
            pe.wait_ge(EM["idx_f"], at(5))
            pe.transpose(bank[:, 7, 0:32], em_f, ident[0:32, 0:32]).then_inc(EM["idx_T"], 1)
            with pe.Fori(0, B) as b:
                for t in range(T // P):
                    g, n = t % 2, b * (T // P) + t
                    pe.wait_ge(EM["posed"], at(n + 1))
                    pe.wait_ge(EM["copied"], at(n + 1 - 2))
                    pe.transpose(bank[:, g, 0:P], em_sum[g], ident[:, :]).then_inc(EM["turned"], 1)

        def em_dve(v):
            v.wait_ge(EM["misc"], at(2, 16))
            v.tensor_copy(em_f, em_tok).then_inc(EM["idx_f"], 1)
            v.wait_ge(EM["idx_f"], at(1))
            v.tensor_scalar(em_neg, em_f, 0.0, float(VOCAB), ALU.is_lt, ALU.mult).then_inc(EM["idx_f"], 1)
            v.wait_ge(EM["idx_f"], at(2))
            v.tensor_tensor(em_f, em_f, em_neg, ALU.add).then_inc(EM["idx_f"], 1)
            v.wait_ge(EM["idx_f"], at(3))
            v.tensor_scalar(em_f, em_f, 0.0, float(VOCAB - 1), ALU.max, ALU.min).then_inc(EM["idx_f"], 2)
            v.wait_ge(EM["idx_T"], at(1))
            v.tensor_copy(em_idx, bank[:, 7, 0:32]).then_inc(EM["idx"], 1)
            with v.Fori(0, B) as b:
                for t in range(T // P):
                    g, n = t % 2, b * (T // P) + t
                    v.wait_ge(gathered[g], (b * (T // P // 2) + t // 2 + 1) * 16)
                    v.wait_ge(EM["turned"], at(n + 1 - 2))
                    v.tensor_tensor(em_sum[g], em_row[g], em_pos[:, t, :], ALU.add).then_inc(EM["posed"], 1)

        def em_act(act):
            with act.Fori(0, B) as b:
                for t in range(T // P):
                    g, n = t % 2, b * (T // P) + t
                    act.wait_ge(EM["turned"], at(n + 1))
                    act.activation(xT[:, bass.ds(n * P, P)], bank[:, g, 0:P], ACT.Copy).then_inc(EM["copied"], 1)

        LR = 4
        take = area()
        ln_c = take([LR, CH])
        ln_sq = take([LR, CH])
        ln_r = take([LR, CH])
        ln_t = take([LR, CH])
        ln_n = take([LR, CH])
        LN_NAMES = ["mean", "cent", "sq", "var", "log", "rstd", "vr", "vrr", "newton", "raw", "norm", "done"]

        def ln_pe(pe, S, base, src):
            with pe.Fori(0, NCH // LR) as i:
                for g in range(LR):
                    n = base + LR * i + g
                    pe.wait_ge(S["cent"], at(n + 1 - LR))
                    pe.matmul(bank[:, g, :], mean_w[:, :], src[:, bass.ds((LR * i + g) * CH, CH)],
                              start=True, stop=True).then_inc(S["mean"], 1)
                for g in range(LR):
                    n = base + LR * i + g
                    pe.wait_ge(S["sq"], at(n + 1))
                    pe.wait_ge(S["vr"], at(n + 1 - LR))
                    pe.matmul(bank[:, LR + g, :], mean_w[:, :], ln_sq[:, g, :],
                              start=True, stop=True).then_inc(S["var"], 1)

        def ln_pool(pool, S, base):
            with pool.Fori(0, NCH // LR) as i:
                for g in range(LR):
                    n = base + LR * i + g
                    t = ln_t[:, g, :]
                    pool.wait_ge(S["vr"], at(n + 1))
                    pool.tensor_tensor(t, t, ln_r[:, g, :], ALU.mult).then_inc(S["vrr"], 1)
                    pool.wait_ge(S["vrr"], at(n + 1))
                    settled(pool)
                    pool.tensor_scalar(t, t, -0.5, 1.5, ALU.mult, ALU.add).then_inc(S["newton"], 1)

        def ln_dve(v, S, base, src, gained=None):
            with v.Fori(0, NCH // LR) as i:
                for g in range(LR):
                    c, n = LR * i + g, base + LR * i + g
                    v.wait_ge(S["mean"], at(n + 1))
                    v.wait_ge(S["raw"], at(n + 1 - LR))
                    v.wait_ge(S["sq"], at(n + 1 - LR))
                    v.tensor_tensor(ln_c[:, g, :], src[:, bass.ds(c * CH, CH)], bank[:, g, :],
                                    ALU.subtract).then_inc(S["cent"], 1)
                for g in range(LR):
                    n = base + LR * i + g
                    v.wait_ge(S["rstd"], at(n + 1))
                    v.wait_ge(S["norm"], at(n + 1 - LR))
                    v.scalar_tensor_tensor(out=ln_t[:, g, :], in0=bank[:, LR + g, :], scalar=EPS,
                                           in1=ln_r[:, g, :], op0=ALU.add, op1=ALU.mult).then_inc(S["vr"], 1)
                    if gained is not None:
                        v.wait_ge(S["done"], at(gained + LR * i + g + 1 - LR))
                    v.tensor_tensor(ln_n[:, g, :], ln_c[:, g, :], ln_r[:, g, :], ALU.mult).then_inc(S["raw"], 1)
                for g in range(LR):
                    c, n = LR * i + g, base + LR * i + g
                    v.wait_ge(S["newton"], at(n + 1))
                    v.wait_ge(S["raw"], at(n + 1))
                    out = hT[:, bass.ds(c * CH, CH)] if gained is None else ln_n[:, g, :]
                    v.tensor_tensor(out, ln_n[:, g, :], ln_t[:, g, :], ALU.mult).then_inc(S["norm"], 1)

        def ln_act(act, S, base, gain):
            settled(act)
            act.preload_act_table_set("natural_log_exp_and_others")
            with act.Fori(0, NCH // LR) as i:
                for g in range(LR):
                    n = base + LR * i + g
                    act.wait_ge(S["cent"], at(n + 1))
                    act.wait_ge(S["var"], at(n + 1 - LR))
                    act.activation(ln_sq[:, g, :], ln_c[:, g, :], ACT.Square).then_inc(S["sq"], 1)
                for g in range(LR):
                    n = base + LR * i + g
                    act.wait_ge(S["var"], at(n + 1))
                    act.wait_ge(S["norm"], at(n + 1 - LR))
                    act.activation(ln_r[:, g, :], bank[:, LR + g, :], ACT.Ln,
                                   bias=eps_t[:, 0:1]).then_inc(S["log"], 1)
                for g in range(LR):
                    n = base + LR * i + g
                    act.wait_ge(S["log"], at(n + 1))
                    act.activation(ln_r[:, g, :], ln_r[:, g, :], ACT.Exp, scale=-0.5).then_inc(S["rstd"], 1)
                if gain is not None:
                    for g in range(LR):
                        act.wait_ge(S["norm"], at(base + LR * i + g + 1))
                        act.activation(hT[:, bass.ds((LR * i + g) * CH, CH)], ln_n[:, g, :], ACT.Identity,
                                       bias=gain[1], scale=gain[0]).then_inc(S["done"], 1)

        def qkv_buffers(g):
            take = area()
            r = dict()
            r["h"] = take([2, 1184])
            r["f"] = take([3, CH])
            r["f2"] = take([3, CH]) if g["mode"] == "causal" else None
            r["qp"] = [take([3, 1152], BF16) for _ in range(2)]
            r["kp"] = [take([3, 1184], BF16) for _ in range(2)]
            r["v"] = [take([H, 12, HD]) for _ in range(2)]
            if g["mode"] == "window":
                r["mi"] = take([B, T], I32)
                r["m"] = take([2, 1184])
                r["mr"] = [take([3, 1184], BF16) for _ in range(2)]
            if g["mode"] == "causal":
                r["cos"] = take([2, T])
                r["sin"] = take([2, T])
            return r

        QB = {m: qkv_buffers(GEO[m]) for m in GEO}
        QK_NAMES = ["h", "h_used", "mm", "evac", "two", "q", "chain", "pads", "m", "mr"]
        QK_DMA = ["stored0", "stored1", "mask", "rope"]

        def qkv_items(g):
            items = [("q", c, w) for c, w in g["q_chunks"]] + [("k", c, w) for c, w in g["k_chunks"]]
            return items + [("v", t, 4) for t in range(0, g["nt"], 4)]

        def n_qk(g):
            return len(g["q_chunks"]) + len(g["k_chunks"])

        def batch_no(g, l, b):
            return (g["before"]["calls"] + l) * B + b

        def pairs(eng, body):
            with eng.Fori(0, B // 2 - 1) as i:
                for p in range(2):
                    body(i, p, True)
            for p in range(2):
                body(B // 2 - 1, p, p == 0)

        def wait_stored(eng, S, l, g, i, p):
            eng.wait_ge(S[f"stored{p}"], at(g["before"]["stores"] + (l * (B // 2) + i) * g["stores"], 16))

        def qkv_pool(pool, S, l, g):
            R = QB[g["mode"]]

            def prepare(i, p):
                b = 2 * i + p
                n = batch_no(g, l, b)
                pool.wait_ge(S["h_used"], at(n + 1 - 2))
                settled(pool)
                main = pool.tensor_scalar(R["h"][:, p, g["pad"]:g["pad"] + T], hT[:, bass.ds(b * T, T)], 1.0,
                                          None, ALU.mult)
                if not g["pad"]:
                    main.then_inc(S["h"], 3)
                    return
                main.then_inc(S["h"], 1)
                pool.tensor_copy(R["h"][:, p, 0:g["pad"]],
                                 hT[:, bass.ds(b * T, 1)].broadcast_to([P, g["pad"]])).then_inc(S["h"], 1)
                pool.tensor_copy(R["h"][:, p, g["pad"] + T:g["nk"]],
                                 hT[:, bass.ds(b * T + T - 1, 1)].broadcast_to([P, g["nk"] - g["pad"] - T])
                                 ).then_inc(S["h"], 1)
                wait_stored(pool, S, l, g, i, p)
                settled(pool)
                pool.tensor_scalar(R["m"][:, p, WIN:WIN + T], R["mi"][:, bass.ds(b, 1), :].rearrange(
                    "p a t -> p (a t)"), 0.0, None, ALU.is_gt).then_inc(S["m"], 1)
                pool.wait_ge(S["m"], at(l * B + b + 1))
                settled(pool)
                for x in range(3):
                    pool.tensor_scalar(R["mr"][p][0:1, x, :], R["m"][0:1, p, :], -MASK_PARTS[x], MASK_PARTS[x],
                                       ALU.mult, ALU.add).then_inc(S["mr"], 1)

            def body(i, p, more):
                if more:
                    prepare(i + p, 1 - p)
                for n, (kind, c, w) in enumerate(qkv_items(g)[:n_qk(g)]):
                    parts = R["qp" if kind == "q" else "kp"][p]
                    pool.wait_ge(S["two"], at(g["before"]["qk"] + (l * B + 2 * i + p) * n_qk(g) + n + 1))
                    pool.tensor_tensor(parts[:, 2, c:c + w], R["f"][:, n % 3, 0:w], parts[:, 1, c:c + w],
                                       ALU.subtract).then_inc(S["q"], 1)

            if g["mode"] == "window":
                pool.wait_ge(S["mask"], at(l + 1, 16))
                settled(pool)
                for p in range(2):
                    for c0, c1 in ((0, WIN), (WIN + T, g["nk"])):
                        pool.memset(R["m"][:, p, c0:c1], 0.0).then_inc(S["pads"], 1)
                pool.wait_ge(S["pads"], at(4 * (l + 1)))
                settled(pool)
            prepare(0, 0)
            pairs(pool, body)

        def qkv_pe(pe, S, l, g, wq, wk, wv, wq2=None, wk2=None, bv=None):
            R = QB[g["mode"]]
            items = qkv_items(g)

            def body(i, p, more):
                b = 2 * i + p
                for n, (kind, c, w) in enumerate(items):
                    s = 2 * (n % 3)
                    m = g["before"]["items"] + (l * B + b) * len(items) + n
                    if n == 0:
                        pe.wait_ge(S["h"], at(3 * (batch_no(g, l, b) + 1)))
                    pe.wait_ge(S["evac"], at(m + 1 - 3))
                    if kind == "v":
                        for t in range(4):
                            hs = R["h"][:, p, (c + t) * g["qt"]:(c + t) * g["qt"] + P]
                            last = pe.matmul(bank[:, s, t * P:(t + 1) * P], hs, wv,
                                             start=True, stop=bv is None)
                            if bv is not None:
                                last = pe.matmul(bank[:, s, t * P:(t + 1) * P], ones_row[:, :], bv,
                                                 start=False, stop=True)
                    else:
                        c0 = c + (g["pad"] if kind == "q" else 0)
                        last = pe.matmul(bank[:, s, 0:w], wq if kind == "q" else wk, R["h"][:, p, c0:c0 + w],
                                         start=True, stop=True)
                        if wq2 is not None:
                            last = pe.matmul(bank[:, s + 1, 0:w], wq2 if kind == "q" else wk2,
                                             R["h"][:, p, c0:c0 + w], start=True, stop=True)
                    last.then_inc(S["mm"], 1)
                pe.wait_ge(S["mm"], at(m + 1))
                pe.sem_inc(S["h_used"], 1)

            pairs(pe, body)

        def qkv_act(act, S, l, g, bq=0.0, bk=0.0):
            R = QB[g["mode"]]
            items = qkv_items(g)

            def body(i, p, more):
                b = 2 * i + p
                for n, (kind, c, w) in enumerate(items):
                    s = n % 3
                    m = g["before"]["items"] + (l * B + b) * len(items) + n
                    act.wait_ge(S["mm"], at(m + 1))
                    if kind == "v":
                        if c == 0:
                            wait_stored(act, S, l, g, i, p)
                        act.activation(R["v"][p][:, :, c:c + 4, :],
                                       bank[:, 2 * s, :].rearrange("p (t h d) -> p h t d", t=4, h=H),
                                       ACT.Copy).then_inc(S["evac"], 1)
                    else:
                        act.wait_ge(S["q"], at(g["before"]["qk"] + (l * B + b) * n_qk(g) + (n + 1 - 3 if n >= 3 else 0)))
                        last = act.activation(R["f"][:, s, 0:w], bank[:, 2 * s, 0:w], ACT.Identity,
                                              bias=bq if kind == "q" else bk)
                        if g["mode"] == "causal":
                            last = act.activation(R["f2"][:, s, 0:w], bank[:, 2 * s + 1, 0:w], ACT.Copy)
                        last.then_inc(S["evac"], 1)

            pairs(act, body)

        def qkv_dve(v, S, l, g):
            R = QB[g["mode"]]
            items = qkv_items(g)
            if g["mode"] == "causal":
                v.wait_ge(S["rope"], at(2, 16))

            def body(i, p, more):
                b = 2 * i + p
                count = [0]
                base = g["before"]["chain"] + (l * B + b) * g["links"]

                def link(ins):
                    ins.then_inc(S["chain"], 1)
                    count[0] += 1
                    v.wait_ge(S["chain"], at(base + count[0]))

                wait_stored(v, S, l, g, i, p)
                for n, (kind, c, w) in enumerate(items[:n_qk(g)]):
                    s = n % 3
                    f = R["f"][:, s, 0:w]
                    parts = R["qp" if kind == "q" else "kp"][p]
                    v.wait_ge(S["evac"], at(g["before"]["items"] + (l * B + b) * len(items) + n + 1))
                    if g["mode"] == "causal":
                        f2 = R["f2"][:, s, 0:w]
                        of = 0 if kind == "q" else 1
                        link(v.tensor_tensor(f, f, R["cos"][:, of, c:c + w], ALU.mult))
                        link(v.tensor_tensor(f2, f2, R["sin"][:, of, c:c + w], ALU.mult))
                        link(v.tensor_tensor(f, f, f2, ALU.add))
                    if g["mode"] == "window" and kind == "k":
                        if n == len(g["q_chunks"]):
                            v.wait_ge(S["m"], at(l * B + b + 1))
                        link(v.tensor_tensor(f, f, R["m"][:, p, c:c + w], ALU.mult))
                    link(v.tensor_copy(parts[:, 0, c:c + w], f))
                    link(v.tensor_tensor(f, f, parts[:, 0, c:c + w], ALU.subtract))
                    v.tensor_copy(parts[:, 1, c:c + w], f).then_inc(S["two"], 1)

            pairs(v, body)

        def qkv_sp(sp, S, l, g):
            R = QB[g["mode"]]
            items = qkv_items(g)
            if g["mode"] == "causal":
                sp.dma_start(R["cos"], A["cos"].rearrange("a p t -> p a t")).then_inc(S["rope"], 16)
                sp.dma_start(R["sin"], A["sin"].rearrange("a p t -> p a t")).then_inc(S["rope"], 16)
            if g["mode"] == "window":
                sp.dma_start(R["mi"], A["mask"].partition_broadcast(P)).then_inc(S["mask"], 16)

            def body(i, p, more):
                b = 2 * i + p
                n, stored = l * B + b, S[f"stored{p}"]
                sp.wait_ge(S["q"], at(g["before"]["qk"] + n * n_qk(g) + len(g["q_chunks"])))
                for j, part in enumerate(Q_PARTS):
                    sp.dma_start(q_stack[bass.ds(b * H, H), j * HD:(j + 1) * HD, 0:g["nq"]],
                                 R["qp"][p][:, part, 0:g["nq"]]).then_inc(stored, 16)
                sp.wait_ge(S["q"], at(g["before"]["qk"] + (n + 1) * n_qk(g)))
                for j, part in enumerate(K_PARTS):
                    sp.dma_start(k_stack[bass.ds(b * H, H), j * HD:(j + 1) * HD, 0:g["nk"]],
                                 R["kp"][p][:, part, 0:g["nk"]]).then_inc(stored, 16)
                if g["mode"] == "window":
                    sp.wait_ge(S["mr"], at(3 * (n + 1)))
                    for h in range(H):
                        sp.dma_start(k_stack[bass.ds(b * H + h, 1), STACK:STACK + 3, 0:g["nk"]],
                                     R["mr"][p][0:1, :, 0:g["nk"]]).then_inc(stored, 16)
                sp.wait_ge(S["evac"], at(g["before"]["items"] + (n + 1) * len(items)))
                sp.dma_start(v_scr[bass.ds(b, 1), :, :, 0:g["nt"] * HD].rearrange("b h p x -> p (b h) x"),
                             R["v"][p][:, :, 0:g["nt"], :].rearrange("p h t d -> p h (t d)")).then_inc(stored, 16)

            pairs(sp, body)
            for p in range(2):
                wait_stored(sp, S, l, g, B // 2, p)

        def first(g, l):
            return (g["before"]["calls"] + l) * U

        def attn_buffers(g):
            take = area()
            r = dict()
            r["q"] = take([g["slots"], g["nq"]], BF16)
            r["k"] = take([g["slots"], g["nk"]], BF16)
            r["vc"] = take([g["slots"], g["nt"], HD])
            if g["mode"] == "window":
                r["vf"] = take([SLOTS, g["nt"], Z_ROWS])
                r["p"] = [take([4 * g["qt"]]) for _ in range(3)]
            else:
                r["vb"] = take([SLOTS, g["nt"], Z_ROWS], BF16)
                r["vr"] = vr_all
                r["vt"] = take([g["nt"], HD])
                r["p"] = [take([T]) for _ in range(4)]
                r["high"] = [x.bitcast(BF16)[:, 1:2 * T:2] for x in r["p"]]
                r["rest"] = [rest_all[:, x, :] for x in range(4)]
            r["mh"] = take([SLOTS, 8, 2])
            r["m"] = take([SLOTS, g["nt"]])
            r["a"] = take([SLOTS, P])
            r["ap"] = take([SLOTS, 3, P], BF16)
            r["z"] = take([2, 4 * g["qt"] * g["steps"] if g["mode"] == "window" else T])
            return r

        AB = {m: attn_buffers(GEO[m]) for m in GEO}
        AT_NAMES = ["init", "vpad", "vchain", "mx", "red", "neg", "mt", "split", "sc", "exp", "rest_v", "rest_p",
                    "pv", "oev", "chain"]
        AT_DMA = ["load0", "load1", "load2", "load3", "row0", "row1", "row2", "row3", "z0", "z1"]

        def slot_sem(S, kind, j):
            return {"load": [S["load0"], S["load1"], S["load2"], S["load3"]], "row": [S["row0"], S["row1"], S["row2"], S["row3"]],
                    "z": [S["z0"], S["z1"]]}[kind][j % (2 if kind == "z" else 4)]

        def scrambled(scr):
            return scr.rearrange("u d t -> u (d t)").rearrange("u (s h r) -> u s h r", s=8, h=HD)

        def nth(g, l, i, j, ring):
            return (g["before"]["calls"] + l) * (U // ring) + i * (g["slots"] // ring) + j // ring + 1

        def loads_in(g, l, i, j):
            return at(3 * nth(g, l, i, j, 4), 16)

        def step_no(g, l, i, j, t):
            return g["before"]["sc"] + (l * U + g["slots"] * i + j) * g["steps"] + t

        def rest_no(g, l, i, j, t):
            who = g["rest"][t]
            n = g["before"]["rest_" + who] + (l * U + g["slots"] * i + j) * g["rest"].count(who)
            return n + g["rest"][0:t + 1].count(who), "rest_" + who

        def following(i, j, t, ahead, steps, slots):
            if t + ahead < steps:
                return i, j, t + ahead
            return i + (j + 1) // slots, (j + 1) % slots, t + ahead - steps

        def walk(eng, g, body):
            n = g["slots"]
            with eng.Fori(0, U // n - 1) as i:
                for j in range(n):
                    body(i, j, True, True)
            for j in range(n):
                body(U // n - 1, j, j < n - 2, j < n - 1)

        def make_rest(eng, S, l, g, i, j, t):
            R = AB[g["mode"]]
            n, name = rest_no(g, l, i, j, t)
            lo = t * P if g["mode"] == "causal" else 0
            m = step_no(g, l, i, j, t)
            eng.wait_ge(S["exp"], at(m + 1))
            eng.wait_ge(S["pv"], at(m + 1 - 4))
            eng.tensor_tensor(R["rest"][t % 4][:, lo:T], R["p"][t % 4][:, lo:T], R["high"][t % 4][:, lo:T],
                              ALU.subtract).then_inc(S[name], 1)

        def attn_sp(sp, S, l, g):
            R = AB[g["mode"]]

            def load(i, j, start=False):
                u, s = g["slots"] * i + j, slot_sem(S, "load", j)
                rows = g["score_rows"]
                if g["slots"] > 4 and j >= 4:
                    sp.wait_ge(s, loads_in(g, l, i, j - 4))
                elif g["slots"] > 4 and not start:
                    sp.wait_ge(s, loads_in(g, l, i, j) - 3 * 16)
                sp.dma_start(R["q"][0:STACK, j, :],
                             q_stack[bass.ds(u, 1), :, 0:g["nq"]].rearrange("u r t -> (u r) t")).then_inc(s, 16)
                sp.dma_start(R["k"][0:rows, j, :],
                             k_stack[bass.ds(u, 1), 0:rows, 0:g["nk"]].rearrange("u r t -> (u r) t")).then_inc(s, 16)
                sp.dma_start(R["vc"][:, j, :, :].rearrange("p t d -> p (t d)"),
                             v_flat[bass.ds(u, 1), :, 0:g["nt"] * HD].rearrange("u p x -> (u p) x")).then_inc(s, 16)

            def row(i, j):
                s = slot_sem(S, "row", j)
                sp.wait_ge(S["split"], at(first(g, l) + g["slots"] * i + j + 1))
                for x in range(3):
                    sp.dma_start(R["q"][g["score_rows"] + x:g["score_rows"] + x + 1, j, :],
                                 R["ap"][0:g["nt"], j % 4, x, 0:g["qt"]]).then_inc(s, 16)

            def store(i, j):
                u, s = g["slots"] * i + j, slot_sem(S, "z", j)
                sp.wait_ge(S["oev"], at(g["before"]["oev"] + (l * U + u + 1) * g["evacs"]))
                for x in g["z_parts"]:
                    z = R["z"][x * HD:(x + 1) * HD, j % 2, 0:T]
                    if g["mode"] == "causal":
                        sp.dma_start(scrambled(z_scr[x])[bass.ds(u, 1), :, :, :].rearrange("u s h r -> (u h) s r"),
                                     z.rearrange("p (s r) -> p s r", s=8)).then_inc(s, 16)
                    else:
                        sp.dma_start(z_scr[x][bass.ds(u, 1), :, :].rearrange("u d t -> (u d) t"), z).then_inc(s, 16)

            def body(i, j, ahead, more):
                if ahead and not g["late"]:
                    row(i + (j + 2) // g["slots"], (j + 2) % g["slots"])
                if more and g["late"]:
                    row(i + (j + 1) // g["slots"], (j + 1) % g["slots"])
                store(i, j)

            sp.wait_ge(S["init"], at(g["before"]["init"] + (l + 1) * g["fills"]))
            for j in range(g["slots"]):
                load(0, j, True)
            row(0, 0)
            if not g["late"]:
                row(0, 1)
            n = g["slots"]
            with sp.Fori(0, U // n - 1) as i:
                for j in range(n):
                    body(i, j, True, True)
                    sp.wait_ge(S["pv"], at(step_no(g, l, i, j + 1, 0)))
                    load(i + 1, j)
            for j in range(n):
                body(U // n - 1, j, j < n - 2, j < n - 1)
            for x in range(2):
                sp.wait_ge(slot_sem(S, "z", x), at(g["before"]["z"] + (l + 1) * (U // 2) * len(g["z_parts"]), 16))

        def attn_pool(pool, S, l, g):
            R = AB[g["mode"]]
            fills = [(R["mh"], -BIG), (R["q"][STACK:STACK + 6, :, :], 1.0), (R["k"][STACK:STACK + 6, :, :], 1.0)]
            if g["mode"] == "window":
                fills += [(R["vf"][:, :, :, HD:3 * HD], 0.0), (R["vf"][:, :, :, 3 * HD:], 1.0)]
            else:
                fills += [(R["vb"][:, :, :, 3 * HD:], 1.0)]
            assert len(fills) == g["fills"]
            for x, (tile, value) in enumerate(fills):
                pool.memset(tile, value).then_inc(S["init"], 1)
                pool.wait_ge(S["init"], at(g["before"]["init"] + l * g["fills"] + x + 1))
                settled(pool)

            def values(i, j, fresh=False):
                u = first(g, l) + g["slots"] * i + j
                pool.wait_ge(slot_sem(S, "load", j), loads_in(g, l, i, j))
                settled(pool)
                v = R["vc"][:, j, :, :]
                if g["mode"] == "window":
                    if not fresh:
                        pool.wait_ge(S["pv"], at(step_no(g, l, i, j, 0) - 3 * g["steps"]))
                        settled(pool)
                    pool.tensor_copy(R["vf"][:, j % 4, :, 0:HD], v).then_inc(S["vpad"], 1)
                    return
                links = 5 * (g["slots"] * i + j + (g["before"]["calls"] - LAYERS) * U)

                def link(x, ins):
                    ins.then_inc(S["vchain"], 1)
                    pool.wait_ge(S["vchain"], at(links + x))
                    settled(pool)

                vb, vr = R["vb"][:, j % 4, :, :], R["vr"][:, j % 4, :, :]
                link(1, pool.tensor_copy(vb[:, :, 0:HD], v))
                link(2, pool.tensor_tensor(R["vt"], v, vb[:, :, 0:HD], ALU.subtract))
                link(3, pool.tensor_copy(vb[:, :, HD:2 * HD], R["vt"]))
                link(4, pool.tensor_tensor(vb[:, :, 2 * HD:3 * HD], R["vt"], vb[:, :, HD:2 * HD], ALU.subtract))
                link(5, pool.tensor_copy(vr[:, :, 0:HD], vb[:, :, 0:HD]))
                pool.tensor_copy(vr[:, :, HD:2 * HD], R["vt"]).then_inc(S["vpad"], 1)

            def split(i, j):
                u = first(g, l) + g["slots"] * i + j
                links = 3 * u
                pool.wait_ge(S["red"], at(g["before"]["red"] + (l * U + g["slots"] * i + j + 1) * (len(max_steps(g)) + 1)))
                settled(pool)
                rest = R["a"][0:g["nt"], j % 4, 0:g["qt"]]
                part = [R["ap"][0:g["nt"], j % 4, x, 0:g["qt"]] for x in range(3)]

                def link(x, ins):
                    ins.then_inc(S["chain"], 1)
                    pool.wait_ge(S["chain"], at(links + x))
                    settled(pool)

                link(1, pool.tensor_copy(part[0], rest))
                link(2, pool.tensor_tensor(rest, rest, part[0], ALU.subtract))
                link(3, pool.tensor_copy(part[1], rest))
                pool.tensor_tensor(part[2], rest, part[1], ALU.subtract).then_inc(S["split"], 1)

            def body(i, j, ahead, more):
                for t in range(g["steps"]):
                    if g["rest"][t] == "p":
                        make_rest(pool, S, l, g, i, j, t)
                    if more and t == 1 and g["late"]:
                        split(i + (j + 1) // g["slots"], (j + 1) % g["slots"])
                    if ahead and t == (0 if g["mode"] == "window" else 5):
                        values(i + (j + 2) // g["slots"], (j + 2) % g["slots"])

            values(0, 0, True)
            values(0, 1, True)
            if g["late"]:
                split(0, 0)
            walk(pool, g, body)

        def attn_pe(pe, S, l, g):
            R = AB[g["mode"]]
            MS = max_steps(g)
            NS = len(MS) + 1
            sr, er = g["score_rows"], g["score_rows"] + 3
            e_ring = 3 if g["mode"] == "window" else 2

            def max_step(i, j, s):
                if s == 0:
                    pe.wait_ge(slot_sem(S, "load", j), loads_in(g, l, i, j))
                pe.wait_ge(S["red"], at(g["before"]["red"] + (l * U + g["slots"] * i + j) * NS + s + 1 - 2))
                t, k0, w = MS[s]
                o = bank[:, (j * NS + s) % 2, :]
                if g["mode"] == "window":
                    pe.matmul(o[0:g["qt"], :], identb[0:g["qt"], 0:g["qt"]], band_q[0:g["qt"], :, :],
                              start=True, stop=False, skip_group_check=True)
                    for x in range(4):
                        c = (t + x) * g["qt"]
                        last = pe.matmul(o[0:g["qt"], x * P:(x + 1) * P], R["q"][0:sr, j, c:c + g["qt"]],
                                         R["k"][0:sr, j, c:c + P], start=False, stop=(x == 3),
                                         skip_group_check=True)
                else:
                    diagonal = g["mode"] == "causal" and k0 + w == (t + 1) * P
                    last = pe.matmul(o[:, 0:w], R["q"][0:sr, j, t * P:(t + 1) * P], R["k"][0:sr, j, k0:k0 + w],
                                     start=True, stop=True)
                    if diagonal:
                        last = pe.matmul(o[:, w - P:w], identb[:, :], causal_q[:, :], start=False, stop=True,
                                         skip_group_check=True)
                last.then_inc(S["mx"], 1)

            def turn_max(i, j):
                u = first(g, l) + g["slots"] * i + j
                pe.wait_ge(S["neg"], at(u + 1))
                pe.wait_ge(S["red"], at(g["before"]["red"] + (l * U + g["slots"] * i + j) * NS + NS - 2))
                pe.transpose(bank[0:g["nt"], (j * NS + NS - 1) % 2, 0:g["qt"]], R["m"][0:g["qt"], j % 4, 0:g["nt"]],
                             ident[0:g["qt"], 0:g["qt"]]).then_inc(S["mt"], 1)

            def score_step(i, j, t):
                m = step_no(g, l, i, j, t)
                if t == 0:
                    pe.wait_ge(slot_sem(S, "row", j), loads_in(g, l, i, j))
                pe.wait_ge(S["exp"], at(m + 1 - e_ring))
                if g["mode"] == "window":
                    o = bank[:, 2 + t, 0:4 * g["qt"]]
                    pe.matmul(o, identb[:, :], band_k[:, :, :], start=True, stop=False, skip_group_check=True)
                    for x in range(4):
                        c = (4 * t + x) * g["qt"]
                        last = pe.matmul(o[:, x * g["qt"]:(x + 1) * g["qt"]], R["k"][0:er, j, c:c + P],
                                         R["q"][0:er, j, c:c + g["qt"]], start=False, stop=(x == 3),
                                         skip_group_check=True)
                else:
                    lo = t * P if g["mode"] == "causal" else 0
                    for half in range(2):
                        c0, c1 = max(lo, half * CH), (half + 1) * CH
                        if c0 >= c1:
                            continue
                        diagonal = g["mode"] == "causal" and c0 == lo
                        o = bank[:, 2 + 2 * (t % 2) + half, :]
                        last = pe.matmul(o[:, c0 - half * CH:CH], R["k"][0:er, j, t * P:(t + 1) * P],
                                         R["q"][0:er, j, c0:c1], start=True, stop=True)
                        if diagonal:
                            last = pe.matmul(o[:, c0 - half * CH:c0 - half * CH + P], identb[:, :],
                                             causal_k[:, :], start=False, stop=True, skip_group_check=True)
                last.then_inc(S["sc"], 1)

            def value_step(i, j, t):
                u = first(g, l) + g["slots"] * i + j
                if t == 0:
                    pe.wait_ge(S["vpad"], at(u + 1))
                if g["mode"] == "window":
                    pe.wait_ge(S["oev"], at(step_no(g, l, i, j, t) + 1 - 3))
                elif t == 0:
                    pe.wait_ge(S["oev"], at(g["before"]["oev"] + (l * U + g["slots"] * i + j)))
                pe.wait_ge(S["exp"], at(step_no(g, l, i, j, t + 1)))
                if g["mode"] == "window":
                    for x in range(4):
                        last = pe.matmul(bank[0:Z_ROWS, 5 + t, x * g["qt"]:(x + 1) * g["qt"]],
                                         R["vf"][:, j % 4, 4 * t + x, :], R["p"][t][:, x * g["qt"]:(x + 1) * g["qt"]],
                                         start=True, stop=True)
                    last.then_inc(S["pv"], 1)
                    return
                lo = t * P if g["mode"] == "causal" else 0
                halves = [(half, max(lo, half * CH), (half + 1) * CH) for half in range(2) if lo < (half + 1) * CH]
                for half, c0, c1 in halves:
                    pe.matmul(bank[0:Z_ROWS, 6 + half, c0 - half * CH:CH], R["vb"][:, j % 4, t, :],
                              R["high"][t % 4][:, c0:c1], start=(t == 0), stop=(g["mode"] == "causal"),
                              skip_group_check=True)
                n, name = rest_no(g, l, i, j, t)
                pe.wait_ge(S[name], at(n))
                for half, c0, c1 in halves:
                    last = pe.matmul(bank[0:Z_ROWS, 6 + half, c0 - half * CH:CH], R["vr"][:, j % 4, t, :],
                                     R["rest"][t % 4][:, c0:c1], start=False,
                                     stop=(g["mode"] == "causal" or t == g["steps"] - 1), skip_group_check=True)
                last.then_inc(S["pv"], 1)

            def body(i, j, ahead, more):
                i2, j2 = i + (j + 2) // g["slots"], (j + 2) % g["slots"]
                for t in range(g["steps"]):
                    now = max_slice(g, t) if ahead else []
                    if more and t == 0 and g["late"]:
                        turn_max(i + (j + 1) // g["slots"], (j + 1) % g["slots"])
                    for x in range(3):
                        for s in now[x:x + 1]:
                            max_step(i2, j2, s)
                        if x == 0 and (more or t + g["ahead"] < g["steps"]):
                            score_step(*following(i, j, t, g["ahead"], g["steps"], g["slots"]))
                        if x == 1:
                            value_step(i, j, t)
                    if ahead and t == g["turn"] and not g["late"]:
                        turn_max(i2, j2)

            for j in range(2):
                for s in range(len(MS)):
                    max_step(0, j, s)
                if j == 0 or not g["late"]:
                    turn_max(0, j)
            for t in range(g["ahead"]):
                score_step(0, 0, t)
            walk(pe, g, body)

        def max_slice(g, t):
            if g["mode"] == "window":
                return [0, 1, 2] if t == 0 else []
            if g["mode"] == "full":
                return [2 * t, 2 * t + 1]
            return [2 * t, 2 * t + 1] if t < 6 else []

        def attn_act(act, S, l, g):
            R = AB[g["mode"]]
            ring = 3 if g["mode"] == "window" else 4
            settled(act)
            act.preload_act_table(ACT.Exp)

            def exp(i, j, t):
                m = step_no(g, l, i, j, t)
                act.wait_ge(S["sc"], at(m + 1))
                act.wait_ge(S["pv"], at(m + 1 - ring))
                if g["mode"] == "window":
                    o, x = R["p"][t], bank[:, 2 + t, 0:4 * g["qt"]]
                else:
                    lo = t * P if g["mode"] == "causal" else 0
                    o = R["p"][t % 4][:, lo:T]
                    b0 = 2 + 2 * (t % 2)
                    x = bank[:, b0:b0 + 2, :].rearrange("p a b -> p (a b)")[:, lo:T]
                act.activation(o, x, ACT.Exp, scale=SCALE).then_inc(S["exp"], 1)

            def sums(i, j, t):
                act.wait_ge(S["pv"], at(step_no(g, l, i, j, t + 1)))
                if t == 0 or g["mode"] != "window":
                    act.wait_ge(slot_sem(S, "z", j),
                                at(g["before"]["z"] + (l * (U // 2) + g["slots"] // 2 * i + j // 2) * len(g["z_parts"]), 16))
                z = R["z"][0:Z_ROWS, j % 2, :]
                if g["mode"] == "window":
                    w = 4 * g["qt"]
                    ins = act.activation(z[:, t * w:(t + 1) * w], bank[0:Z_ROWS, 5 + t, 0:w], ACT.Copy)
                elif g["mode"] == "causal":
                    ins = act.activation(z.rearrange("p (s r) -> p s r", s=8),
                                         bank[0:Z_ROWS, 6:8, :].rearrange("p a b -> p (a b)").rearrange(
                                             "p (r s) -> p s r", s=8), ACT.Copy)
                else:
                    ins = act.activation(z, bank[0:Z_ROWS, 6:8, :].rearrange("p a b -> p (a b)"), ACT.Copy)
                ins.then_inc(S["oev"], 1)

            def body(i, j, ahead, more):
                for t in range(g["steps"]):
                    if more or t + g["ahead"] < g["steps"]:
                        exp(*following(i, j, t, g["ahead"], g["steps"], g["slots"]))
                    if g["mode"] == "window" or t == g["steps"] - 1:
                        sums(i, j, t)

            for t in range(g["ahead"]):
                exp(0, 0, t)
            walk(act, g, body)

        def attn_dve(v, S, l, g):
            R = AB[g["mode"]]
            MS = max_steps(g)
            NS = len(MS) + 1

            def reduced(i, j):
                return g["before"]["red"] + (l * U + g["slots"] * i + j) * NS

            def maximum(i, j, s):
                t, k0, w = MS[s]
                v.wait_ge(S["mx"], at(g["before"]["mx"] + (l * U + g["slots"] * i + j) * len(MS) + s + 1))
                o = bank[:, (j * NS + s) % 2, :]
                if g["mode"] == "window":
                    ins = v.tensor_reduce(R["m"][0:g["qt"], j % 4, t:t + 4],
                                          o[0:g["qt"], :].rearrange("p (t k) -> p t k", t=4), AX_X, ALU.max)
                else:
                    ins = v.tensor_reduce(R["mh"][:, j % 4, t, k0 // CH:k0 // CH + 1], o[:, 0:w], AX_X, ALU.max)
                ins.then_inc(S["red"], 1)
                if s == len(MS) - 1:
                    v.wait_ge(S["red"], at(reduced(i, j) + NS - 1))
                    if g["mode"] == "window":
                        v.sem_inc(S["neg"], 1)
                    else:
                        v.tensor_reduce(R["m"][:, j % 4, 0:g["nt"]], R["mh"][:, j % 4, :, :], AX_X, ALU.max
                                        ).then_inc(S["neg"], 1)

            def split(i, j):
                u = first(g, l) + g["slots"] * i + j
                v.wait_ge(S["mt"], at(u + 1))
                mt = bank[0:g["nt"], (j * NS + NS - 1) % 2, 0:g["qt"]]
                rest = R["a"][0:g["nt"], j % 4, 0:g["qt"]]
                if g["late"]:
                    v.tensor_scalar(rest, mt, -1.0, None, ALU.mult).then_inc(S["red"], 1)
                    return
                part = [R["ap"][0:g["nt"], j % 4, x, 0:g["qt"]] for x in range(3)]
                v.tensor_scalar(part[0], mt, -1.0, None, ALU.mult).then_inc(S["chain"], 1)
                v.wait_ge(S["chain"], at(3 * u + 1))
                v.scalar_tensor_tensor(out=rest, in0=mt, scalar=-1.0, in1=part[0], op0=ALU.mult,
                                       op1=ALU.subtract).then_inc(S["red"], 1)
                v.wait_ge(S["red"], at(reduced(i, j) + NS))
                v.tensor_copy(part[1], rest).then_inc(S["chain"], 1)
                v.wait_ge(S["chain"], at(3 * u + 2))
                v.tensor_tensor(part[2], rest, part[1], ALU.subtract).then_inc(S["chain"], 1)
                v.wait_ge(S["chain"], at(3 * u + 3))
                v.sem_inc(S["split"], 1)

            def rest_of(i, j, t):
                if g["rest"][t] == "v":
                    make_rest(v, S, l, g, i, j, t)

            def body(i, j, ahead, more):
                i2, j2 = i + (j + 2) // g["slots"], (j + 2) % g["slots"]
                for t in range(g["steps"]):
                    now = max_slice(g, t) if ahead else []
                    if more and t == 0 and g["late"]:
                        split(i + (j + 1) // g["slots"], (j + 1) % g["slots"])
                    for s in now[0:1]:
                        maximum(i2, j2, s)
                    if more or t + 2 < g["steps"]:
                        rest_of(*following(i, j, t, 2, g["steps"], g["slots"]))
                    for s in now[1:]:
                        maximum(i2, j2, s)
                    if ahead and t == g["turn"] and not g["late"]:
                        split(i2, j2)

            for j in range(2):
                for s in range(len(MS)):
                    maximum(0, j, s)
                if j == 0 or not g["late"]:
                    split(0, j)
            rest_of(0, 0, 0)
            rest_of(0, 0, 1)
            walk(v, g, body)

        take = area()
        ou_n = take([2, CH])
        ou_n1 = take([2, CH])
        ou_n2 = take([2, CH])
        ou_d = take([2, CH])
        ou_z = take([2, CH])
        ou_r = take([2, CH])
        ou_t = take([2, CH])
        OU_NAMES = ["n1", "n2", "log", "rec", "dr", "newton", "raw", "z", "mm", "x"]
        OU_DMA = ["in0", "in1"]

        def out_loads(l, b, parts):
            if parts:
                return 2 * LAYERS * B + 4 * ((l - LAYERS) * B + b)
            return 2 * (l * B + b)

        def out_sp(sp, S, l, scramble=False, parts=True):
            with sp.Fori(0, B) as b:
                for g in range(2):
                    n = l * NCH + 2 * b + g
                    sp.wait_ge(S["z"], at(n + 1 - 2))
                    for buf, src in ((ou_d, z_scr[3]), (ou_n, z_scr[0]), (ou_n1, z_scr[1]), (ou_n2, z_scr[2]))[
                            0:4 if parts else 2]:
                        if scramble:
                            rows = scrambled(src).rearrange("u s h r -> u (s h) r").rearrange(
                                "(b k m) p r -> b m p k r", k=H // 2, m=2)
                            sp.dma_start(buf[:, g, :].rearrange("p (k r) -> p k r", r=P),
                                         rows[bass.ds(b, 1), g, :, :, :].rearrange("b p k r -> (b p) k r")
                                         ).then_inc(S["in0"] if g == 0 else S["in1"], 16)
                            continue
                        sp.dma_start(buf[:, g, :], src[bass.ds(b * H, H), :, g * CH:(g + 1) * CH].rearrange(
                            "u d t -> (u d) t")).then_inc(S["in0"] if g == 0 else S["in1"], 16)

        def out_act(act, S, l, parts=True):
            settled(act)
            act.preload_act_table_set("natural_log_exp_and_others")
            with act.Fori(0, B) as b:
                for g in range(2):
                    n = l * NCH + 2 * b + g
                    act.wait_ge(S["in0"] if g == 0 else S["in1"], at(out_loads(l, b + 1, parts), 16))
                    act.wait_ge(S["z"], at(n + 1 - 2))
                    act.activation(ou_r[:, g, :], ou_d[:, g, :], ACT.Ln).then_inc(S["log"], 1)
                    act.wait_ge(S["log"], at(n + 1))
                    act.activation(ou_r[:, g, :], ou_r[:, g, :], ACT.Exp, scale=-1.0).then_inc(S["rec"], 1)

        def out_pool(pool, S, l, parts=True):
            with pool.Fori(0, B) as b:
                for g in range(2):
                    n = l * NCH + 2 * b + g
                    if parts:
                        pool.wait_ge(S["in0"] if g == 0 else S["in1"], at(out_loads(l, b + 1, parts), 16))
                        pool.tensor_tensor(ou_n[:, g, :], ou_n[:, g, :], ou_n1[:, g, :], ALU.add).then_inc(S["n1"], 1)
                    pool.wait_ge(S["rec"], at(n + 1))
                    pool.wait_ge(S["z"], at(n + 1 - 2))
                    pool.tensor_tensor(ou_t[:, g, :], ou_d[:, g, :], ou_r[:, g, :], ALU.mult).then_inc(S["dr"], 1)
                    pool.wait_ge(S["dr"], at(n + 1))
                    settled(pool)
                    pool.tensor_scalar(ou_t[:, g, :], ou_t[:, g, :], -1.0, 2.0, ALU.mult, ALU.add
                                       ).then_inc(S["newton"], 1)

        def out_dve(v, S, l, bias, project=True, parts=True):
            def z(n, g):
                if parts:
                    v.wait_ge(S["n1"], at(n + 1 - LAYERS * NCH))
                    v.tensor_tensor(ou_n[:, g, :], ou_n[:, g, :], ou_n2[:, g, :], ALU.add).then_inc(S["n2"], 1)
                    v.wait_ge(S["n2"], at(n + 1 - LAYERS * NCH))
                v.wait_ge(S["rec"], at(n + 1))
                v.wait_ge(S["mm"], at(n + 1 - 2))
                v.tensor_tensor(ou_z[:, g, :], ou_n[:, g, :], ou_r[:, g, :], ALU.mult).then_inc(S["raw"], 1)
                v.wait_ge(S["raw"], at(n + 1))
                v.wait_ge(S["newton"], at(n + 1))
                v.tensor_tensor(ou_z[:, g, :], ou_z[:, g, :], ou_t[:, g, :], ALU.mult).then_inc(S["z"], 1)

            def add(n, g, c):
                x = xT[:, bass.ds(c * CH, CH)]
                if project:
                    v.wait_ge(S["mm"], at(n + 1))
                    v.scalar_tensor_tensor(out=x, in0=bank[:, g, :], scalar=bias, in1=x, op0=ALU.add,
                                           op1=ALU.add).then_inc(S["x"], 1)
                else:
                    v.wait_ge(S["z"], at(n + 1))
                    v.tensor_tensor(x, x, ou_z[:, g, :], ALU.add).then_inc(S["mm"], 1)

            with v.Fori(0, B) as b:
                n = l * NCH + 2 * b
                z(n, 0)
                z(n + 1, 1)
                add(n, 0, 2 * b)
                add(n + 1, 1, 2 * b + 1)

        def out_pe(pe, S, l, wo):
            with pe.Fori(0, B) as b:
                for g in range(2):
                    n = l * NCH + 2 * b + g
                    pe.wait_ge(S["z"], at(n + 1))
                    pe.wait_ge(S["x"], at(n + 1 - 2))
                    pe.matmul(bank[:, g, :], wo, ou_z[:, g, :], start=True, stop=True).then_inc(S["mm"], 1)

        take = area()
        ff_r = take([2, FB, CH])
        FF_NAMES = ["up", "act", "down", "x"]

        def ffn_pe(pe, S, l):
            def up(c, g):
                for k in range(FB):
                    pe.wait_ge(S["act"], at((l * NCH + c) * FB + k + 1 - 4))
                    pe.matmul(bank[:, k, :], w_tok1[:, k * P:(k + 1) * P], hT[:, bass.ds(c * CH, CH)],
                              start=True, stop=True).then_inc(S["up"], 1)

            def down(c, g):
                pe.wait_ge(S["x"], at(l * NCH + c + 1 - 2))
                for k in range(FB):
                    pe.wait_ge(S["act"], at((l * NCH + c) * FB + k + 1))
                    last = pe.matmul(bank[:, 4 + g, :], w_tok2[:, k, :], ff_r[:, g, k, :],
                                     start=(k == 0), stop=(k == FB - 1))
                last.then_inc(S["down"], 1)

            up(0, 0)
            with pe.Fori(0, NCH // 2 - 1) as i:
                up(2 * i + 1, 1)
                down(2 * i, 0)
                up(2 * i + 2, 0)
                down(2 * i + 1, 1)
            up(NCH - 1, 1)
            down(NCH - 2, 0)
            down(NCH - 1, 1)

        def ffn_act(act, S, l):
            with act.Fori(0, NCH // 2) as i:
                for g in range(2):
                    c = l * NCH + 2 * i + g
                    act.wait_ge(S["down"], at(c + 1 - 2))
                    for k in range(FB):
                        act.wait_ge(S["up"], at(c * FB + k + 1))
                        act.activation(ff_r[:, g, k, :], bank[:, k, :], ACT.Relu,
                                       bias=b1_tok[:, k:k + 1]).then_inc(S["act"], 1)

        def ffn_dve(v, S, l):
            with v.Fori(0, NCH // 2) as i:
                for g in range(2):
                    v.wait_ge(S["down"], at(l * NCH + 2 * i + g + 1))
                    x = xT[:, bass.ds((2 * i + g) * CH, CH)]
                    v.scalar_tensor_tensor(out=x, in0=bank[:, 4 + g, :], scalar=vec_tok[:, 5:6], in1=x,
                                           op0=ALU.add, op1=ALU.add).then_inc(S["x"], 1)

        NT_ = N // P
        take = area()
        ga_l = take([2, CH])
        ga_buf = [take([NT_ * E1]) for _ in range(6)]
        ga_m = [take([NT_]) for _ in range(4)]
        ga_out = take([4, P])
        GA_NAMES = ["mm", "lg", "turn", "tok", "chain", "shift", "exp", "gates", "rows", "copied"]
        GA_DMA = ["out"]

        def gate_views(E):
            return [x[:, 0:NT_ * E].rearrange("p (t e) -> p t e", e=E) for x in ga_buf]

        def gate_pe(pe, S, E, wr):
            with pe.Fori(0, NCH // 2) as i:
                for g in range(2):
                    n = 2 * i + g
                    pe.wait_ge(S["lg"], at(n + 1 - 2))
                    pe.matmul(bank[0:E, g, :], wr, hT[:, bass.ds(n * CH, CH)], start=True, stop=True
                              ).then_inc(S["mm"], 1)
                    pe.wait_ge(S["lg"], at(n + 1))
                    pe.wait_ge(S["tok"], at(n + 1 - 2))
                    settled(pe)
                    for t in range(4):
                        last = pe.transpose(bank[:, 2 + g, t * E:(t + 1) * E], ga_l[0:E, g, t * P:(t + 1) * P],
                                            ident[0:E, 0:E])
                    last.then_inc(S["turn"], 1)
            pe.wait_ge(S["gates"], at(1))
            for x in range(NT_ * E // P):
                last = pe.transpose(bank[:, 4, x * P:(x + 1) * P], ga_buf[5][:, x * P:(x + 1) * P], ident[:, :])
            last.then_inc(S["rows"], 1)

        def gate_act(act, S, E, bias):
            with act.Fori(0, NCH // 2) as i:
                for g in range(2):
                    n = 2 * i + g
                    act.wait_ge(S["mm"], at(n + 1))
                    act.wait_ge(S["turn"], at(n + 1 - 2))
                    act.activation(ga_l[0:E, g, :], bank[0:E, g, :], ACT.Identity, bias=bias).then_inc(S["lg"], 1)
            key = gate_views(E)[1]
            act.wait_ge(S["shift"], at(1))
            act.activation(key, key, ACT.Exp).then_inc(S["exp"], 1)

        def gate_dve(v, S, E):
            lt, key, order, first, second, w = gate_views(E)
            count = [0]

            def link(ins):
                ins.then_inc(S["chain"], 1)
                count[0] += 1
                v.wait_ge(S["chain"], at(count[0]))

            def wide(x):
                return x.unsqueeze(2).broadcast_to([P, NT_, E])

            def pick(one, source, top):
                link(v.tensor_reduce(top, source, AX_X, ALU.max))
                link(v.tensor_tensor(key, source, wide(top), ALU.is_equal))
                link(v.tensor_tensor(key, key, order, ALU.mult))
                link(v.tensor_reduce(ga_m[2], key, AX_X, ALU.max))
                link(v.tensor_tensor(one, order, wide(ga_m[2]), ALU.is_equal))

            for e in range(E):
                link(v.memset(order[:, :, e:e + 1], float(E - e)))
            with v.Fori(0, NCH // 2) as i:
                for g in range(2):
                    n = 2 * i + g
                    v.wait_ge(S["turn"], at(n + 1))
                    v.tensor_copy(ga_buf[0][:, bass.ds(n * 4 * E, 4 * E)], bank[:, 2 + g, 0:4 * E]
                                  ).then_inc(S["tok"], 1)
            v.wait_ge(S["tok"], at(NCH))
            pick(first, lt, ga_m[0])
            link(v.tensor_scalar(w, first, -1.0, 1.0, ALU.mult, ALU.add))
            link(v.tensor_tensor(w, w, lt, ALU.mult))
            link(v.scalar_tensor_tensor(out=w, in0=first, scalar=-BIG, in1=w, op0=ALU.mult, op1=ALU.add))
            pick(second, w, ga_m[1])
            link(v.tensor_tensor(w, first, second, ALU.add))
            link(v.tensor_tensor(key, lt, wide(ga_m[0]), ALU.subtract))
            v.sem_inc(S["shift"], 1)
            v.wait_ge(S["exp"], at(1))
            link(v.tensor_tensor(key, key, w, ALU.mult))
            link(v.tensor_reduce(ga_m[2], key, AX_X, ALU.add))
            link(v.reciprocal(ga_m[3], ga_m[2]))
            v.tensor_tensor(w, key, wide(ga_m[3]), ALU.mult).then_inc(S["gates"], 1)
            v.wait_ge(S["rows"], at(1))
            n = NT_ * E // P
            v.tensor_copy(ga_out[:, 0:n, :], bank[:, 4, 0:n * P].rearrange("p (a b) -> p a b", a=n)
                          ).then_inc(S["copied"], 1)

        def gate_sp(sp, S, E, scr):
            sp.wait_ge(S["copied"], at(1))
            sp.dma_start(scr.rearrange("t e p -> (t e) p").rearrange("(x r) p -> r x p", r=P),
                         ga_out[:, 0:NT_ * E // P, :]).then_inc(S["out"], 16)
            sp.wait_ge(S["out"], at(1, 16))

        take = area()
        mo_r = take([2, FB, CH])
        mo_g = take([4, CH])
        mo_t = take([2, CH])
        MO_NAMES = ["up", "act", "down", "t", "x"]
        MO_DMA = ["g0", "g1", "g2", "g3"]

        def moe_sp(sp, S):
            with sp.Fori(0, NCH) as c:
                for e in range(E0):
                    sp.wait_ge(S["t"], at(c * E0 + e + 1 - 4))
                    sp.dma_start(mo_g[:, e % 4, :].rearrange("p (t q) -> p t q", t=4),
                                 g0_scr[bass.ds(c * 4, 4), e, :].partition_broadcast(P)
                                 ).then_inc([S["g0"], S["g1"], S["g2"], S["g3"]][e % 4], 16)

        def moe_pe(pe, S):
            def up(c, e):
                for k in range(FB):
                    pe.wait_ge(S["act"], at((c * E0 + e) * FB + k + 1 - 4))
                    pe.matmul(bank[:, k, :], w_e1[:, e, k * P:(k + 1) * P], hT[:, bass.ds(c * CH, CH)],
                              start=True, stop=True).then_inc(S["up"], 1)

            def down(c, e):
                n = c * E0 + e
                pe.wait_ge(S["t"], at(n + 1 - 2))
                for k in range(FB):
                    pe.wait_ge(S["act"], at(n * FB + k + 1))
                    last = pe.matmul(bank[:, 4 + e % 2, :], w_e2[:, e, k, :], mo_r[:, e % 2, k, :],
                                     start=(k == 0), stop=(k == FB - 1))
                last.then_inc(S["down"], 1)

            up(0, 0)
            with pe.Fori(0, NCH - 1) as c:
                for e in range(E0):
                    if e < E0 - 1:
                        up(c, e + 1)
                    else:
                        up(c + 1, 0)
                    down(c, e)
            for e in range(E0):
                if e < E0 - 1:
                    up(NCH - 1, e + 1)
                down(NCH - 1, e)

        def moe_act(act, S):
            settled(act)
            act.preload_act_table(ACT.Gelu)
            with act.Fori(0, NCH) as c:
                for e in range(E0):
                    n = c * E0 + e
                    act.wait_ge(S["down"], at(n + 1 - 2))
                    for k in range(FB):
                        act.wait_ge(S["up"], at(n * FB + k + 1))
                        act.activation(mo_r[:, e % 2, k, :], bank[:, k, :], ACT.Gelu).then_inc(S["act"], 1)

        def moe_dve(v, S):
            with v.Fori(0, NCH) as c:
                for e in range(E0):
                    n = c * E0 + e
                    v.wait_ge(S["down"], at(n + 1))
                    v.wait_ge([S["g0"], S["g1"], S["g2"], S["g3"]][e % 4], at(c * 2 + e // 4 + 1, 16))
                    v.wait_ge(S["x"], at(n + 1 - 2))
                    v.tensor_tensor(mo_t[:, e % 2, :], bank[:, 4 + e % 2, :], mo_g[:, e % 4, :],
                                    ALU.mult).then_inc(S["t"], 1)
                    v.wait_ge(S["t"], at(n + 1))
                    x = xT[:, bass.ds(c * CH, CH)]
                    v.tensor_tensor(x, x, mo_t[:, e % 2, :], ALU.add).then_inc(S["x"], 1)

        E2 = E1 + 1
        ROWS = E2 * I1
        KB = -(-ROWS // P)
        GB = E1 * I1 // P
        take = area()
        sw_wg = take([ROWS])
        sw_wu = take([ROWS])
        sw_w2 = take([KB, P])
        sw_p = take([7, KB])
        sw_c = take([2, KB])
        sw_n = take([2, KB])
        sw_eb = take([P])
        sw_cw = take([CH])
        sw_g = take([4, CH])
        sw_gt = take([3, CH])
        sw_gg = take([5, CH])
        sw_sg = take([3, CH])
        sw_ut = take([3, CH])
        sw_u = take([5, CH])
        sw_t = take([2, CH])
        sw_o = take([3, CH])
        SW_NAMES = ["prep", "ones", "hg", "hu", "gt", "ut", "gg", "clip", "u", "sg", "t", "o", "down", "x"]
        SW_DMA = ["w", "g0", "g1", "g2", "g3", "cw"]

        def rows(k):
            return min(P, ROWS - k * P)

        def over(c, k, r):
            if k >= r:
                return at(c * KB + k + 1 - r)
            last = max(x for x in range(KB) if x % r == k)
            return at(c * KB + last + 1 - KB)

        def slot(k, r):
            return k % r if k < GB else r

        def over_slot(c, k, r):
            if k >= GB:
                return at(c * KB)
            if k >= r:
                return at(c * KB + k + 1 - r)
            last = max(x for x in range(GB) if x % r == k)
            return at(c * KB + last + 1 - KB)

        def segments(k):
            out, r = [], k * P
            while r < (k + 1) * P:
                end = min((k + 1) * P, (r // I1 + 1) * I1)
                out.append((r - k * P, end - r, r // I1))
                r = end
            return out

        def swi_sp(sp, S):
            for dst, src in ((sw_wg, A["sw1g"]), (sw_wu, A["sw1u"]), (sw_w2, A["sw2"]), (sw_p, A["sact"]),
                             (sw_eb[0:E2], A["sb2"])):
                sp.dma_start(dst, src).then_inc(S["w"], 16)
            sp.wait_ge(S["ones"], at(1))
            with sp.Fori(0, NCH) as c:
                sp.wait_ge(S["down"], at(c * KB))
                sp.dma_start(sw_cw[0:E1, :].rearrange("e (t q) -> e t q", t=4),
                             g1_scr[bass.ds(c * 4, 4), :, :].rearrange("t e q -> e t q")).then_inc(S["cw"], 16)
                for k in range(GB):
                    sp.wait_ge(S["u"], at(c * GB + k + 1 - 4))
                    for r, n, e in segments(k):
                        sp.dma_start(sw_g[r:r + n, k % 4, :].rearrange("p (t q) -> p t q", t=4),
                                     g1_scr[bass.ds(c * 4, 4), e, :].partition_broadcast(n)
                                     ).then_inc([S["g0"], S["g1"], S["g2"], S["g3"]][k % 4], 16)

        def swi_pool(pool, S):
            pool.memset(sw_cw[0:E2, :], 1.0).then_inc(S["ones"], 1)
            with pool.Fori(0, NCH) as c:
                for k in range(GB):
                    pool.wait_ge(S["clip"], at(c * KB + k + 1))
                    pool.wait_ge([S["g0"], S["g1"], S["g2"], S["g3"]][k % 4],
                                 at(2 * (c * (GB // 4) + k // 4 + 1), 16))
                    pool.tensor_tensor(sw_u[:, k % 4, :], sw_u[:, k % 4, :], sw_g[:, k % 4, :],
                                       ALU.mult).then_inc(S["u"], 1)

        def swi_pe(pe, S):
            def hidden(c, k):
                m = rows(k)
                for x, (w, done, read) in enumerate(((sw_wg, S["hg"], S["gt"]), (sw_wu, S["hu"], S["ut"]))):
                    pe.wait_ge(read, over(c, k, 3))
                    pe.matmul(bank[0:m, 3 * x + k % 3, :], w[:, k * P:k * P + m],
                              hT[:, bass.ds(c * CH, CH)], start=True, stop=True).then_inc(done, 1)

            def down(c, k):
                if k == 0:
                    pe.wait_ge(S["x"], at(c))
                    pe.wait_ge(S["cw"], at(c + 1, 16))
                    pe.matmul(bank[:, 6, :], sw_eb[0:E2, :], sw_cw[0:E2, :], start=True, stop=False)
                pe.wait_ge(S["o"], at(c * KB + k + 1))
                pe.matmul(bank[:, 6, :], sw_w2[0:rows(k), k, :], sw_o[0:rows(k), k % 3, :],
                          start=False, stop=(k == KB - 1)).then_inc(S["down"], 1)

            def chunk(c, more):
                for k in range(KB):
                    if k + 3 < KB:
                        hidden(c, k + 3)
                    elif more:
                        hidden(c + 1, k + 3 - KB)
                    down(c, k)

            pe.wait_ge(S["w"], at(5, 16))
            for k in range(3):
                hidden(0, k)
            with pe.Fori(0, NCH - 1) as c:
                chunk(c, True)
            chunk(NCH - 1, False)

        def swi_act(act, S):
            act.wait_ge(S["prep"], at(1))
            act.activation(sw_c, sw_c, ACT.Exp, scale=-1.0).then_inc(S["prep"], 1)
            act.wait_ge(S["prep"], at(2))
            act.activation(sw_c, sw_c, ACT.Ln, bias=one_t[:, 0:1]).then_inc(S["prep"], 1)
            act.preload_act_table(ACT.Sigmoid)

            def move(c, k):
                for x, (ready, done, read, dst) in enumerate(((S["hg"], S["gt"], S["gg"], sw_gt),
                                                              (S["hu"], S["ut"], S["clip"], sw_ut))):
                    m = rows(k)
                    act.wait_ge(ready, at(c * KB + k + 1))
                    act.wait_ge(read, over(c, k, 3))
                    act.activation(dst[0:m, k % 3, :], bank[0:m, 3 * x + k % 3, :], ACT.Identity,
                                   bias=sw_p[0:m, x, k:k + 1]).then_inc(done, 1)

            def chunk(c, more):
                for k in range(KB):
                    if k + 2 < KB:
                        move(c, k + 2)
                    elif more:
                        move(c + 1, k + 2 - KB)
                    m = rows(k)
                    act.wait_ge(S["gg"], at(c * KB + k + 1))
                    act.wait_ge(S["t"], over_slot(c, k, 2))
                    act.activation(sw_sg[0:m, slot(k, 2), :], sw_gg[0:m, slot(k, 4), :], ACT.Sigmoid,
                                   scale=sw_p[0:m, 2, k:k + 1]).then_inc(S["sg"], 1)

            act.wait_ge(S["prep"], at(8))
            move(0, 0)
            move(0, 1)
            with act.Fori(0, NCH - 1) as c:
                chunk(c, True)
            chunk(NCH - 1, False)

        def swi_dve(v, S):
            raw = sw_p[:, 5:7, :]
            v.wait_ge(S["w"], at(5, 16))
            v.scalar_tensor_tensor(out=sw_c, in0=raw, scalar=-1.0, in1=raw, op0=ALU.mult,
                                   op1=ALU.max).then_inc(S["prep"], 1)
            v.wait_ge(S["prep"], at(3))
            v.scalar_tensor_tensor(out=sw_c, in0=raw, scalar=0.0, in1=sw_c, op0=ALU.max,
                                   op1=ALU.add).then_inc(S["prep"], 1)
            v.wait_ge(S["prep"], at(4))
            v.tensor_scalar(sw_n, sw_c, -1.0, None, ALU.mult).then_inc(S["prep"], 1)
            for x, part in enumerate((sw_n[:, 1, :], sw_c[:, 1, :], sw_p[:, 1, :])):
                v.wait_ge(S["prep"], at(5 + x))
                v.tensor_tensor(part, part, sw_p[:, 4, :], ALU.add).then_inc(S["prep"], 1)
            v.wait_ge(S["prep"], at(8))

            def clip(c, k):
                n, m = c * KB + k, rows(k)
                v.wait_ge(S["gt"], at(n + 1))
                v.wait_ge(S["t"], over_slot(c, k, 4))
                v.tensor_scalar(sw_gg[0:m, slot(k, 4), :], sw_gt[0:m, k % 3, :], sw_c[0:m, 0, k:k + 1],
                                sw_n[0:m, 0, k:k + 1], ALU.min, ALU.max).then_inc(S["gg"], 1)
                v.wait_ge(S["ut"], at(n + 1))
                v.wait_ge(S["o"], over_slot(c, k, 4))
                v.tensor_scalar(sw_u[0:m, slot(k, 4), :], sw_ut[0:m, k % 3, :], sw_c[0:m, 1, k:k + 1],
                                sw_n[0:m, 1, k:k + 1], ALU.min, ALU.max).then_inc(S["clip"], 1)

            def product(c, k):
                n, m = c * KB + k, rows(k)
                v.wait_ge(S["sg"], at(n + 1))
                v.scalar_tensor_tensor(out=sw_t[0:m, k % 2, :], in0=sw_sg[0:m, slot(k, 2), :],
                                       scalar=sw_p[0:m, 3, k:k + 1], in1=sw_gg[0:m, slot(k, 4), :],
                                       op0=ALU.mult, op1=ALU.mult).then_inc(S["t"], 1)
                v.wait_ge(S["t"], at(n + 1))
                if k < GB:
                    v.wait_ge(S["u"], at(c * GB + k + 1))
                v.wait_ge(S["down"], over(c, k, 3))
                v.tensor_tensor(sw_o[0:m, k % 3, :], sw_t[0:m, k % 2, :], sw_u[0:m, slot(k, 4), :],
                                ALU.mult).then_inc(S["o"], 1)

            def chunk(c, more):
                for k in range(KB):
                    if k + 2 < KB:
                        clip(c, k + 2)
                    elif more:
                        clip(c + 1, k + 2 - KB)
                    product(c, k)
                v.wait_ge(S["down"], at((c + 1) * KB))
                x = xT[:, bass.ds(c * CH, CH)]
                v.tensor_tensor(x, x, bank[:, 6, :], ALU.add).then_inc(S["x"], 1)

            clip(0, 0)
            clip(0, 1)
            with v.Fori(0, NCH - 1) as c:
                chunk(c, True)
            chunk(NCH - 1, False)

        take = area()
        fi_s = take([2, CH])
        fi_o = take([2, CH])
        FI = sems("fi", ["staged", "turned", "copied"], ["out0", "out1"])

        def fin_dve(v):
            with v.Fori(0, NCH // 2) as i:
                for g in range(2):
                    v.wait_ge(FI["turned"], at(2 * i + g + 1 - 2))
                    v.tensor_copy(fi_s[:, g, :], xT[:, bass.ds((2 * i + g) * CH, CH)]).then_inc(FI["staged"], 1)

        def fin_pe(pe):
            with pe.Fori(0, NCH // 2) as i:
                for g in range(2):
                    pe.wait_ge(FI["staged"], at(2 * i + g + 1))
                    pe.wait_ge(FI["copied"], at(2 * i + g + 1 - 2))
                    for t in range(4):
                        last = pe.transpose(bank[:, g, t * P:(t + 1) * P], fi_s[:, g, t * P:(t + 1) * P], ident[:, :])
                    last.then_inc(FI["turned"], 1)

        def fin_act(act):
            with act.Fori(0, NCH // 2) as i:
                for g in range(2):
                    act.wait_ge(FI["turned"], at(2 * i + g + 1))
                    act.wait_ge(FI["out0"] if g == 0 else FI["out1"], at(i, 16))
                    act.activation(fi_o[:, g, :], bank[:, g, :], ACT.Copy).then_inc(FI["copied"], 1)

        def fin_sp(sp):
            with sp.Fori(0, NCH // 2) as i:
                for g in range(2):
                    sp.wait_ge(FI["copied"], at(2 * i + g + 1))
                    sp.dma_start(A["out"][bass.ds((2 * i + g) * CH, CH), :].rearrange("(t q) d -> q t d", q=P),
                                 fi_o[:, g, :].rearrange("p (t d) -> p t d", t=4)
                                 ).then_inc(FI["out0"] if g == 0 else FI["out1"], 16)
            sp.wait_ge(FI["out0"], at(NCH // 2, 16))
            sp.wait_ge(FI["out1"], at(NCH // 2, 16))

        win, full, causal = (GEO[m] for m in ("window", "full", "causal"))
        LN = sems("ln", LN_NAMES)
        QKV = sems("qkv", QK_NAMES, QK_DMA)
        AT = sems("attn", AT_NAMES, AT_DMA)
        OU = sems("out", OU_NAMES, OU_DMA)
        FT = sems("ffn_tok", FF_NAMES)
        G0, G1 = (sems(x, GA_NAMES, GA_DMA) for x in ("gate0", "gate1"))
        MO = sems("moe", MO_NAMES, MO_DMA)
        SW = sems("swi", SW_NAMES, SW_DMA)
        RE = sems("res", ["x"])
        v_flat = v_scr.rearrange("b h p x -> (b h) p x")
        N_W = 11
        ln_at = lambda k: NCH * k

        def vt(i):
            return vec_tok[:, i:i + 1]

        def va(i):
            return vec_a0[:, i:i + 1]

        def started(eng):
            eng.wait_ge(s_credit, 1)
            eng.wait_ge(s_const, 2)

        block = ctx.enter_context(nc.Block())

        @block.sync
        def _(sp):
            started(sp)
            em_sp(sp)
            for dst, src in ((w_a0, A["a0_w"]), (vec_a0, A["a0_v"]), (bv_a0, A["a0_bv"]), (w_a1, A["a1_w"]),
                             (wr0, A["wr0"]), (wr1, A["wr1"]), (br1, A["br1"]), (w_e1, A["e1"]), (w_e2, A["e2"])):
                sp.dma_start(dst[:], src).then_inc(s_w, 16)
            phase_end(sp, "em")
            with sp.Fori(0, LAYERS) as l:
                for dst, src in ((w_tok, A["tok_w"]), (w_tok1, A["tok_w1"]), (w_tok2, A["tok_w2"]),
                                 (vec_tok, A["tok_v"]), (b1_tok, A["tok_b1"])):
                    shape = "o p a b -> (o p) a b" if len(dst.shape) == 3 else "o p a -> (o p) a"
                    s = src[bass.ds(l, 1)]
                    sp.dma_start(dst[:], s.rearrange(shape)).then_inc(s_wl, 16)
                phase_end(sp, "ln1", l)
                qkv_sp(sp, QKV, l, win)
                phase_end(sp, "qkv", l)
                attn_sp(sp, AT, l, win)
                phase_end(sp, "attn", l)
                out_sp(sp, OU, l, parts=False)
                phase_end(sp, "out", l)
                phase_end(sp, "ln2", l)
                phase_end(sp, "ffn", l)
            phase_end(sp, "ln3")
            phase_end(sp, "res")
            phase_end(sp, "ln4")
            qkv_sp(sp, QKV, 0, full)
            phase_end(sp, "qkv0")
            attn_sp(sp, AT, 0, full)
            phase_end(sp, "attn0")
            out_sp(sp, OU, LAYERS)
            phase_end(sp, "out0")
            phase_end(sp, "ln5")
            gate_sp(sp, G0, E0, g0_scr)
            phase_end(sp, "gate0")
            moe_sp(sp, MO)
            phase_end(sp, "moe")
            phase_end(sp, "ln6")
            qkv_sp(sp, QKV, 0, causal)
            phase_end(sp, "qkv1")
            attn_sp(sp, AT, 0, causal)
            phase_end(sp, "attn1")
            out_sp(sp, OU, LAYERS + 1, scramble=True)
            phase_end(sp, "out1")
            phase_end(sp, "ln7")
            gate_sp(sp, G1, E1, g1_scr)
            phase_end(sp, "gate1")
            swi_sp(sp, SW)
            phase_end(sp, "swi")
            fin_sp(sp)

        @block.gpsimd
        def _(pool):
            for s, step in credited:
                pool.sem_inc(s, CREDIT * step)
            pool.sem_inc(s_credit, 1)
            pool.memset(ident[:, :], 0.0)
            pool.memset(identb[:, :], 0.0)
            pool.memset(mean_w[:, :], 1.0 / P)
            pool.memset(eps_t[:, :], EPS)
            pool.memset(one_t[:, :], 1.0)
            pool.memset(ones_row[:, :], 1.0)
            pool.memset(band_q[:, :, :], 0.0)
            pool.memset(band_k[:, :, :], 0.0)
            pool.memset(causal_q[:, :], 0.0)
            pool.memset(causal_k[:, :], 0.0).then_inc(s_const, 1)
            pool.wait_ge(s_const, 1)
            for j in range(SLOTS):
                for x in (2, 3):
                    pool.tensor_scalar(vr_all[:, j, :, x * HD:(x + 1) * HD],
                                       mean_w[:, :].rearrange("p (t d) -> p t d", d=HD), 0.0, float(x - 2),
                                       ALU.mult, ALU.add)

            def keep(m, pattern, base, mult):
                return pool.affine_select(out=m, in_=m, compare_op=ALU.is_ge, fill=OUTSIDE, base=base,
                                          pattern=pattern, channel_multiplier=mult)

            qt = P - 2 * WIN
            order = [0]

            def link(ins):
                ins.then_inc(s_pool, 1)
                order[0] += 1
                pool.wait_ge(s_pool, order[0])

            link(pool.affine_select(out=ident[:, :], in_=ident[:, :], compare_op=ALU.not_equal, fill=1.0,
                                    base=0, pattern=[[-1, P]], channel_multiplier=1))
            link(pool.affine_select(out=identb[:, :], in_=identb[:, :], compare_op=ALU.not_equal, fill=1.0,
                                    base=0, pattern=[[-1, P]], channel_multiplier=1))
            link(keep(band_q[:, :, :], [[0, 4], [1, P]], 0, -1))
            link(keep(band_q[:, :, :], [[0, 4], [-1, P]], 2 * WIN, 1))
            link(keep(band_k[:, :, :], [[0, 4], [-1, qt]], 0, 1))
            link(keep(band_k[:, :, :], [[0, 4], [1, qt]], 2 * WIN, -1))
            link(keep(causal_q[:, :], [[-1, P]], 0, 1))
            link(keep(causal_k[:, :], [[1, P]], 0, -1))
            pool.sem_inc(s_const, 1)
            em_pool(pool)
            phase_end(pool, "em")
            with pool.Fori(0, LAYERS) as l:
                ln_pool(pool, LN, l * (2 * NCH))
                phase_end(pool, "ln1", l)
                qkv_pool(pool, QKV, l, win)
                phase_end(pool, "qkv", l)
                attn_pool(pool, AT, l, win)
                phase_end(pool, "attn", l)
                out_pool(pool, OU, l, parts=False)
                phase_end(pool, "out", l)
                ln_pool(pool, LN, l * (2 * NCH) + NCH)
                phase_end(pool, "ln2", l)
                phase_end(pool, "ffn", l)
            ln_pool(pool, LN, ln_at(4))
            phase_end(pool, "ln3")
            phase_end(pool, "res")
            ln_pool(pool, LN, ln_at(5))
            phase_end(pool, "ln4")
            qkv_pool(pool, QKV, 0, full)
            phase_end(pool, "qkv0")
            attn_pool(pool, AT, 0, full)
            phase_end(pool, "attn0")
            out_pool(pool, OU, LAYERS)
            phase_end(pool, "out0")
            ln_pool(pool, LN, ln_at(6))
            phase_end(pool, "ln5")
            phase_end(pool, "gate0")
            phase_end(pool, "moe")
            ln_pool(pool, LN, ln_at(7))
            phase_end(pool, "ln6")
            qkv_pool(pool, QKV, 0, causal)
            phase_end(pool, "qkv1")
            attn_pool(pool, AT, 0, causal)
            phase_end(pool, "attn1")
            out_pool(pool, OU, LAYERS + 1)
            phase_end(pool, "out1")
            ln_pool(pool, LN, ln_at(8))
            phase_end(pool, "ln7")
            phase_end(pool, "gate1")
            swi_pool(pool, SW)
            phase_end(pool, "swi")

        @block.tensor
        def _(pe):
            started(pe)
            em_pe(pe)
            phase_end(pe, "em")
            with pe.Fori(0, LAYERS) as l:
                pe.wait_ge(s_wl, (l + 1) * 5 * 16)
                settled(pe)
                ln_pe(pe, LN, l * (2 * NCH), xT)
                phase_end(pe, "ln1", l)
                qkv_pe(pe, QKV, l, win, w_tok[:, 0, :], w_tok[:, 1, :], w_tok[:, 2, :])
                phase_end(pe, "qkv", l)
                attn_pe(pe, AT, l, win)
                phase_end(pe, "attn", l)
                out_pe(pe, OU, l, w_tok[:, 3, :])
                phase_end(pe, "out", l)
                ln_pe(pe, LN, l * (2 * NCH) + NCH, xT)
                phase_end(pe, "ln2", l)
                ffn_pe(pe, FT, l)
                phase_end(pe, "ffn", l)
            pe.wait_ge(s_w, 16 * 9)
            ln_pe(pe, LN, ln_at(4), xT)
            phase_end(pe, "ln3")
            phase_end(pe, "res")
            ln_pe(pe, LN, ln_at(5), hT)
            phase_end(pe, "ln4")
            qkv_pe(pe, QKV, 0, full, w_a0[:, 0, :], w_a0[:, 1, :], w_a0[:, 2, :], bv=bv_a0[:, :])
            phase_end(pe, "qkv0")
            attn_pe(pe, AT, 0, full)
            phase_end(pe, "attn0")
            out_pe(pe, OU, LAYERS, w_a0[:, 3, :])
            phase_end(pe, "out0")
            ln_pe(pe, LN, ln_at(6), xT)
            phase_end(pe, "ln5")
            gate_pe(pe, G0, E0, wr0[:, :])
            phase_end(pe, "gate0")
            moe_pe(pe, MO)
            phase_end(pe, "moe")
            ln_pe(pe, LN, ln_at(7), xT)
            phase_end(pe, "ln6")
            qkv_pe(pe, QKV, 0, causal, w_a1[:, 0, :], w_a1[:, 2, :], w_a1[:, 4, :],
                   wq2=w_a1[:, 1, :], wk2=w_a1[:, 3, :])
            phase_end(pe, "qkv1")
            attn_pe(pe, AT, 0, causal)
            phase_end(pe, "attn1")
            phase_end(pe, "out1")
            ln_pe(pe, LN, ln_at(8), xT)
            phase_end(pe, "ln7")
            gate_pe(pe, G1, E1, wr1[:, :])
            phase_end(pe, "gate1")
            swi_pe(pe, SW)
            phase_end(pe, "swi")
            fin_pe(pe)

        @block.vector
        def _(v):
            started(v)
            em_dve(v)
            phase_end(v, "em")
            with v.Fori(0, LAYERS) as l:
                ln_dve(v, LN, l * (2 * NCH), xT, l * (2 * NCH))
                phase_end(v, "ln1", l)
                qkv_dve(v, QKV, l, win)
                phase_end(v, "qkv", l)
                attn_dve(v, AT, l, win)
                phase_end(v, "attn", l)
                out_dve(v, OU, l, vt(4), parts=False)
                phase_end(v, "out", l)
                ln_dve(v, LN, l * (2 * NCH) + NCH, xT, l * (2 * NCH) + NCH)
                phase_end(v, "ln2", l)
                ffn_dve(v, FT, l)
                phase_end(v, "ffn", l)
            v.wait_ge(s_w, 16 * 9)
            ln_dve(v, LN, ln_at(4), xT)
            phase_end(v, "ln3")
            with v.Fori(0, NCH) as c:
                x = xT[:, bass.ds(c * CH, CH)]
                v.tensor_tensor(x, x, hT[:, bass.ds(c * CH, CH)], ALU.add).then_inc(RE["x"], 1)
            v.wait_ge(RE["x"], at(NCH))
            phase_end(v, "res")
            ln_dve(v, LN, ln_at(5), hT, ln_at(4))
            phase_end(v, "ln4")
            qkv_dve(v, QKV, 0, full)
            phase_end(v, "qkv0")
            attn_dve(v, AT, 0, full)
            phase_end(v, "attn0")
            out_dve(v, OU, LAYERS, va(4))
            phase_end(v, "out0")
            ln_dve(v, LN, ln_at(6), xT)
            phase_end(v, "ln5")
            gate_dve(v, G0, E0)
            phase_end(v, "gate0")
            moe_dve(v, MO)
            phase_end(v, "moe")
            ln_dve(v, LN, ln_at(7), xT)
            phase_end(v, "ln6")
            qkv_dve(v, QKV, 0, causal)
            phase_end(v, "qkv1")
            attn_dve(v, AT, 0, causal)
            phase_end(v, "attn1")
            out_dve(v, OU, LAYERS + 1, None, project=False)
            phase_end(v, "out1")
            ln_dve(v, LN, ln_at(8), xT)
            phase_end(v, "ln7")
            gate_dve(v, G1, E1)
            phase_end(v, "gate1")
            swi_dve(v, SW)
            phase_end(v, "swi")
            fin_dve(v)

        @block.scalar
        def _(act):
            started(act)
            em_act(act)
            phase_end(act, "em")
            with act.Fori(0, LAYERS) as l:
                act.wait_ge(s_wl, (l + 1) * 5 * 16)
                ln_act(act, LN, l * (2 * NCH), (vt(0), vt(1)))
                phase_end(act, "ln1", l)
                qkv_act(act, QKV, l, win)
                phase_end(act, "qkv", l)
                attn_act(act, AT, l, win)
                phase_end(act, "attn", l)
                out_act(act, OU, l, parts=False)
                phase_end(act, "out", l)
                ln_act(act, LN, l * (2 * NCH) + NCH, (vt(2), vt(3)))
                phase_end(act, "ln2", l)
                ffn_act(act, FT, l)
                phase_end(act, "ffn", l)
            act.wait_ge(s_w, 16 * 9)
            ln_act(act, LN, ln_at(4), None)
            phase_end(act, "ln3")
            phase_end(act, "res")
            ln_act(act, LN, ln_at(5), (va(0), va(1)))
            phase_end(act, "ln4")
            qkv_act(act, QKV, 0, full, bq=va(2), bk=va(3))
            phase_end(act, "qkv0")
            attn_act(act, AT, 0, full)
            phase_end(act, "attn0")
            out_act(act, OU, LAYERS)
            phase_end(act, "out0")
            ln_act(act, LN, ln_at(6), None)
            phase_end(act, "ln5")
            gate_act(act, G0, E0, 0.0)
            phase_end(act, "gate0")
            moe_act(act, MO)
            phase_end(act, "moe")
            ln_act(act, LN, ln_at(7), None)
            phase_end(act, "ln6")
            qkv_act(act, QKV, 0, causal)
            phase_end(act, "qkv1")
            attn_act(act, AT, 0, causal)
            phase_end(act, "attn1")
            out_act(act, OU, LAYERS + 1)
            phase_end(act, "out1")
            ln_act(act, LN, ln_at(8), None)
            phase_end(act, "ln7")
            gate_act(act, G1, E1, br1[:, 0:1])
            phase_end(act, "gate1")
            swi_act(act, SW)
            phase_end(act, "swi")
            fin_act(act)


def rope_tables():
    t = np.arange(T, dtype=np.float64)
    out = []
    for d in (P, P // 2):
        i = np.arange(d // 2, dtype=np.float64)
        theta = 10000.0 ** (-(2.0 * (i - 1.0))) / d
        ang = t[:, None] * theta[None, :]
        cos, sin = np.cos(ang).astype(np.float32), np.sin(ang).astype(np.float32)
        c = np.repeat(cos, 2, axis=1).T
        s = np.stack([sin, -sin], axis=-1).reshape(T, d).T
        out.append((c, s))
    return out


def kernel(**inputs):
    import concourse.bacc as _bacc
    from concourse import mybir as _mybir
    from concourse.bass_utils import run_bass_kernel_spmd as _run

    x = {k: np.asarray(v) for k, v in inputs.items()}

    def pack(*arrays):
        return np.ascontiguousarray(np.stack(arrays, axis=-1))

    def blocks(rows):
        short = -len(rows) % P
        rows = np.concatenate([rows, np.zeros((short, rows.shape[1]), rows.dtype)])
        return rows.reshape(-1, P, rows.shape[1]).transpose(1, 0, 2)

    def columns(w, order):
        return w[:, order]

    swap = np.arange(P) ^ 1
    twice = np.concatenate([np.arange(HD) + HD * (h // 2) for h in range(H)])
    twice_swap = np.concatenate([(np.arange(HD) ^ 1) + HD * (h // 2) for h in range(H)])
    t = "L0_tok_"
    a, f, g, m = "L0_attn_", "L0_ffn_", "L1_attn_", "L1_ffn_"
    (cq, sq), (ck, sk) = rope_tables()
    wx, bx = x[a + "w_xyz"], x[a + "b_xyz"]
    w1 = np.concatenate([x[m + "expert_w1"], x[m + "shared_w1"][None]])
    acts = np.concatenate([x[m + "expert_act"], x[m + "shared_act"][None]])
    b1 = np.concatenate([x[m + "expert_b1"], x[m + "shared_b1"][None]])
    w2 = np.concatenate([x[m + "expert_w2"], x[m + "shared_w2"][None]])
    arrays = {
        "x": x["x"], "mask": x["mask_BS_i1_0"], "tok": x[t + "tok_emb"], "pos": x[t + "pos_emb"],
        "tok_w": np.stack([x[t + "Wq"], x[t + "Wk"], x[t + "Wv"], x[t + "Wo"]], axis=2),
        "tok_w1": x[t + "W1"],
        "tok_w2": x[t + "W2"].reshape(LAYERS, FB, P, P).transpose(0, 2, 1, 3),
        "tok_v": pack(x[t + "ln1_g"], x[t + "ln1_b"], x[t + "ln2_g"], x[t + "ln2_b"], x[t + "bo"], x[t + "b2"]),
        "tok_b1": x[t + "b1"].reshape(LAYERS, FB, P).transpose(0, 2, 1),
        "a0_w": np.stack([wx[:, 0:P], wx[:, P:2 * P], wx[:, 2 * P:], x[a + "w_end"]], axis=1),
        "a0_v": pack(x[a + "gamma"], x[a + "beta"], bx[0:P], bx[P:2 * P], x[a + "b_end"]),
        "a0_bv": bx[None, 2 * P:],
        "a1_w": np.stack([x[g + "Wq"], columns(x[g + "Wq"], swap), columns(x[g + "Wk"], twice),
                          columns(x[g + "Wk"], twice_swap), columns(x[g + "Wv"], twice)], axis=1),
        "cos": np.stack([cq, ck[twice]]), "sin": np.stack([sq, sk[twice]]),
        "wr0": x[f + "Wr"].T, "wr1": x[m + "gate_w"], "br1": x[m + "gate_b"][:, None],
        "e1": x[f + "W1"].transpose(2, 0, 1),
        "e2": x[f + "W2"].reshape(E0, P, FB, P).transpose(3, 0, 2, 1),
        "sw1g": w1[..., 0::2].transpose(1, 0, 2).reshape(P, -1),
        "sw1u": w1[..., 1::2].transpose(1, 0, 2).reshape(P, -1),
        "sw2": blocks(w2.reshape(-1, P)),
        "sact": blocks(np.concatenate([b1[:, 0::2].reshape(-1, 1), b1[:, 1::2].reshape(-1, 1),
                                       np.repeat(acts, I1, axis=0)], axis=1)).transpose(0, 2, 1),
        "sb2": np.concatenate([x[m + "expert_b2"], x[m + "shared_b2"][None]]),
    }
    nc = _bacc.Bacc("TRN2", target_bir_lowering=False, num_devices=1)
    sent, aps = {}, {}
    for name, v in arrays.items():
        v = np.ascontiguousarray(v)
        sent[f"in_{name}"] = v
        aps[name] = nc.dram_tensor(f"in_{name}", v.shape, _mybir.dt.from_np(v.dtype), kind="ExternalInput").ap()
    aps["out"] = nc.dram_tensor("out", (N, P), _mybir.dt.float32, kind="ExternalOutput").ap()
    build(nc, aps)
    r = _run(nc, [sent], core_ids=[0])
    return r.results[0]["out"].reshape(B, T, P)
```

```python
from contextlib import ExitStack

import numpy as np

import concourse.bass as bass
from concourse import mybir

F32 = mybir.dt.float32
BF16 = mybir.dt.bfloat16
F32R = mybir.dt.float32r
I32 = mybir.dt.int32
ALU = mybir.AluOpType
ACT = mybir.ActivationFunctionType
AX_X = mybir.AxisListType.X

P = 128
B, T = 4, 1024
N = B * T
CH = 512
NCH = N // CH
H, HD = 8, 16
U = B * H
VOCAB = 8000
LAYERS = 2
FF = 512
FB = FF // P
E0 = 8
E1 = 16
I1 = 96
WIN = 16
EPS = 1e-5
CREDIT = 4
SLOTS = 4
REST_FULL = "vpvpvpvp"
REST_CAUSAL = "vpvpvpvp"
BIG = 3.0e38
TWO_ONES = float(np.array([0x3F803F80], np.uint32).view(np.float32)[0])
OUTSIDE = -1.0e30
MASKED = -4.0e9
MASK_PARTS = (-3992977408.0, -7012352.0, -10240.0)
SCALE = 0.25
Q_PARTS = (0, 0, 1, 1, 0, 2)
K_PARTS = (0, 1, 0, 1, 2, 0)
STACK = 16 * len(Q_PARTS)
Z_ROWS = 4 * HD


def geometry(mode):
    if mode == "window":
        qt, nt, pad = P - 2 * WIN, 12, WIN
        return dict(mode=mode, qt=qt, nt=nt, pad=pad, nq=qt * nt, nk=qt * (nt - 1) + P,
                               q_chunks=[(0, 352), (352, 352), (704, 320)],
                               k_chunks=[(0, 352), (352, 352), (704, 320)],
                               score_rows=STACK + 3, steps=3)
    return dict(mode=mode, qt=P, nt=T // P, pad=0, nq=T, nk=T,
                           q_chunks=[(0, CH), (CH, CH)], k_chunks=[(0, CH), (CH, CH)],
                           score_rows=STACK, steps=T // P)


def geometries():
    out = {}
    before = dict(calls=0, mx=0, red=0, sc=0, items=0, qk=0, chain=0, init=0, oev=0, stores=0, z=0, rest_v=0, rest_p=0, rest_n=0)
    for mode, calls in (("window", LAYERS), ("full", 1), ("causal", 1)):
        g = geometry(mode)
        g["before"] = dict(before)
        n_qk = len(g["q_chunks"]) + len(g["k_chunks"])
        g["splits"] = [2 + (2 if mode == "causal" else 1 if mode == "window" and k >= len(g["q_chunks"]) else 0)
                    for k in range(n_qk)]
        g["links"] = sum(g["splits"])
        g["stores"] = 13
        g["rest"] = {"window": "nnn", "full": REST_FULL, "causal": REST_CAUSAL}[mode]
        g["z_parts"] = (0, 3) if mode == "window" else (0, 1, 2, 3)
        g["ahead"] = 1 if mode == "window" else 3
        g["evacs"] = 3 if mode == "window" else 1
        g["slots"] = 2 * SLOTS if mode == "window" else SLOTS
        g["late"], g["turn"] = mode == "full", {"window": 1, "full": 0, "causal": 6}[mode]
        g["fills"] = 3 if mode == "window" else 2
        before["calls"] += calls
        before["init"] += calls * g["fills"]
        before["stores"] += calls * (B // 2) * g["stores"]
        before["oev"] += calls * U * g["evacs"]
        before["z"] += calls * (U // 2) * len(g["z_parts"])
        for who in "vpn":
            before["rest_" + who] += calls * U * g["rest"].count(who)
        before["mx"] += calls * U * len(max_steps(g))
        before["red"] += calls * U * (len(max_steps(g)) + 1)
        before["sc"] += calls * U * g["steps"]
        before["items"] += calls * B * (n_qk + g["nt"] // 4)
        before["qk"] += calls * B * n_qk
        before["chain"] += calls * B * g["links"]
        out[mode] = g
    return out


def max_steps(g):
    if g["mode"] == "window":
        return [(4 * s, 0, CH) for s in range(3)]
    out = []
    for t in range(g["nt"]):
        end = (t + 1) * P if g["mode"] == "causal" else T
        out += [(t, k0, min(CH, end - k0)) for k0 in range(0, end, CH)]
    return out


def at(n, step=1):
    return (n + CREDIT) * step


def build(nc, A):
    with ExitStack() as ctx:
        def sb(name, shape, dt=F32):
            return ctx.enter_context(nc.sbuf_tensor(name, shape, dt))

        credited = []

        def sem(name):
            return ctx.enter_context(nc.semaphore(name))

        def sems(prefix, names, dma=()):
            made = {}
            for n in list(names) + list(dma):
                made[n] = sem(f"{prefix}_{n}")
                credited.append((made[n], 16 if n in dma else 1))
            return made

        def scratch(name, shape, dt=F32):
            return nc.dram_tensor(name, shape, dt, kind="Internal").ap()

        q_stack = scratch("q_stack", (U, STACK, 1152), BF16)
        k_stack = scratch("k_stack", (U, STACK + 3, 1184), BF16)
        v_scr = scratch("v_scr", (B, H, P, 12 * HD))
        z_scr = [scratch(f"z_scr{x}", (U, HD, T)) for x in range(4)]
        g0_scr = scratch("g0_scr", (N // P, E0, P))
        g1_scr = scratch("g1_scr", (N // P, E1, P))

        xT = sb("xT", [P, N])
        hT = sb("hT", [P, N])
        ident = sb("ident", [P, P])
        identb = sb("identb", [P, P], BF16)
        mean_w = sb("mean_w", [P, P])
        band_q = sb("band_q", [P, 4, P], BF16)
        band_k = sb("band_k", [P, 4, P - 2 * WIN], BF16)
        causal_q = sb("causal_q", [P, P], BF16)
        causal_k = sb("causal_k", [P, P], BF16)
        mask_f = sb("mask_f", [P, B, 1184], BF16)
        eps_t = sb("eps_t", [P, 1])
        one_t = sb("one_t", [P, 1])
        ones_row = sb("ones_row", [1, P])
        w_tok = sb("w_tok", [P, 4, P])
        w_tok1 = sb("w_tok1", [P, FF])
        w_tok2 = sb("w_tok2", [P, FB, P])
        vec_tok = sb("vec_tok", [P, 6])
        b1_tok = sb("b1_tok", [P, FB])
        w_a0 = sb("w_a0", [P, 4, P])
        vec_a0 = sb("vec_a0", [P, 5])
        bv_a0 = sb("bv_a0", [1, P])
        w_a1 = sb("w_a1", [P, 5, P])
        wr0 = sb("wr0", [P, E0])
        wr1 = sb("wr1", [P, E1])
        br1 = sb("br1", [P, E1])
        w_e2 = sb("w_e2", [P, E0, FB, P])

        vr_all = sb("vr_all", [P, SLOTS, T // P, Z_ROWS], F32R)
        r_work = sb("r_work", [P, 10 * 1024], F32R)
        h_chunk = sb("h_chunk", [P, CH])

        WORK = 21 * 1024 - CH
        work = sb("work", [P, WORK])

        def area():
            used = [0]

            def take(shape, dt=F32, parts=P):
                n = int(np.prod(shape))
                words = n if dt in (F32, I32) else (n + 1) // 2
                v = work[0:parts, used[0]:used[0] + words]
                used[0] += words
                assert used[0] <= WORK, used[0]
                if dt != F32:
                    v = v.bitcast(dt)
                if len(shape) == 2:
                    v = v.rearrange("p (a b) -> p a b", a=shape[0])
                if len(shape) == 3:
                    v = v.rearrange("p (a b c) -> p a b c", a=shape[0], b=shape[1])
                return v

            return take

        bank = ctx.enter_context(nc.psum_tensor("bank", [P, 8, CH], F32))

        s_const = sem("const_ready")
        s_w = sem("weights_in")
        s_wl = sem("layer_weights_in")
        s_credit = sem("credit_given")
        s_pool = sem("masks_built")
        s_phase = sem("phase_end")
        s_settled = sem("settled")
        GEO = geometries()

        layer_phases = ("ln1", "qkv", "attn", "out", "ln2", "ffn")
        late_phases = ("ln3", "res", "ln4", "qkv0", "attn0", "out0", "ln5", "gate0", "moe",
                       "ln6", "qkv1", "attn1", "out1", "ln7", "gate1", "swi")

        def settled(eng):
            eng.sem_inc(s_settled, 1)

        def phase_end(eng, name, l=0):
            if name == "em":
                k = 1
            elif name in layer_phases:
                k = l * len(layer_phases) + (2 + layer_phases.index(name))
            else:
                k = 2 + LAYERS * len(layer_phases) + late_phases.index(name)
            settled(eng)
            eng.drain().then_inc(s_phase, 1)
            eng.wait_ge(s_phase, 5 * k)
            settled(eng)

        EM = sems("em", ["idx_f", "idx_T", "idx", "posed", "turned", "copied", "cur", "mask_rows"],
                  ["tok", "pos", "mask", "mask_out"])
        gathered = [sem(f"gathered{x}") for x in range(4)]
        TB = T // P
        take = area()
        em_tok = take([P], I32, 32)
        em_f = take([P], F32, 32)
        em_neg = take([P], F32, 32)
        em_idx = take([N // P], I32)
        em_cur = [take([TB], I32) for _ in range(2)]
        em_row = [take([P]) for _ in range(4)]
        em_sum = [take([P]) for _ in range(4)]
        em_pos = take([TB, P])
        em_mi = take([B, T], I32)
        em_mr = [take([3, 1184], BF16) for _ in range(B)]

        def em_batches(eng, body):
            with eng.Fori(0, B // 2) as i:
                for p in range(2):
                    body(2 * i + p, p)

        def em_sp(sp):
            sp.dma_start(em_tok, A["x"].rearrange("b (t p) -> (b t) p", p=P)).then_inc(EM["tok"], 16)
            sp.dma_start(em_pos, A["pos"].rearrange("(t p) d -> p t d", p=P)).then_inc(EM["pos"], 16)
            sp.dma_start(em_mi, A["mask"].partition_broadcast(P)).then_inc(EM["mask"], 16)

        def em_sp_mask(sp):
            for b in range(B):
                sp.wait_ge(EM["mask_rows"], at(3 * (b + 1) + 1))
                for h in range(H):
                    sp.dma_start(k_stack[b * H + h:b * H + h + 1, STACK:STACK + 3, :], em_mr[b][0:1, :, :]
                                 ).then_inc(EM["mask_out"], 16)
            sp.wait_ge(EM["mask_out"], at(B * H, 16))

        def em_pool(pool):
            pool.wait_ge(EM["idx"], at(1))

            def body(b, p):
                settled(pool)
                pool.tensor_copy(em_cur[p], em_idx[:, bass.ds(b * TB, TB)]).then_inc(EM["cur"], 1)
                pool.wait_ge(EM["cur"], at(b + 1))
                settled(pool)
                for t in range(TB):
                    g, n = t % 4, b * TB + t
                    pool.wait_ge(EM["posed"], at(n + 1 - 4))
                    settled(pool)
                    pool.indirect_dma_start(out=em_row[g], out_offset=None, in_=A["tok"],
                                            in_offset=bass.IndirectOffsetOnAxis(ap=em_cur[p][:, t:t + 1], axis=0),
                                            ).then_inc(gathered[g], 16)

            em_batches(pool, body)

        def em_pe(pe):
            pe.wait_ge(EM["idx_f"], at(5))
            pe.transpose(bank[:, 7, 0:32], em_f, ident[0:32, 0:32]).then_inc(EM["idx_T"], 1)

            def body(b, p):
                for t in range(TB):
                    g, n = t % 4, b * TB + t
                    pe.wait_ge(EM["posed"], at(n + 1))
                    pe.wait_ge(EM["copied"], at(n + 1 - 4))
                    pe.transpose(bank[:, g, 0:P], em_sum[g], ident[:, :]).then_inc(EM["turned"], 1)

            em_batches(pe, body)

        def em_dve(v):
            v.wait_ge(EM["tok"], at(1, 16))
            v.tensor_copy(em_f, em_tok).then_inc(EM["idx_f"], 1)
            v.wait_ge(EM["idx_f"], at(1))
            v.tensor_scalar(em_neg, em_f, 0.0, float(VOCAB), ALU.is_lt, ALU.mult).then_inc(EM["idx_f"], 1)
            v.wait_ge(EM["idx_f"], at(2))
            v.tensor_tensor(em_f, em_f, em_neg, ALU.add).then_inc(EM["idx_f"], 1)
            v.wait_ge(EM["idx_f"], at(3))
            v.tensor_scalar(em_f, em_f, 0.0, float(VOCAB - 1), ALU.max, ALU.min).then_inc(EM["idx_f"], 2)
            v.wait_ge(EM["idx_T"], at(1))
            v.tensor_copy(em_idx, bank[:, 7, 0:32]).then_inc(EM["idx"], 1)
            v.wait_ge(s_const, 1)
            v.wait_ge(EM["mask"], at(1, 16))
            for b in range(B):
                m = v.tensor_scalar(mask_f[:, b, WIN:WIN + T], em_mi[:, b, :], 0.0, None, ALU.is_gt)
            m.then_inc(EM["mask_rows"], 1)
            v.wait_ge(EM["mask_rows"], at(1))
            for b in range(B):
                for x in range(3):
                    v.tensor_scalar(em_mr[b][0:1, x, :], mask_f[0:1, b, :], -MASK_PARTS[x], MASK_PARTS[x],
                                    ALU.mult, ALU.add).then_inc(EM["mask_rows"], 1)
            v.wait_ge(EM["pos"], at(1, 16))

            def body(b, p):
                for t in range(TB):
                    g, n = t % 4, b * TB + t
                    v.wait_ge(gathered[g], (b * (TB // 4) + t // 4 + 1) * 16)
                    v.wait_ge(EM["turned"], at(n + 1 - 4))
                    v.tensor_tensor(em_sum[g], em_row[g], em_pos[:, t, :], ALU.add).then_inc(EM["posed"], 1)

            em_batches(v, body)

        def em_act(act):
            def body(b, p):
                for t in range(TB):
                    g, n = t % 4, b * TB + t
                    act.wait_ge(EM["turned"], at(n + 1))
                    act.activation(xT[:, bass.ds(n * P, P)], bank[:, g, 0:P], ACT.Copy).then_inc(EM["copied"], 1)

            em_batches(act, body)

        take = area()
        ln_c = take([NCH, CH])
        ln_sq = take([4, CH])
        ln_r = take([NCH, CH])
        ln_t = take([NCH, CH])
        ln_n = take([NCH, CH])
        LN_NAMES = ["mean", "cent", "sq", "var", "log", "rstd", "vr", "vrr", "newton", "raw", "norm", "done"]

        def ln_pe(pe, S, base, src):
            for c in range(NCH):
                if c >= 4:
                    pe.wait_ge(S["cent"], at(base + c + 1 - 4))
                pe.matmul(bank[:, c % 4, :], mean_w[:, :], src[:, c * CH:(c + 1) * CH],
                          start=True, stop=True).then_inc(S["mean"], 1)
            for c in range(NCH):
                pe.wait_ge(S["sq"], at(base + c + 1))
                if c >= 4:
                    pe.wait_ge(S["vr"], at(base + c + 1 - 4))
                pe.matmul(bank[:, 4 + c % 4, :], mean_w[:, :], ln_sq[:, c % 4, :],
                          start=True, stop=True).then_inc(S["var"], 1)

        def ln_pool(pool, S, base):
            for c in range(NCH):
                t = ln_t[:, c, :]
                pool.wait_ge(S["vr"], at(base + c + 1))
                pool.tensor_tensor(t, t, ln_r[:, c, :], ALU.mult).then_inc(S["vrr"], 1)
                pool.wait_ge(S["vrr"], at(base + c + 1))
                settled(pool)
                pool.tensor_scalar(t, t, -0.5, 1.5, ALU.mult, ALU.add).then_inc(S["newton"], 1)

        def ln_dve(v, S, base, src, gained=False):
            def norm(c):
                v.wait_ge(S["newton"], at(base + c + 1))
                v.wait_ge(S["raw"], at(base + c + 1))
                out = ln_n[:, c, :] if gained else hT[:, c * CH:(c + 1) * CH]
                v.tensor_tensor(out, ln_n[:, c, :], ln_t[:, c, :], ALU.mult).then_inc(S["norm"], 1)

            for c in range(NCH):
                v.wait_ge(S["mean"], at(base + c + 1))
                v.tensor_tensor(ln_c[:, c, :], src[:, c * CH:(c + 1) * CH], bank[:, c % 4, :],
                                ALU.subtract).then_inc(S["cent"], 1)
            for c in range(NCH):
                v.wait_ge(S["rstd"], at(base + c + 1))
                v.scalar_tensor_tensor(out=ln_t[:, c, :], in0=bank[:, 4 + c % 4, :], scalar=EPS,
                                       in1=ln_r[:, c, :], op0=ALU.add, op1=ALU.mult).then_inc(S["vr"], 1)
                v.tensor_tensor(ln_n[:, c, :], ln_c[:, c, :], ln_r[:, c, :], ALU.mult).then_inc(S["raw"], 1)
                if c:
                    norm(c - 1)
            norm(NCH - 1)

        def ln_act(act, S, base, gain, weights=None):
            def apply(c):
                act.wait_ge(S["norm"], at(base + c + 1))
                act.activation(hT[:, c * CH:(c + 1) * CH], ln_n[:, c, :], ACT.Identity,
                               bias=gain[1], scale=gain[0]).then_inc(S["done"], 1)

            settled(act)
            act.preload_act_table_set("natural_log_exp_and_others")
            for c in range(NCH):
                act.wait_ge(S["cent"], at(base + c + 1))
                if c >= 4:
                    act.wait_ge(S["var"], at(base + c + 1 - 4))
                act.activation(ln_sq[:, c % 4, :], ln_c[:, c, :], ACT.Square).then_inc(S["sq"], 1)
            for c in range(NCH):
                act.wait_ge(S["var"], at(base + c + 1))
                act.activation(ln_r[:, c, :], bank[:, 4 + c % 4, :], ACT.Ln,
                               bias=eps_t[:, 0:1]).then_inc(S["log"], 1)
                act.wait_ge(S["log"], at(base + c + 1))
                act.activation(ln_r[:, c, :], ln_r[:, c, :], ACT.Exp, scale=-0.5).then_inc(S["rstd"], 1)
                if c == 3 and weights is not None:
                    act.wait_ge(s_wl, weights)
                    settled(act)
                if gain is not None and c >= 3:
                    apply(c - 3)
            if gain is not None:
                for c in range(NCH - 3, NCH):
                    apply(c)

        def qkv_buffers(g):
            take = area()
            r = dict()
            r["h"] = take([2, 1184])
            r["f"] = take([3, CH])
            r["f2"] = take([3, CH]) if g["mode"] == "causal" else None
            r["qp"] = [take([3, 1152], BF16) for _ in range(2)]
            r["kp"] = [take([3, 1184], BF16) for _ in range(2)]
            r["v"] = [take([H, 12, HD]) for _ in range(2)]
            if g["mode"] == "causal":
                r["cos"] = take([2, T])
                r["sin"] = take([2, T])
            return r

        QB = {m: qkv_buffers(GEO[m]) for m in GEO}
        QK_NAMES = ["h", "h_used", "mm", "evac", "two", "q", "chain", "pads", "sin"]
        QK_DMA = ["stored0", "stored1", "rope"]

        def qkv_items(g):
            items = [("q", c, w) for c, w in g["q_chunks"]] + [("k", c, w) for c, w in g["k_chunks"]]
            return items + [("v", t, 4) for t in range(0, g["nt"], 4)]

        def n_qk(g):
            return len(g["q_chunks"]) + len(g["k_chunks"])

        def batch_no(g, l, b):
            return (g["before"]["calls"] + l) * B + b

        def pairs(eng, body):
            with eng.Fori(0, B // 2 - 1) as i:
                for p in range(2):
                    body(i, p, True)
            for p in range(2):
                body(B // 2 - 1, p, p == 0)

        def wait_stored(eng, S, l, g, i, p):
            eng.wait_ge(S[f"stored{p}"], at(g["before"]["stores"] + (l * (B // 2) + i) * g["stores"], 16))

        def qkv_pool(pool, S, l, g):
            R = QB[g["mode"]]

            items = qkv_items(g)

            def rotate(i, p, n):
                kind, c, w = items[n]
                b, f2 = 2 * i + p, R["f2"][:, n % 3, 0:w]
                pool.wait_ge(S["evac"], at(g["before"]["items"] + (l * B + b) * len(items) + n + 1))
                pool.tensor_tensor(f2, f2, R["sin"][:, 0 if kind == "q" else 1, c:c + w], ALU.mult
                                   ).then_inc(S["sin"], 1)

            def body(i, p, more):
                if g["mode"] == "causal":
                    rotate(i, p, 0)
                for n, (kind, c, w) in enumerate(items[:n_qk(g)]):
                    if g["mode"] == "causal" and n + 1 < n_qk(g):
                        rotate(i, p, n + 1)
                    parts = R["qp" if kind == "q" else "kp"][p]
                    c0 = c + (g["pad"] if kind == "k" else 0)
                    pool.wait_ge(S["two"], at(g["before"]["qk"] + (l * B + 2 * i + p) * n_qk(g) + n + 1))
                    pool.tensor_tensor(parts[:, 2, c0:c0 + w], R["f"][:, n % 3, 0:w], parts[:, 1, c0:c0 + w],
                                       ALU.subtract).then_inc(S["q"], 1)

            if g["mode"] == "causal":
                pool.wait_ge(S["rope"], at(2, 16))
            pairs(pool, body)

        def qkv_pe(pe, S, l, g, wq, wk, wv, wq2=None, wk2=None, bv=None):
            R = QB[g["mode"]]
            items = qkv_items(g)

            def body(i, p, more):
                b = 2 * i + p
                for n, (kind, c, w) in enumerate(items):
                    s = 2 * (n % 3)
                    m = g["before"]["items"] + (l * B + b) * len(items) + n
                    if kind == "v" and c == 0:
                        pe.wait_ge(S["h"], at(3 * (batch_no(g, l, b) + 1)))
                    pe.wait_ge(S["evac"], at(m + 1 - 3))
                    if kind == "v":
                        for t in range(4):
                            hs = R["h"][:, p, (c + t) * g["qt"]:(c + t) * g["qt"] + P]
                            last = pe.matmul(bank[:, s, t * P:(t + 1) * P], hs, wv,
                                             start=True, stop=bv is None)
                            if bv is not None:
                                last = pe.matmul(bank[:, s, t * P:(t + 1) * P], ones_row[:, :], bv,
                                                 start=False, stop=True)
                    else:
                        x = hT[:, bass.ds(b * T + c, w)]
                        last = pe.matmul(bank[:, s, 0:w], wq if kind == "q" else wk, x,
                                         start=True, stop=True)
                        if wq2 is not None:
                            last = pe.matmul(bank[:, s + 1, 0:w], wq2 if kind == "q" else wk2,
                                             x, start=True, stop=True)
                    last.then_inc(S["mm"], 1)
                pe.wait_ge(S["mm"], at(m + 1))
                pe.sem_inc(S["h_used"], 1)

            pairs(pe, body)

        def qkv_act(act, S, l, g, bq=0.0, bk=0.0):
            R = QB[g["mode"]]
            items = qkv_items(g)

            def body(i, p, more):
                b = 2 * i + p
                for n, (kind, c, w) in enumerate(items):
                    s = n % 3
                    m = g["before"]["items"] + (l * B + b) * len(items) + n
                    act.wait_ge(S["mm"], at(m + 1))
                    if kind == "v":
                        if c == 0:
                            wait_stored(act, S, l, g, i, p)
                        act.activation(R["v"][p][:, :, c:c + 4, :],
                                       bank[:, 2 * s, :].rearrange("p (t h d) -> p h t d", t=4, h=H),
                                       ACT.Copy).then_inc(S["evac"], 1)
                    else:
                        act.wait_ge(S["q"], at(g["before"]["qk"] + (l * B + b) * n_qk(g) + (n + 1 - 3 if n >= 3 else 0)))
                        last = act.activation(R["f"][:, s, 0:w], bank[:, 2 * s, 0:w], ACT.Identity,
                                              bias=bq if kind == "q" else bk)
                        if g["mode"] == "causal":
                            last = act.activation(R["f2"][:, s, 0:w], bank[:, 2 * s + 1, 0:w], ACT.Copy)
                        last.then_inc(S["evac"], 1)

            pairs(act, body)

        def qkv_dve(v, S, l, g):
            R = QB[g["mode"]]
            items = qkv_items(g)
            if g["mode"] == "causal":
                v.wait_ge(S["rope"], at(2, 16))
            if g["mode"] == "window":
                for p in range(2):
                    for pad in (R["qp"][p][:, :, T:g["nq"]], R["kp"][p][:, :, 0:WIN], R["kp"][p][:, :, WIN + T:g["nk"]]):
                        v.memset(pad, 0.0).then_inc(S["pads"], 1)

            def prepare(i, p):
                b = 2 * i + p
                n = batch_no(g, l, b)
                v.wait_ge(S["h_used"], at(n + 1 - 2))
                main = v.tensor_copy(R["h"][:, p, g["pad"]:g["pad"] + T], hT[:, bass.ds(b * T, T)])
                if not g["pad"]:
                    main.then_inc(S["h"], 3)
                    return
                main.then_inc(S["h"], 1)
                v.tensor_copy(R["h"][:, p, 0:g["pad"]],
                                 hT[:, bass.ds(b * T, 1)].broadcast_to([P, g["pad"]])).then_inc(S["h"], 1)
                v.tensor_copy(R["h"][:, p, g["pad"] + T:g["nk"]],
                                 hT[:, bass.ds(b * T + T - 1, 1)].broadcast_to([P, g["nk"] - g["pad"] - T])
                                 ).then_inc(S["h"], 1)

            def body(i, p, more):
                b = 2 * i + p
                if more:
                    prepare(i + p, 1 - p)
                count = [0]
                base = g["before"]["chain"] + (l * B + b) * g["links"]

                def link(ins):
                    ins.then_inc(S["chain"], 1)
                    count[0] += 1
                    v.wait_ge(S["chain"], at(base + count[0]))

                wait_stored(v, S, l, g, i, p)
                for n, (kind, c, w) in enumerate(items[:n_qk(g)]):
                    s = n % 3
                    f = R["f"][:, s, 0:w]
                    parts = R["qp" if kind == "q" else "kp"][p]
                    c0 = c + (g["pad"] if kind == "k" else 0)
                    v.wait_ge(S["evac"], at(g["before"]["items"] + (l * B + b) * len(items) + n + 1))
                    if g["mode"] == "causal":
                        f2 = R["f2"][:, s, 0:w]
                        of = 0 if kind == "q" else 1
                        link(v.tensor_tensor(f, f, R["cos"][:, of, c:c + w], ALU.mult))
                        v.wait_ge(S["sin"], at((l * B + b) * n_qk(g) + n + 1))
                        link(v.tensor_tensor(f, f, f2, ALU.add))
                    if g["mode"] == "window" and kind == "k":
                        link(v.tensor_tensor(f, f, mask_f[:, bass.ds(b, 1), c0:c0 + w].rearrange("p a t -> p (a t)"),
                                             ALU.mult))
                    link(v.tensor_copy(parts[:, 0, c0:c0 + w], f))
                    link(v.tensor_tensor(f, f, parts[:, 0, c0:c0 + w], ALU.subtract))
                    v.tensor_copy(parts[:, 1, c0:c0 + w], f).then_inc(S["two"], 1)

            prepare(0, 0)
            pairs(v, body)

        def qkv_sp(sp, S, l, g):
            R = QB[g["mode"]]
            items = qkv_items(g)
            if g["mode"] == "causal":
                sp.dma_start(R["cos"], A["cos"].rearrange("a p t -> p a t")).then_inc(S["rope"], 16)
                sp.dma_start(R["sin"], A["sin"].rearrange("a p t -> p a t")).then_inc(S["rope"], 16)
            if g["mode"] == "window":
                sp.wait_ge(S["pads"], at(6 * (l + 1)))
                settled(sp)

            def body(i, p, more):
                b = 2 * i + p
                n, stored = l * B + b, S[f"stored{p}"]
                sp.wait_ge(S["q"], at(g["before"]["qk"] + n * n_qk(g) + len(g["q_chunks"])))
                for j, part in enumerate(Q_PARTS):
                    sp.dma_start(q_stack[bass.ds(b * H, H), j * HD:(j + 1) * HD, 0:g["nq"]],
                                 R["qp"][p][:, part, 0:g["nq"]]).then_inc(stored, 16)
                sp.wait_ge(S["q"], at(g["before"]["qk"] + (n + 1) * n_qk(g)))
                for j, part in enumerate(K_PARTS):
                    sp.dma_start(k_stack[bass.ds(b * H, H), j * HD:(j + 1) * HD, 0:g["nk"]],
                                 R["kp"][p][:, part, 0:g["nk"]]).then_inc(stored, 16)
                sp.wait_ge(S["evac"], at(g["before"]["items"] + (n + 1) * len(items)))
                sp.dma_start(v_scr[bass.ds(b, 1), :, :, 0:g["nt"] * HD].rearrange("b h p x -> p (b h) x"),
                             R["v"][p][:, :, 0:g["nt"], :].rearrange("p h t d -> p h (t d)")).then_inc(stored, 16)

            pairs(sp, body)
            for p in range(2):
                wait_stored(sp, S, l, g, B // 2, p)

        def first(g, l):
            return (g["before"]["calls"] + l) * U

        def attn_buffers(g):
            take = area()
            r = dict()
            r["q"] = take([g["slots"], g["nq"]], BF16)
            r["k"] = take([g["slots"], g["nk"]], BF16)
            r["vc"] = take([g["slots"], g["nt"], HD])
            if g["mode"] == "window":
                r["vf"] = take([SLOTS, g["nt"], Z_ROWS])
                r["p"] = [take([4 * g["qt"]]) for _ in range(3)]
            else:
                r["vb"] = take([SLOTS, g["nt"], Z_ROWS], BF16)
                r["vr"] = vr_all
                r["vt"] = take([g["nt"], HD])
                r["p"] = [take([T]) for _ in range(4)]
                r["high"] = [x.bitcast(BF16)[:, 1:2 * T:2] for x in r["p"]]
                r["rest"] = [r_work[:, x * T:(x + 1) * T] for x in range(4)]
            r["mh"] = take([SLOTS, 8, 2])
            r["m"] = take([SLOTS, g["nt"]])
            r["a"] = take([SLOTS, P])
            r["ap"] = take([SLOTS, 3, P], BF16)
            r["z"] = take([2, 4 * g["qt"] * g["steps"] if g["mode"] == "window" else T])
            return r

        AB = {m: attn_buffers(GEO[m]) for m in GEO}
        AT_NAMES = ["init", "init_k", "vpad", "vchain", "mx", "red", "neg", "mt", "split", "sc", "exp", "rest_v", "rest_p",
                    "pv", "oev", "chain"]
        AT_DMA = ["load0", "load1", "load2", "load3", "row0", "row1", "row2", "row3", "z0", "z1"]

        def slot_sem(S, kind, j):
            return {"load": [S["load0"], S["load1"], S["load2"], S["load3"]], "row": [S["row0"], S["row1"], S["row2"], S["row3"]],
                    "z": [S["z0"], S["z1"]]}[kind][j % (2 if kind == "z" else 4)]

        def scrambled(scr):
            return scr.rearrange("u d t -> u (d t)").rearrange("u (s h r) -> u s h r", s=8, h=HD)

        def nth(g, l, i, j, ring):
            return (g["before"]["calls"] + l) * (U // ring) + i * (g["slots"] // ring) + j // ring + 1

        def loads_in(g, l, i, j):
            return at(3 * nth(g, l, i, j, 4), 16)

        def step_no(g, l, i, j, t):
            return g["before"]["sc"] + (l * U + g["slots"] * i + j) * g["steps"] + t

        def rest_no(g, l, i, j, t):
            who = g["rest"][t]
            n = g["before"]["rest_" + who] + (l * U + g["slots"] * i + j) * g["rest"].count(who)
            return n + g["rest"][0:t + 1].count(who), "rest_" + who

        def following(i, j, t, ahead, steps, slots):
            if t + ahead < steps:
                return i, j, t + ahead
            return i + (j + 1) // slots, (j + 1) % slots, t + ahead - steps

        def walk(eng, g, body):
            n = g["slots"]
            with eng.Fori(0, U // n - 1) as i:
                for j in range(n):
                    body(i, j, True, True)
            for j in range(n):
                body(U // n - 1, j, j < n - 2, j < n - 1)

        def make_rest(eng, S, l, g, i, j, t):
            R = AB[g["mode"]]
            n, name = rest_no(g, l, i, j, t)
            lo = t * P if g["mode"] == "causal" else 0
            m = step_no(g, l, i, j, t)
            eng.wait_ge(S["exp"], at(m + 1))
            eng.wait_ge(S["pv"], at(m + 1 - 4))
            eng.tensor_tensor(R["rest"][t % 4][:, lo:T], R["p"][t % 4][:, lo:T], R["high"][t % 4][:, lo:T],
                              ALU.subtract).then_inc(S[name], 1)

        def attn_sp(sp, S, l, g):
            R = AB[g["mode"]]

            def load(i, j, start=False):
                u, s = g["slots"] * i + j, slot_sem(S, "load", j)
                rows = g["score_rows"]
                if g["slots"] > 4 and j >= 4:
                    sp.wait_ge(s, loads_in(g, l, i, j - 4))
                elif g["slots"] > 4 and not start:
                    sp.wait_ge(s, loads_in(g, l, i, j) - 3 * 16)
                sp.dma_start(R["q"][0:STACK, j, :],
                             q_stack[bass.ds(u, 1), :, 0:g["nq"]].rearrange("u r t -> (u r) t")).then_inc(s, 16)
                sp.dma_start(R["k"][0:rows, j, :],
                             k_stack[bass.ds(u, 1), 0:rows, 0:g["nk"]].rearrange("u r t -> (u r) t")).then_inc(s, 16)
                sp.dma_start(R["vc"][:, j, :, :].rearrange("p t d -> p (t d)"),
                             v_flat[bass.ds(u, 1), :, 0:g["nt"] * HD].rearrange("u p x -> (u p) x")).then_inc(s, 16)

            def row(i, j):
                s = slot_sem(S, "row", j)
                sp.wait_ge(S["split"], at(first(g, l) + g["slots"] * i + j + 1))
                for x in range(3):
                    sp.dma_start(R["q"][g["score_rows"] + x:g["score_rows"] + x + 1, j, :],
                                 R["ap"][0:g["nt"], j % 4, x, 0:g["qt"]]).then_inc(s, 16)

            def store(i, j):
                u, s = g["slots"] * i + j, slot_sem(S, "z", j)
                sp.wait_ge(S["oev"], at(g["before"]["oev"] + (l * U + u + 1) * g["evacs"]))
                for x in g["z_parts"]:
                    z = R["z"][x * HD:(x + 1) * HD, j % 2, 0:T]
                    if g["mode"] == "causal":
                        sp.dma_start(scrambled(z_scr[x])[bass.ds(u, 1), :, :, :].rearrange("u s h r -> (u h) s r"),
                                     z.rearrange("p (s r) -> p s r", s=8)).then_inc(s, 16)
                    else:
                        sp.dma_start(z_scr[x][bass.ds(u, 1), :, :].rearrange("u d t -> (u d) t"), z).then_inc(s, 16)

            def body(i, j, ahead, more):
                if ahead and not g["late"]:
                    row(i + (j + 2) // g["slots"], (j + 2) % g["slots"])
                if more and g["late"]:
                    row(i + (j + 1) // g["slots"], (j + 1) % g["slots"])
                store(i, j)

            sp.wait_ge(S["init"], at(2 * (g["before"]["calls"] + l + 1)))
            sp.wait_ge(S["init_k"], at(g["before"]["init"] + (l + 1) * g["fills"]))
            for j in range(g["slots"]):
                load(0, j, True)
            row(0, 0)
            if not g["late"]:
                row(0, 1)
            n = g["slots"]
            with sp.Fori(0, U // n - 1) as i:
                for j in range(n):
                    body(i, j, True, True)
                    sp.wait_ge(S["pv"], at(step_no(g, l, i, j + 1, 0)))
                    load(i + 1, j)
            for j in range(n):
                body(U // n - 1, j, j < n - 2, j < n - 1)
            for x in range(2):
                sp.wait_ge(slot_sem(S, "z", x), at(g["before"]["z"] + (l + 1) * (U // 2) * len(g["z_parts"]), 16))

        def ones_rows(buf):
            return buf[STACK:STACK + 6, :, :].rearrange("p a b -> p (a b)").bitcast(F32)

        def attn_pool(pool, S, l, g):
            R = AB[g["mode"]]
            fills = [(R["mh"], -BIG), (ones_rows(R["q"]), TWO_ONES)]
            for x, (tile, value) in enumerate(fills):
                pool.memset(tile, value).then_inc(S["init"], 1)
                pool.wait_ge(S["init"], at(2 * (g["before"]["calls"] + l) + x + 1))
                settled(pool)

            def values(i, j, fresh=False):
                u = first(g, l) + g["slots"] * i + j
                pool.wait_ge(slot_sem(S, "load", j), loads_in(g, l, i, j))
                settled(pool)
                v = R["vc"][:, j, :, :]
                if g["mode"] == "window":
                    if not fresh:
                        pool.wait_ge(S["pv"], at(step_no(g, l, i, j, 0) - 3 * g["steps"]))
                        settled(pool)
                    pool.tensor_copy(R["vf"][:, j % 4, :, 0:HD], v).then_inc(S["vpad"], 1)
                    return
                links = 5 * (g["slots"] * i + j + (g["before"]["calls"] - LAYERS) * U)

                def link(x, ins):
                    ins.then_inc(S["vchain"], 1)
                    pool.wait_ge(S["vchain"], at(links + x))
                    settled(pool)

                vb, vr = R["vb"][:, j % 4, :, :], R["vr"][:, j % 4, :, :]
                link(1, pool.tensor_copy(vb[:, :, 0:HD], v))
                link(2, pool.tensor_tensor(R["vt"], v, vb[:, :, 0:HD], ALU.subtract))
                link(3, pool.tensor_copy(vb[:, :, HD:2 * HD], R["vt"]))
                link(4, pool.tensor_tensor(vb[:, :, 2 * HD:3 * HD], R["vt"], vb[:, :, HD:2 * HD], ALU.subtract))
                link(5, pool.tensor_copy(vr[:, :, 0:HD], vb[:, :, 0:HD]))
                pool.tensor_copy(vr[:, :, HD:2 * HD], R["vt"]).then_inc(S["vpad"], 1)

            def split(i, j):
                u = first(g, l) + g["slots"] * i + j
                links = 3 * u
                pool.wait_ge(S["red"], at(g["before"]["red"] + (l * U + g["slots"] * i + j + 1) * (len(max_steps(g)) + 1)))
                settled(pool)
                rest = R["a"][0:g["nt"], j % 4, 0:g["qt"]]
                part = [R["ap"][0:g["nt"], j % 4, x, 0:g["qt"]] for x in range(3)]

                def link(x, ins):
                    ins.then_inc(S["chain"], 1)
                    pool.wait_ge(S["chain"], at(links + x))
                    settled(pool)

                link(1, pool.tensor_copy(part[0], rest))
                link(2, pool.tensor_tensor(rest, rest, part[0], ALU.subtract))
                link(3, pool.tensor_copy(part[1], rest))
                pool.tensor_tensor(part[2], rest, part[1], ALU.subtract).then_inc(S["split"], 1)

            def body(i, j, ahead, more):
                for t in range(g["steps"]):
                    if g["rest"][t] == "p":
                        make_rest(pool, S, l, g, i, j, t)
                    if more and t == 1 and g["late"]:
                        split(i + (j + 1) // g["slots"], (j + 1) % g["slots"])
                    if ahead and t == (0 if g["mode"] == "window" else 5):
                        values(i + (j + 2) // g["slots"], (j + 2) % g["slots"])

            values(0, 0, True)
            values(0, 1, True)
            if g["late"]:
                split(0, 0)
            walk(pool, g, body)

        def attn_pe(pe, S, l, g):
            R = AB[g["mode"]]
            MS = max_steps(g)
            NS = len(MS) + 1
            sr, er = g["score_rows"], g["score_rows"] + 3
            e_ring = 3 if g["mode"] == "window" else 2

            def max_step(i, j, s):
                if s == 0:
                    pe.wait_ge(slot_sem(S, "load", j), loads_in(g, l, i, j))
                pe.wait_ge(S["red"], at(g["before"]["red"] + (l * U + g["slots"] * i + j) * NS + s + 1 - 2))
                t, k0, w = MS[s]
                o = bank[:, (j * NS + s) % 2, :]
                if g["mode"] == "window":
                    pe.matmul(o[0:g["qt"], :], identb[0:g["qt"], 0:g["qt"]], band_q[0:g["qt"], :, :],
                              start=True, stop=False, skip_group_check=True)
                    for x in range(4):
                        c = (t + x) * g["qt"]
                        last = pe.matmul(o[0:g["qt"], x * P:(x + 1) * P], R["q"][0:sr, j, c:c + g["qt"]],
                                         R["k"][0:sr, j, c:c + P], start=False, stop=(x == 3),
                                         skip_group_check=True)
                else:
                    diagonal = g["mode"] == "causal" and k0 + w == (t + 1) * P
                    last = pe.matmul(o[:, 0:w], R["q"][0:sr, j, t * P:(t + 1) * P], R["k"][0:sr, j, k0:k0 + w],
                                     start=True, stop=True)
                    if diagonal:
                        last = pe.matmul(o[:, w - P:w], identb[:, :], causal_q[:, :], start=False, stop=True,
                                         skip_group_check=True)
                last.then_inc(S["mx"], 1)

            def turn_max(i, j):
                u = first(g, l) + g["slots"] * i + j
                pe.wait_ge(S["neg"], at(u + 1))
                pe.wait_ge(S["red"], at(g["before"]["red"] + (l * U + g["slots"] * i + j) * NS + NS - 2))
                pe.transpose(bank[0:g["nt"], (j * NS + NS - 1) % 2, 0:g["qt"]], R["m"][0:g["qt"], j % 4, 0:g["nt"]],
                             ident[0:g["qt"], 0:g["qt"]]).then_inc(S["mt"], 1)

            def score_step(i, j, t):
                m = step_no(g, l, i, j, t)
                if t == 0:
                    pe.wait_ge(slot_sem(S, "row", j), loads_in(g, l, i, j))
                pe.wait_ge(S["exp"], at(m + 1 - e_ring))
                if g["mode"] == "window":
                    o = bank[:, 2 + t, 0:4 * g["qt"]]
                    pe.matmul(o, identb[:, :], band_k[:, :, :], start=True, stop=False, skip_group_check=True)
                    for x in range(4):
                        c = (4 * t + x) * g["qt"]
                        last = pe.matmul(o[:, x * g["qt"]:(x + 1) * g["qt"]], R["k"][0:er, j, c:c + P],
                                         R["q"][0:er, j, c:c + g["qt"]], start=False, stop=(x == 3),
                                         skip_group_check=True)
                else:
                    lo = t * P if g["mode"] == "causal" else 0
                    for half in range(2):
                        c0, c1 = max(lo, half * CH), (half + 1) * CH
                        if c0 >= c1:
                            continue
                        diagonal = g["mode"] == "causal" and c0 == lo
                        o = bank[:, 2 + 2 * (t % 2) + half, :]
                        last = pe.matmul(o[:, c0 - half * CH:CH], R["k"][0:er, j, t * P:(t + 1) * P],
                                         R["q"][0:er, j, c0:c1], start=True, stop=True)
                        if diagonal:
                            last = pe.matmul(o[:, c0 - half * CH:c0 - half * CH + P], identb[:, :],
                                             causal_k[:, :], start=False, stop=True, skip_group_check=True)
                last.then_inc(S["sc"], 1)

            def value_step(i, j, t):
                u = first(g, l) + g["slots"] * i + j
                if t == 0:
                    pe.wait_ge(S["vpad"], at(u + 1))
                if g["mode"] == "window":
                    pe.wait_ge(S["oev"], at(step_no(g, l, i, j, t) + 1 - 3))
                elif t == 0:
                    pe.wait_ge(S["oev"], at(g["before"]["oev"] + (l * U + g["slots"] * i + j)))
                pe.wait_ge(S["exp"], at(step_no(g, l, i, j, t + 1)))
                if g["mode"] == "window":
                    for x in range(4):
                        last = pe.matmul(bank[0:Z_ROWS, 5 + t, x * g["qt"]:(x + 1) * g["qt"]],
                                         R["vf"][:, j % 4, 4 * t + x, :], R["p"][t][:, x * g["qt"]:(x + 1) * g["qt"]],
                                         start=True, stop=True)
                    last.then_inc(S["pv"], 1)
                    return
                lo = t * P if g["mode"] == "causal" else 0
                halves = [(half, max(lo, half * CH), (half + 1) * CH) for half in range(2) if lo < (half + 1) * CH]
                for half, c0, c1 in halves:
                    pe.matmul(bank[0:Z_ROWS, 6 + half, c0 - half * CH:CH], R["vb"][:, j % 4, t, :],
                              R["high"][t % 4][:, c0:c1], start=(t == 0), stop=(g["mode"] == "causal"),
                              skip_group_check=True)
                n, name = rest_no(g, l, i, j, t)
                pe.wait_ge(S[name], at(n))
                for half, c0, c1 in halves:
                    last = pe.matmul(bank[0:Z_ROWS, 6 + half, c0 - half * CH:CH], R["vr"][:, j % 4, t, :],
                                     R["rest"][t % 4][:, c0:c1], start=False,
                                     stop=(g["mode"] == "causal" or t == g["steps"] - 1), skip_group_check=True)
                last.then_inc(S["pv"], 1)

            def body(i, j, ahead, more):
                i2, j2 = i + (j + 2) // g["slots"], (j + 2) % g["slots"]
                for t in range(g["steps"]):
                    now = max_slice(g, t) if ahead else []
                    if more and t == 0 and g["late"]:
                        turn_max(i + (j + 1) // g["slots"], (j + 1) % g["slots"])
                    for x in range(3):
                        for s in now[x:x + 1]:
                            max_step(i2, j2, s)
                        if x == 0 and (more or t + g["ahead"] < g["steps"]):
                            score_step(*following(i, j, t, g["ahead"], g["steps"], g["slots"]))
                        if x == 1:
                            value_step(i, j, t)
                    if ahead and t == g["turn"] and not g["late"]:
                        turn_max(i2, j2)

            for j in range(2):
                for s in range(len(MS)):
                    max_step(0, j, s)
                if j == 0 or not g["late"]:
                    turn_max(0, j)
            for t in range(g["ahead"]):
                score_step(0, 0, t)
            walk(pe, g, body)

        def max_slice(g, t):
            if g["mode"] == "window":
                return [0, 1, 2] if t == 0 else []
            if g["mode"] == "full":
                return [2 * t, 2 * t + 1]
            return [2 * t, 2 * t + 1] if t < 6 else []

        def attn_act(act, S, l, g):
            R = AB[g["mode"]]
            ring = 3 if g["mode"] == "window" else 4
            settled(act)
            act.preload_act_table(ACT.Exp)

            def exp(i, j, t):
                m = step_no(g, l, i, j, t)
                act.wait_ge(S["sc"], at(m + 1))
                act.wait_ge(S["pv"], at(m + 1 - ring))
                if g["mode"] == "window":
                    o, x = R["p"][t], bank[:, 2 + t, 0:4 * g["qt"]]
                else:
                    lo = t * P if g["mode"] == "causal" else 0
                    o = R["p"][t % 4][:, lo:T]
                    b0 = 2 + 2 * (t % 2)
                    x = bank[:, b0:b0 + 2, :].rearrange("p a b -> p (a b)")[:, lo:T]
                act.activation(o, x, ACT.Exp, scale=SCALE).then_inc(S["exp"], 1)

            def sums(i, j, t):
                act.wait_ge(S["pv"], at(step_no(g, l, i, j, t + 1)))
                if t == 0 or g["mode"] != "window":
                    act.wait_ge(slot_sem(S, "z", j),
                                at(g["before"]["z"] + (l * (U // 2) + g["slots"] // 2 * i + j // 2) * len(g["z_parts"]), 16))
                z = R["z"][0:Z_ROWS, j % 2, :]
                if g["mode"] == "window":
                    w = 4 * g["qt"]
                    ins = act.activation(z[:, t * w:(t + 1) * w], bank[0:Z_ROWS, 5 + t, 0:w], ACT.Copy)
                elif g["mode"] == "causal":
                    ins = act.activation(z.rearrange("p (s r) -> p s r", s=8),
                                         bank[0:Z_ROWS, 6:8, :].rearrange("p a b -> p (a b)").rearrange(
                                             "p (r s) -> p s r", s=8), ACT.Copy)
                else:
                    ins = act.activation(z, bank[0:Z_ROWS, 6:8, :].rearrange("p a b -> p (a b)"), ACT.Copy)
                ins.then_inc(S["oev"], 1)

            def body(i, j, ahead, more):
                for t in range(g["steps"]):
                    if more or t + g["ahead"] < g["steps"]:
                        exp(*following(i, j, t, g["ahead"], g["steps"], g["slots"]))
                    if g["mode"] == "window" or t == g["steps"] - 1:
                        sums(i, j, t)

            for t in range(g["ahead"]):
                exp(0, 0, t)
            walk(act, g, body)

        def attn_dve(v, S, l, g):
            R = AB[g["mode"]]
            MS = max_steps(g)
            NS = len(MS) + 1

            def reduced(i, j):
                return g["before"]["red"] + (l * U + g["slots"] * i + j) * NS

            def maximum(i, j, s):
                t, k0, w = MS[s]
                v.wait_ge(S["mx"], at(g["before"]["mx"] + (l * U + g["slots"] * i + j) * len(MS) + s + 1))
                o = bank[:, (j * NS + s) % 2, :]
                if g["mode"] == "window":
                    ins = v.tensor_reduce(R["m"][0:g["qt"], j % 4, t:t + 4],
                                          o[0:g["qt"], :].rearrange("p (t k) -> p t k", t=4), AX_X, ALU.max)
                else:
                    ins = v.tensor_reduce(R["mh"][:, j % 4, t, k0 // CH:k0 // CH + 1], o[:, 0:w], AX_X, ALU.max)
                ins.then_inc(S["red"], 1)
                if s == len(MS) - 1:
                    v.wait_ge(S["red"], at(reduced(i, j) + NS - 1))
                    if g["mode"] == "window":
                        v.sem_inc(S["neg"], 1)
                    else:
                        v.tensor_reduce(R["m"][:, j % 4, 0:g["nt"]], R["mh"][:, j % 4, :, :], AX_X, ALU.max
                                        ).then_inc(S["neg"], 1)

            def split(i, j):
                u = first(g, l) + g["slots"] * i + j
                v.wait_ge(S["mt"], at(u + 1))
                mt = bank[0:g["nt"], (j * NS + NS - 1) % 2, 0:g["qt"]]
                rest = R["a"][0:g["nt"], j % 4, 0:g["qt"]]
                if g["late"]:
                    v.tensor_scalar(rest, mt, -1.0, None, ALU.mult).then_inc(S["red"], 1)
                    return
                part = [R["ap"][0:g["nt"], j % 4, x, 0:g["qt"]] for x in range(3)]
                v.tensor_scalar(part[0], mt, -1.0, None, ALU.mult).then_inc(S["chain"], 1)
                v.wait_ge(S["chain"], at(3 * u + 1))
                v.scalar_tensor_tensor(out=rest, in0=mt, scalar=-1.0, in1=part[0], op0=ALU.mult,
                                       op1=ALU.subtract).then_inc(S["red"], 1)
                v.wait_ge(S["red"], at(reduced(i, j) + NS))
                v.tensor_copy(part[1], rest).then_inc(S["chain"], 1)
                v.wait_ge(S["chain"], at(3 * u + 2))
                v.tensor_tensor(part[2], rest, part[1], ALU.subtract).then_inc(S["chain"], 1)
                v.wait_ge(S["chain"], at(3 * u + 3))
                v.sem_inc(S["split"], 1)

            def rest_of(i, j, t):
                if g["rest"][t] == "v":
                    make_rest(v, S, l, g, i, j, t)

            def body(i, j, ahead, more):
                i2, j2 = i + (j + 2) // g["slots"], (j + 2) % g["slots"]
                for t in range(g["steps"]):
                    now = max_slice(g, t) if ahead else []
                    if more and t == 0 and g["late"]:
                        split(i + (j + 1) // g["slots"], (j + 1) % g["slots"])
                    for s in now:
                        maximum(i2, j2, s)
                    if more or t + 2 < g["steps"]:
                        rest_of(*following(i, j, t, 2, g["steps"], g["slots"]))
                    if ahead and t == g["turn"] and not g["late"]:
                        split(i2, j2)

            fills = [(ones_rows(R["k"]), TWO_ONES)]
            if g["mode"] == "window":
                fills += [(R["vf"][:, :, :, HD:3 * HD], 0.0), (R["vf"][:, :, :, 3 * HD:], 1.0)]
            else:
                fills += [(R["vb"][:, :, :, 3 * HD:], 1.0)]
            assert len(fills) == g["fills"]
            for tile, value in fills:
                v.memset(tile, value).then_inc(S["init_k"], 1)
            for j in range(2):
                for s in range(len(MS)):
                    maximum(0, j, s)
                if j == 0 or not g["late"]:
                    split(0, j)
            rest_of(0, 0, 0)
            rest_of(0, 0, 1)
            walk(v, g, body)

        OR = 4
        take = area()
        ou_n = take([OR, CH])
        ou_n1 = take([OR, CH])
        ou_n2 = take([OR, CH])
        ou_d = take([OR, CH])
        ou_z = take([OR, CH])
        ou_r = take([OR, CH])
        ou_t = take([OR, CH])
        OU_NAMES = ["n1", "n2", "log", "rec", "dr", "newton", "raw", "z", "mm", "x"]
        OU_DMA = ["in0", "in1", "in2", "in3"]

        def out_in(S, l, c, parts):
            uses = NCH // OR
            before = 2 * uses * (LAYERS if parts else l) + (4 * uses * (l - LAYERS) if parts else 0)
            return S[f"in{c % OR}"], at(before + (4 if parts else 2) * (c // OR + 1), 16)

        def out_sp(sp, S, l, scramble=False, parts=True):
            for c in range(NCH):
                b, g, s = c // 2, c % 2, S[f"in{c % OR}"]
                if c >= OR:
                    sp.wait_ge(S["z"], at(l * NCH + c + 1 - OR))
                for buf, src in ((ou_d, z_scr[3]), (ou_n, z_scr[0]), (ou_n1, z_scr[1]), (ou_n2, z_scr[2]))[
                        0:4 if parts else 2]:
                    if scramble:
                        rows = scrambled(src).rearrange("u s h r -> u (s h) r").rearrange(
                            "(b k m) p r -> b m p k r", k=H // 2, m=2)
                        sp.dma_start(buf[:, c % OR, :].rearrange("p (k r) -> p k r", r=P), rows[b, g, :, :, :]
                                     ).then_inc(s, 16)
                    else:
                        sp.dma_start(buf[:, c % OR, :], src[b * H:(b + 1) * H, :, g * CH:(g + 1) * CH].rearrange(
                            "u d t -> (u d) t")).then_inc(s, 16)

        def out_act(act, S, l, parts=True):
            settled(act)
            act.preload_act_table_set("natural_log_exp_and_others")
            for c in range(NCH):
                n, g = l * NCH + c, c % OR
                act.wait_ge(*out_in(S, l, c, parts))
                if c >= OR:
                    act.wait_ge(S["z"], at(n + 1 - OR))
                act.activation(ou_r[:, g, :], ou_d[:, g, :], ACT.Ln).then_inc(S["log"], 1)
                act.wait_ge(S["log"], at(n + 1))
                act.activation(ou_r[:, g, :], ou_r[:, g, :], ACT.Exp, scale=-1.0).then_inc(S["rec"], 1)

        def out_pool(pool, S, l, parts=True):
            for c in range(NCH):
                n, g = l * NCH + c, c % OR
                if parts:
                    pool.wait_ge(*out_in(S, l, c, parts))
                    pool.tensor_tensor(ou_n[:, g, :], ou_n[:, g, :], ou_n1[:, g, :], ALU.add).then_inc(S["n1"], 1)
                pool.wait_ge(S["rec"], at(n + 1))
                if c >= OR:
                    pool.wait_ge(S["z"], at(n + 1 - OR))
                pool.tensor_tensor(ou_t[:, g, :], ou_d[:, g, :], ou_r[:, g, :], ALU.mult).then_inc(S["dr"], 1)
                pool.wait_ge(S["dr"], at(n + 1))
                settled(pool)
                pool.tensor_scalar(ou_t[:, g, :], ou_t[:, g, :], -1.0, 2.0, ALU.mult, ALU.add
                                   ).then_inc(S["newton"], 1)

        def out_dve(v, S, l, bias, project=True, parts=True):
            def raw(c):
                n, g = l * NCH + c, c % OR
                if parts:
                    v.wait_ge(S["n1"], at(n + 1 - LAYERS * NCH))
                    v.tensor_tensor(ou_n[:, g, :], ou_n[:, g, :], ou_n2[:, g, :], ALU.add).then_inc(S["n2"], 1)
                    v.wait_ge(S["n2"], at(n + 1 - LAYERS * NCH))
                v.wait_ge(S["rec"], at(n + 1))
                if c >= OR:
                    v.wait_ge(S["mm"], at(n + 1 - OR))
                v.tensor_tensor(ou_z[:, g, :], ou_n[:, g, :], ou_r[:, g, :], ALU.mult).then_inc(S["raw"], 1)

            def z(c):
                n, g = l * NCH + c, c % OR
                v.wait_ge(S["raw"], at(n + 1))
                v.wait_ge(S["newton"], at(n + 1))
                v.tensor_tensor(ou_z[:, g, :], ou_z[:, g, :], ou_t[:, g, :], ALU.mult).then_inc(S["z"], 1)

            def add(c):
                n, g = l * NCH + c, c % OR
                x = xT[:, c * CH:(c + 1) * CH]
                if project:
                    v.wait_ge(S["mm"], at(n + 1))
                    v.scalar_tensor_tensor(out=x, in0=bank[:, g, :], scalar=bias, in1=x, op0=ALU.add,
                                           op1=ALU.add).then_inc(S["x"], 1)
                else:
                    v.wait_ge(S["z"], at(n + 1))
                    v.tensor_tensor(x, x, ou_z[:, g, :], ALU.add).then_inc(S["mm"], 1)

            for c in range(NCH + 3):
                if c >= 3:
                    add(c - 3)
                if c < NCH:
                    raw(c)
                if 1 <= c <= NCH:
                    z(c - 1)

        def out_pe(pe, S, l, wo):
            for c in range(NCH):
                n, g = l * NCH + c, c % OR
                pe.wait_ge(S["z"], at(n + 1))
                if c >= OR:
                    pe.wait_ge(S["x"], at(n + 1 - OR))
                pe.matmul(bank[:, g, :], wo, ou_z[:, g, :], start=True, stop=True).then_inc(S["mm"], 1)

        take = area()
        ff_r = take([2, FB, CH])
        FF_NAMES = ["up", "act", "down", "x"]

        def ffn_pe(pe, S, l):
            def up(c, g):
                for k in range(FB):
                    pe.wait_ge(S["act"], at((l * NCH + c) * FB + k + 1 - 4))
                    pe.matmul(bank[:, k, :], w_tok1[:, k * P:(k + 1) * P], hT[:, bass.ds(c * CH, CH)],
                              start=True, stop=True).then_inc(S["up"], 1)

            def down(c, g):
                pe.wait_ge(S["x"], at(l * NCH + c + 1 - 2))
                for k in range(FB):
                    pe.wait_ge(S["act"], at((l * NCH + c) * FB + k + 1))
                    last = pe.matmul(bank[:, 4 + g, :], w_tok2[:, k, :], ff_r[:, g, k, :],
                                     start=(k == 0), stop=(k == FB - 1))
                last.then_inc(S["down"], 1)

            up(0, 0)
            with pe.Fori(0, NCH // 2 - 1) as i:
                up(2 * i + 1, 1)
                down(2 * i, 0)
                up(2 * i + 2, 0)
                down(2 * i + 1, 1)
            up(NCH - 1, 1)
            down(NCH - 2, 0)
            down(NCH - 1, 1)

        def ffn_act(act, S, l):
            with act.Fori(0, NCH // 2) as i:
                for g in range(2):
                    c = l * NCH + 2 * i + g
                    act.wait_ge(S["down"], at(c + 1 - 2))
                    for k in range(FB):
                        act.wait_ge(S["up"], at(c * FB + k + 1))
                        act.activation(ff_r[:, g, k, :], bank[:, k, :], ACT.Relu,
                                       bias=b1_tok[:, k:k + 1]).then_inc(S["act"], 1)

        def ffn_dve(v, S, l):
            with v.Fori(0, NCH // 2) as i:
                for g in range(2):
                    v.wait_ge(S["down"], at(l * NCH + 2 * i + g + 1))
                    x = xT[:, bass.ds((2 * i + g) * CH, CH)]
                    v.scalar_tensor_tensor(out=x, in0=bank[:, 4 + g, :], scalar=vec_tok[:, 5:6], in1=x,
                                           op0=ALU.add, op1=ALU.add).then_inc(S["x"], 1)

        NT_ = N // P
        take = area()
        ga_buf = [take([NT_ * E1]) for _ in range(6)]
        ga_m = [take([NT_]) for _ in range(4)]
        ga_out = take([4, P])
        GA_NAMES = ["mm", "chain", "shift", "exp", "gates", "rows", "copied"]
        GA_DMA = ["out"]

        def gate_views(E):
            return [x[:, 0:NT_ * E].rearrange("p (t e) -> p t e", e=E) for x in ga_buf]

        def gate_pe(pe, S, E, wr):
            for t in range(NT_):
                last = pe.matmul(bank[:, 0, t * E:(t + 1) * E], hT[:, t * P:(t + 1) * P], wr, start=True, stop=True)
            last.then_inc(S["mm"], 1)
            pe.wait_ge(S["gates"], at(1))
            for x in range(NT_ * E // P):
                last = pe.transpose(bank[:, 4, x * P:(x + 1) * P], ga_buf[5][:, x * P:(x + 1) * P], ident[:, :])
            last.then_inc(S["rows"], 1)

        def gate_act(act, S, E):
            key = gate_views(E)[1]
            act.wait_ge(S["shift"], at(1))
            act.activation(key, key, ACT.Exp).then_inc(S["exp"], 1)

        def gate_dve(v, S, E, bias=None):
            lt, key, order, first, second, w = gate_views(E)
            count = [0]

            def link(ins):
                ins.then_inc(S["chain"], 1)
                count[0] += 1
                v.wait_ge(S["chain"], at(count[0]))

            def wide(x):
                return x.unsqueeze(2).broadcast_to([P, NT_, E])

            def pick(one, source, top):
                link(v.tensor_reduce(top, source, AX_X, ALU.max))
                link(v.tensor_tensor(key, source, wide(top), ALU.is_equal))
                link(v.tensor_tensor(key, key, order, ALU.mult))
                link(v.tensor_reduce(ga_m[2], key, AX_X, ALU.max))
                link(v.tensor_tensor(one, order, wide(ga_m[2]), ALU.is_equal))

            for e in range(E):
                link(v.memset(order[:, :, e:e + 1], float(E - e)))
            v.wait_ge(S["mm"], at(1))
            logits = bank[:, 0, 0:NT_ * E].rearrange("p (t e) -> p t e", e=E)
            if bias is None:
                link(v.tensor_copy(lt, logits))
            else:
                link(v.tensor_tensor(lt, logits, bias.unsqueeze(1).broadcast_to([P, NT_, E]), ALU.add))
            pick(first, lt, ga_m[0])
            link(v.tensor_scalar(w, first, -1.0, 1.0, ALU.mult, ALU.add))
            link(v.tensor_tensor(w, w, lt, ALU.mult))
            link(v.scalar_tensor_tensor(out=w, in0=first, scalar=-BIG, in1=w, op0=ALU.mult, op1=ALU.add))
            pick(second, w, ga_m[1])
            link(v.tensor_tensor(w, first, second, ALU.add))
            link(v.tensor_tensor(key, lt, wide(ga_m[0]), ALU.subtract))
            v.sem_inc(S["shift"], 1)
            v.wait_ge(S["exp"], at(1))
            link(v.tensor_tensor(key, key, w, ALU.mult))
            link(v.tensor_reduce(ga_m[2], key, AX_X, ALU.add))
            link(v.reciprocal(ga_m[3], ga_m[2]))
            v.tensor_tensor(w, key, wide(ga_m[3]), ALU.mult).then_inc(S["gates"], 1)
            v.wait_ge(S["rows"], at(1))
            n = NT_ * E // P
            v.tensor_copy(ga_out[:, 0:n, :], bank[:, 4, 0:n * P].rearrange("p (a b) -> p a b", a=n)
                          ).then_inc(S["copied"], 1)

        def gate_sp(sp, S, E, scr):
            sp.wait_ge(S["copied"], at(1))
            sp.dma_start(scr.rearrange("t e p -> (t e) p").rearrange("(x r) p -> r x p", r=P),
                         ga_out[:, 0:NT_ * E // P, :]).then_inc(S["out"], 16)
            sp.wait_ge(S["out"], at(1, 16))

        SPLIT = sems("split", ["w_high", "w_low", "h_in", "h_high", "h_low"], ["raw"])
        take = area()
        take([5 * 1024])
        raw_w = take([E0 * FF])
        W_PIECES = 4

        def split_sizes(which):
            return (E0 * FF, 2 * (E1 + 1) * I1)[which]

        def w_part(which, x):
            n = split_sizes(which)
            return r_work[:, x * n:(x + 1) * n]

        def h_part(p, x):
            return r_work[:, 8192 + (2 * p + x) * CH:8192 + (2 * p + x + 1) * CH]

        def weights_split(pool, which):
            n = split_sizes(which) // W_PIECES
            high, low = w_part(which, 0), w_part(which, 1)
            pool.wait_ge(SPLIT["raw"], at(1 if which == 0 else 3, 16))
            for x in range(W_PIECES):
                c = slice(x * n, (x + 1) * n)
                pool.tensor_scalar(high[:, c], raw_w[:, c], 1.0, None, ALU.mult).then_inc(SPLIT["w_high"], 1)
            for x in range(W_PIECES):
                c = slice(x * n, (x + 1) * n)
                pool.wait_ge(SPLIT["w_high"], at(which * W_PIECES + x + 1))
                pool.tensor_tensor(low[:, c], raw_w[:, c], high[:, c], ALU.subtract).then_inc(SPLIT["w_low"], 1)

        def input_split(pool, which, i, p, step=None):
            c = 2 * i + p
            h = h_chunk[:, :]
            if step in (None, 0):
                pool.wait_ge(SPLIT["h_low"], at(which * NCH + c))
                settled(pool)
                pool.tensor_copy(h, hT[:, bass.ds(c * CH, CH)]).then_inc(SPLIT["h_in"], 1)
            if step in (None, 1):
                pool.wait_ge(SPLIT["h_in"], at(which * NCH + c + 1))
                settled(pool)
                pool.tensor_scalar(h_part(p, 0), h, 1.0, None, ALU.mult).then_inc(SPLIT["h_high"], 1)
            if step in (None, 2):
                pool.wait_ge(SPLIT["h_high"], at(which * NCH + c + 1))
                pool.tensor_tensor(h_part(p, 1), h, h_part(p, 0), ALU.subtract).then_inc(SPLIT["h_low"], 1)

        def split_product(pe, out, high, low, p):
            pe.matmul(out, high, h_part(p, 0), start=True, stop=False)
            pe.matmul(out, high, h_part(p, 1), start=False, stop=False)
            return pe.matmul(out, low, h_part(p, 0), start=False, stop=True)

        def chunk_pairs(eng, body, start=0):
            with eng.Fori(start, NCH // 2 - 1) as i:
                for p in range(2):
                    body(i, p, 2)
            for p in range(2):
                body(NCH // 2 - 1, p, 1 - p)

        take = area()
        mo_r = take([2, FB, CH])
        mo_g = take([4, CH])
        mo_t = take([2, CH])
        MO_NAMES = ["up", "act", "down", "t", "x"]
        MO_DMA = ["g0", "g1", "g2", "g3"]

        def moe_sp(sp, S):
            with sp.Fori(0, NCH) as c:
                for e in range(E0):
                    sp.wait_ge(S["t"], at(c * E0 + e + 1 - 4))
                    sp.dma_start(mo_g[:, e % 4, :].rearrange("p (t q) -> p t q", t=4),
                                 g0_scr[bass.ds(c * 4, 4), e, :].partition_broadcast(P)
                                 ).then_inc([S["g0"], S["g1"], S["g2"], S["g3"]][e % 4], 16)

        def moe_pool(pool):
            def body(i, p, left):
                if left == 2:
                    pool.wait_ge(MO["up"], at((2 * i + p + 1) * E0 * FB))
                    settled(pool)
                    input_split(pool, 0, i + 1, p)

            input_split(pool, 0, 0, 0)
            input_split(pool, 0, 0, 1)
            chunk_pairs(pool, body)

        def moe_pe(pe, S):
            def up(i, p, e):
                c = 2 * i + p
                if e == 0:
                    pe.wait_ge(SPLIT["h_low"], at(c + 1))
                for k in range(FB):
                    pe.wait_ge(S["act"], at((c * E0 + e) * FB + k + 1 - 4))
                    w = slice(e * FF + k * P, e * FF + (k + 1) * P)
                    split_product(pe, bank[:, k, :], w_part(0, 0)[:, w], w_part(0, 1)[:, w], p).then_inc(S["up"], 1)

            def down(c, e):
                n = c * E0 + e
                pe.wait_ge(S["t"], at(n + 1 - 2))
                for k in range(FB):
                    pe.wait_ge(S["act"], at(n * FB + k + 1))
                    last = pe.matmul(bank[:, 4 + e % 2, :], w_e2[:, e, k, :], mo_r[:, e % 2, k, :],
                                     start=(k == 0), stop=(k == FB - 1))
                last.then_inc(S["down"], 1)

            def body(i, p, left):
                for e in range(E0):
                    if e < E0 - 1:
                        up(i, p, e + 1)
                    elif left:
                        up(i + p, 1 - p, 0)
                    down(2 * i + p, e)

            up(0, 0, 0)
            chunk_pairs(pe, body)

        def moe_act(act, S):
            settled(act)
            act.preload_act_table(ACT.Gelu)
            with act.Fori(0, NCH) as c:
                for e in range(E0):
                    n = c * E0 + e
                    act.wait_ge(S["down"], at(n + 1 - 2))
                    for k in range(FB):
                        act.wait_ge(S["up"], at(n * FB + k + 1))
                        act.activation(mo_r[:, e % 2, k, :], bank[:, k, :], ACT.Gelu).then_inc(S["act"], 1)

        def moe_dve(v, S):
            with v.Fori(0, NCH) as c:
                for e in range(E0):
                    n = c * E0 + e
                    v.wait_ge(S["down"], at(n + 1))
                    v.wait_ge([S["g0"], S["g1"], S["g2"], S["g3"]][e % 4], at(c * 2 + e // 4 + 1, 16))
                    v.wait_ge(S["x"], at(n + 1 - 2))
                    v.tensor_tensor(mo_t[:, e % 2, :], bank[:, 4 + e % 2, :], mo_g[:, e % 4, :],
                                    ALU.mult).then_inc(S["t"], 1)
                    v.wait_ge(S["t"], at(n + 1))
                    x = xT[:, bass.ds(c * CH, CH)]
                    v.tensor_tensor(x, x, mo_t[:, e % 2, :], ALU.add).then_inc(S["x"], 1)

        E2 = E1 + 1
        ROWS = E2 * I1
        KB = -(-ROWS // P)
        GB = E1 * I1 // P
        take = area()
        sw_w2 = take([KB, P])
        sw_p = take([7, KB])
        sw_c = take([2, KB])
        sw_n = take([2, KB])
        sw_eb = take([P])
        sw_cw = take([CH])
        sw_g = take([4, CH])
        sw_gt = take([3, CH])
        sw_gg = take([5, CH])
        sw_sg = take([3, CH])
        sw_ut = take([3, CH])
        sw_u = take([5, CH])
        sw_t = take([2, CH])
        sw_o = take([3, CH])
        SW_NAMES = ["prep", "ones", "hg", "hu", "gt", "ut", "gg", "clip", "u", "sg", "t", "o", "down", "x"]
        SW_DMA = ["w", "g0", "g1", "g2", "g3", "cw"]

        def rows(k):
            return min(P, ROWS - k * P)

        def over(c, k, r):
            if k >= r:
                return at(c * KB + k + 1 - r)
            last = max(x for x in range(KB) if x % r == k)
            return at(c * KB + last + 1 - KB)

        def slot(k, r):
            return k % r if k < GB else r

        def over_slot(c, k, r):
            if k >= GB:
                return at(c * KB)
            if k >= r:
                return at(c * KB + k + 1 - r)
            last = max(x for x in range(GB) if x % r == k)
            return at(c * KB + last + 1 - KB)

        def segments(k):
            out, r = [], k * P
            while r < (k + 1) * P:
                end = min((k + 1) * P, (r // I1 + 1) * I1)
                out.append((r - k * P, end - r, r // I1))
                r = end
            return out

        def swi_sp(sp, S):
            for dst, src in ((sw_w2, A["sw2"]), (sw_p, A["sact"]),
                             (sw_eb[0:E2], A["sb2"])):
                sp.dma_start(dst, src).then_inc(S["w"], 16)
            sp.wait_ge(S["ones"], at(1))
            with sp.Fori(0, NCH) as c:
                for k in range(GB):
                    if k == 4:
                        sp.wait_ge(S["down"], at(c * KB))
                        sp.dma_start(sw_cw[0:E1, :].rearrange("e (t q) -> e t q", t=4),
                                     g1_scr[bass.ds(c * 4, 4), :, :].rearrange("t e q -> e t q")
                                     ).then_inc(S["cw"], 16)
                    sp.wait_ge(S["u"], at(c * GB + k + 1 - 4))
                    for r, n, e in segments(k):
                        sp.dma_start(sw_g[r:r + n, k % 4, :].rearrange("p (t q) -> p t q", t=4),
                                     g1_scr[bass.ds(c * 4, 4), e, :].partition_broadcast(n)
                                     ).then_inc([S["g0"], S["g1"], S["g2"], S["g3"]][k % 4], 16)

        def swi_pool(pool, S):
            pool.memset(sw_cw[0:E2, :], 1.0).then_inc(S["ones"], 1)

            def body(i, p, left):
                c = 2 * i + p
                for k in range(GB):
                    pool.wait_ge(S["clip"], at(c * KB + k + 1))
                    pool.wait_ge([S["g0"], S["g1"], S["g2"], S["g3"]][k % 4],
                                 at(2 * (c * (GB // 4) + k // 4 + 1), 16))
                    pool.tensor_tensor(sw_u[:, k % 4, :], sw_u[:, k % 4, :], sw_g[:, k % 4, :],
                                       ALU.mult).then_inc(S["u"], 1)
                    if left and k in (3, 5, 7):
                        pool.wait_ge(S["hu"], at(c * KB))
                        settled(pool)
                        input_split(pool, 1, i + p, 1 - p, (k - 3) // 2)

            input_split(pool, 1, 0, 0)
            chunk_pairs(pool, body)

        def swi_pe(pe, S):
            def hidden(i, p, k):
                m, c = rows(k), 2 * i + p
                if k == 0:
                    pe.wait_ge(SPLIT["h_low"], at(NCH + c + 1))
                for x, (done, read) in enumerate(((S["hg"], S["gt"]), (S["hu"], S["ut"]))):
                    w = slice(x * ROWS + k * P, x * ROWS + k * P + m)
                    pe.wait_ge(read, over(c, k, 3))
                    split_product(pe, bank[0:m, 3 * x + k % 3, :], w_part(1, 0)[:, w], w_part(1, 1)[:, w], p
                                  ).then_inc(done, 1)

            def down(c, p, k):
                if k == 0:
                    pe.wait_ge(S["x"], at(c + 1 - 2))
                if k == KB - 1:
                    pe.wait_ge(S["cw"], at(c + 1, 16))
                    pe.matmul(bank[:, 6 + p, :], sw_eb[0:E2, :], sw_cw[0:E2, :], start=False, stop=False)
                pe.wait_ge(S["o"], at(c * KB + k + 1))
                pe.matmul(bank[:, 6 + p, :], sw_w2[0:rows(k), k, :], sw_o[0:rows(k), k % 3, :],
                          start=(k == 0), stop=(k == KB - 1)).then_inc(S["down"], 1)

            def body(i, p, left):
                for k in range(KB):
                    if k + 3 < KB:
                        hidden(i, p, k + 3)
                    elif left:
                        hidden(i + p, 1 - p, k + 3 - KB)
                    down(2 * i + p, p, k)

            pe.wait_ge(S["w"], at(3, 16))
            for k in range(3):
                hidden(0, 0, k)
            chunk_pairs(pe, body)

        def swi_act(act, S):
            act.wait_ge(S["prep"], at(1))
            act.activation(sw_c, sw_c, ACT.Exp, scale=-1.0).then_inc(S["prep"], 1)
            act.wait_ge(S["prep"], at(2))
            act.activation(sw_c, sw_c, ACT.Ln, bias=one_t[:, 0:1]).then_inc(S["prep"], 1)
            act.preload_act_table(ACT.Sigmoid)

            def move(c, k):
                for x, (ready, done, read, dst) in enumerate(((S["hg"], S["gt"], S["gg"], sw_gt),
                                                              (S["hu"], S["ut"], S["clip"], sw_ut))):
                    m = rows(k)
                    act.wait_ge(ready, at(c * KB + k + 1))
                    act.wait_ge(read, over(c, k, 3))
                    act.activation(dst[0:m, k % 3, :], bank[0:m, 3 * x + k % 3, :], ACT.Identity,
                                   bias=sw_p[0:m, x, k:k + 1]).then_inc(done, 1)

            def chunk(c, more):
                for k in range(KB):
                    if k + 2 < KB:
                        move(c, k + 2)
                    elif more:
                        move(c + 1, k + 2 - KB)
                    m = rows(k)
                    act.wait_ge(S["gg"], at(c * KB + k + 1))
                    act.wait_ge(S["t"], over_slot(c, k, 2))
                    act.activation(sw_sg[0:m, slot(k, 2), :], sw_gg[0:m, slot(k, 4), :], ACT.Sigmoid,
                                   scale=sw_p[0:m, 2, k:k + 1]).then_inc(S["sg"], 1)

            act.wait_ge(S["prep"], at(8))
            move(0, 0)
            move(0, 1)
            with act.Fori(0, NCH - 1) as c:
                chunk(c, True)
            chunk(NCH - 1, False)

        def swi_dve(v, S):
            raw = sw_p[:, 5:7, :]
            v.wait_ge(S["w"], at(3, 16))
            v.scalar_tensor_tensor(out=sw_c, in0=raw, scalar=-1.0, in1=raw, op0=ALU.mult,
                                   op1=ALU.max).then_inc(S["prep"], 1)
            v.wait_ge(S["prep"], at(3))
            v.scalar_tensor_tensor(out=sw_c, in0=raw, scalar=0.0, in1=sw_c, op0=ALU.max,
                                   op1=ALU.add).then_inc(S["prep"], 1)
            v.wait_ge(S["prep"], at(4))
            v.tensor_scalar(sw_n, sw_c, -1.0, None, ALU.mult).then_inc(S["prep"], 1)
            for x, part in enumerate((sw_n[:, 1, :], sw_c[:, 1, :], sw_p[:, 1, :])):
                v.wait_ge(S["prep"], at(5 + x))
                v.tensor_tensor(part, part, sw_p[:, 4, :], ALU.add).then_inc(S["prep"], 1)
            v.wait_ge(S["prep"], at(8))

            def clip(c, k):
                n, m = c * KB + k, rows(k)
                v.wait_ge(S["gt"], at(n + 1))
                v.wait_ge(S["t"], over_slot(c, k, 4))
                v.tensor_scalar(sw_gg[0:m, slot(k, 4), :], sw_gt[0:m, k % 3, :], sw_c[0:m, 0, k:k + 1],
                                sw_n[0:m, 0, k:k + 1], ALU.min, ALU.max).then_inc(S["gg"], 1)
                v.wait_ge(S["ut"], at(n + 1))
                v.wait_ge(S["o"], over_slot(c, k, 4))
                v.tensor_scalar(sw_u[0:m, slot(k, 4), :], sw_ut[0:m, k % 3, :], sw_c[0:m, 1, k:k + 1],
                                sw_n[0:m, 1, k:k + 1], ALU.min, ALU.max).then_inc(S["clip"], 1)

            def product(c, p, k):
                n, m = c * KB + k, rows(k)
                v.wait_ge(S["sg"], at(n + 1))
                v.scalar_tensor_tensor(out=sw_t[0:m, (p + k) % 2, :], in0=sw_sg[0:m, slot(k, 2), :],
                                       scalar=sw_p[0:m, 3, k:k + 1], in1=sw_gg[0:m, slot(k, 4), :],
                                       op0=ALU.mult, op1=ALU.mult).then_inc(S["t"], 1)
                v.wait_ge(S["t"], at(n + 1))
                if k < GB:
                    v.wait_ge(S["u"], at(c * GB + k + 1))
                v.wait_ge(S["down"], over(c, k, 3))
                v.tensor_tensor(sw_o[0:m, k % 3, :], sw_t[0:m, (p + k) % 2, :], sw_u[0:m, slot(k, 4), :],
                                ALU.mult).then_inc(S["o"], 1)

            def add(c, p):
                v.wait_ge(S["down"], at((c + 1) * KB))
                x = xT[:, bass.ds(c * CH, CH)]
                v.tensor_tensor(x, x, bank[:, 6 + p, :], ALU.add).then_inc(S["x"], 1)

            def body(i, p, left, first=False):
                c = 2 * i + p
                for k in range(KB):
                    if k + 2 < KB:
                        clip(c, k + 2)
                    elif left:
                        clip(c + 1, k + 2 - KB)
                    product(c, p, k)
                    if k == 1 and not (first and p == 0):
                        add(c - 1, 1 - p)

            clip(0, 0)
            clip(0, 1)
            body(0, 0, 2, first=True)
            body(0, 1, 2, first=True)
            chunk_pairs(v, body, start=1)
            add(NCH - 1, 1)

        take = area()
        fi_o = take([NCH, CH])
        FI = sems("fi", ["turned", "by_act", "by_dve"], ["out"])

        def fin_pe(pe):
            for c in range(NCH):
                for t in range(4):
                    last = pe.transpose(bank[:, c, t * P:(t + 1) * P], xT[:, c * CH + t * P:c * CH + (t + 1) * P],
                                        ident[:, :])
                last.then_inc(FI["turned"], 1)

        def fin_act(act):
            for c in range(0, NCH, 2):
                act.wait_ge(FI["turned"], at(c + 1))
                act.activation(fi_o[:, c, :], bank[:, c, :], ACT.Copy).then_inc(FI["by_act"], 1)

        def fin_dve(v):
            for c in range(1, NCH, 2):
                v.wait_ge(FI["turned"], at(c + 1))
                v.tensor_copy(fi_o[:, c, :], bank[:, c, :]).then_inc(FI["by_dve"], 1)

        def fin_sp(sp):
            for c in range(NCH):
                sp.wait_ge(FI["by_act"] if c % 2 == 0 else FI["by_dve"], at(c // 2 + 1))
                sp.dma_start(A["out"][c * CH:(c + 1) * CH, :].rearrange("(t q) d -> q t d", q=P),
                             fi_o[:, c, :].rearrange("p (t d) -> p t d", t=4)).then_inc(FI["out"], 16)
            sp.wait_ge(FI["out"], at(NCH, 16))

        win, full, causal = (GEO[m] for m in ("window", "full", "causal"))
        LN = sems("ln", LN_NAMES)
        QKV = sems("qkv", QK_NAMES, QK_DMA)
        AT = sems("attn", AT_NAMES, AT_DMA)
        OU = sems("out", OU_NAMES, OU_DMA)
        FT = sems("ffn_tok", FF_NAMES)
        G0, G1 = (sems(x, GA_NAMES, GA_DMA) for x in ("gate0", "gate1"))
        MO = sems("moe", MO_NAMES, MO_DMA)
        SW = sems("swi", SW_NAMES, SW_DMA)
        RE = sems("res", ["x"])
        v_flat = v_scr.rearrange("b h p x -> (b h) p x")
        N_W = 11
        ln_at = lambda k: NCH * k

        def vt(i):
            return vec_tok[:, i:i + 1]

        def va(i):
            return vec_a0[:, i:i + 1]

        def started(eng, k):
            for s, step in credited[k::5]:
                eng.sem_inc(s, CREDIT * step)
            eng.sem_inc(s_credit, 1)
            eng.wait_ge(s_credit, 5)

        block = ctx.enter_context(nc.Block())

        @block.sync
        def _(sp):
            started(sp, 1)
            em_sp(sp)
            for dst, src in ((w_a0, A["a0_w"]), (vec_a0, A["a0_v"]), (bv_a0, A["a0_bv"]), (w_a1, A["a1_w"]),
                             (wr0, A["wr0"]), (wr1, A["wr1"]), (br1, A["br1"].broadcast_to([P, E1]))):
                sp.dma_start(dst[:], src).then_inc(s_w, 16)
            em_sp_mask(sp)
            phase_end(sp, "em")
            with sp.Fori(0, LAYERS) as l:
                for dst, src in ((w_tok, A["tok_w"]), (w_tok1, A["tok_w1"]), (w_tok2, A["tok_w2"]),
                                 (vec_tok, A["tok_v"]), (b1_tok, A["tok_b1"])):
                    shape = "o p a b -> (o p) a b" if len(dst.shape) == 3 else "o p a -> (o p) a"
                    s = src[bass.ds(l, 1)]
                    sp.dma_start(dst[:], s.rearrange(shape)).then_inc(s_wl, 16)
                phase_end(sp, "ln1", l)
                qkv_sp(sp, QKV, l, win)
                phase_end(sp, "qkv", l)
                attn_sp(sp, AT, l, win)
                phase_end(sp, "attn", l)
                out_sp(sp, OU, l, parts=False)
                phase_end(sp, "out", l)
                phase_end(sp, "ln2", l)
                phase_end(sp, "ffn", l)
            phase_end(sp, "ln3")
            phase_end(sp, "res")
            phase_end(sp, "ln4")
            qkv_sp(sp, QKV, 0, full)
            phase_end(sp, "qkv0")
            sp.dma_start(w_e2[:], A["e2"]).then_inc(s_w, 16)
            attn_sp(sp, AT, 0, full)
            phase_end(sp, "attn0")
            out_sp(sp, OU, LAYERS)
            phase_end(sp, "out0")
            phase_end(sp, "ln5")
            sp.dma_start(raw_w, A["e1"].rearrange("p e f -> p (e f)")).then_inc(SPLIT["raw"], 16)
            gate_sp(sp, G0, E0, g0_scr)
            phase_end(sp, "gate0")
            moe_sp(sp, MO)
            phase_end(sp, "moe")
            phase_end(sp, "ln6")
            qkv_sp(sp, QKV, 0, causal)
            phase_end(sp, "qkv1")
            attn_sp(sp, AT, 0, causal)
            phase_end(sp, "attn1")
            out_sp(sp, OU, LAYERS + 1, scramble=True)
            phase_end(sp, "out1")
            phase_end(sp, "ln7")
            for x, src in enumerate((A["sw1g"], A["sw1u"])):
                sp.dma_start(raw_w[:, x * ROWS:(x + 1) * ROWS], src).then_inc(SPLIT["raw"], 16)
            gate_sp(sp, G1, E1, g1_scr)
            phase_end(sp, "gate1")
            swi_sp(sp, SW)
            phase_end(sp, "swi")
            fin_sp(sp)

        @block.gpsimd
        def _(pool):
            started(pool, 0)
            pool.memset(mask_f[:, :, 0:WIN], 0.0)
            pool.memset(mask_f[:, :, WIN + T:], 0.0)
            pool.memset(ident[:, :], 0.0)
            pool.memset(identb[:, :], 0.0)
            pool.memset(mean_w[:, :], 1.0 / P)
            pool.memset(eps_t[:, :], EPS)
            pool.memset(one_t[:, :], 1.0)
            pool.memset(ones_row[:, :], 1.0)
            pool.memset(band_q[:, :, :], 0.0)
            pool.memset(band_k[:, :, :], 0.0)
            pool.memset(causal_q[:, :], 0.0)
            pool.memset(causal_k[:, :], 0.0).then_inc(s_const, 1)
            pool.wait_ge(s_const, 1)
            def keep(m, pattern, base, mult):
                return pool.affine_select(out=m, in_=m, compare_op=ALU.is_ge, fill=OUTSIDE, base=base,
                                          pattern=pattern, channel_multiplier=mult)

            qt = P - 2 * WIN
            order = [0]

            def link(ins):
                ins.then_inc(s_pool, 1)
                order[0] += 1
                pool.wait_ge(s_pool, order[0])

            link(pool.affine_select(out=ident[:, :], in_=ident[:, :], compare_op=ALU.not_equal, fill=1.0,
                                    base=0, pattern=[[-1, P]], channel_multiplier=1))
            link(pool.affine_select(out=identb[:, :], in_=identb[:, :], compare_op=ALU.not_equal, fill=1.0,
                                    base=0, pattern=[[-1, P]], channel_multiplier=1))
            pool.sem_inc(s_const, 1)
            em_pool(pool)
            for j in range(SLOTS):
                for x in (2, 3):
                    pool.tensor_scalar(vr_all[:, j, :, x * HD:(x + 1) * HD],
                                       mean_w[:, :].rearrange("p (t d) -> p t d", d=HD), 0.0, float(x - 2),
                                       ALU.mult, ALU.add)

            link(keep(band_q[:, :, :], [[0, 4], [1, P]], 0, -1))
            link(keep(band_q[:, :, :], [[0, 4], [-1, P]], 2 * WIN, 1))
            link(keep(band_k[:, :, :], [[0, 4], [-1, qt]], 0, 1))
            link(keep(band_k[:, :, :], [[0, 4], [1, qt]], 2 * WIN, -1))
            link(keep(causal_q[:, :], [[-1, P]], 0, 1))
            link(keep(causal_k[:, :], [[1, P]], 0, -1))
            phase_end(pool, "em")
            with pool.Fori(0, LAYERS) as l:
                ln_pool(pool, LN, l * (2 * NCH))
                phase_end(pool, "ln1", l)
                qkv_pool(pool, QKV, l, win)
                phase_end(pool, "qkv", l)
                attn_pool(pool, AT, l, win)
                phase_end(pool, "attn", l)
                out_pool(pool, OU, l, parts=False)
                phase_end(pool, "out", l)
                ln_pool(pool, LN, l * (2 * NCH) + NCH)
                phase_end(pool, "ln2", l)
                phase_end(pool, "ffn", l)
            ln_pool(pool, LN, ln_at(4))
            phase_end(pool, "ln3")
            phase_end(pool, "res")
            ln_pool(pool, LN, ln_at(5))
            phase_end(pool, "ln4")
            qkv_pool(pool, QKV, 0, full)
            phase_end(pool, "qkv0")
            attn_pool(pool, AT, 0, full)
            phase_end(pool, "attn0")
            out_pool(pool, OU, LAYERS)
            phase_end(pool, "out0")
            ln_pool(pool, LN, ln_at(6))
            phase_end(pool, "ln5")
            weights_split(pool, 0)
            phase_end(pool, "gate0")
            moe_pool(pool)
            phase_end(pool, "moe")
            ln_pool(pool, LN, ln_at(7))
            phase_end(pool, "ln6")
            qkv_pool(pool, QKV, 0, causal)
            phase_end(pool, "qkv1")
            attn_pool(pool, AT, 0, causal)
            phase_end(pool, "attn1")
            out_pool(pool, OU, LAYERS + 1)
            phase_end(pool, "out1")
            ln_pool(pool, LN, ln_at(8))
            phase_end(pool, "ln7")
            weights_split(pool, 1)
            phase_end(pool, "gate1")
            swi_pool(pool, SW)
            phase_end(pool, "swi")

        @block.tensor
        def _(pe):
            started(pe, 2)
            pe.wait_ge(s_const, 2)
            em_pe(pe)
            phase_end(pe, "em")
            with pe.Fori(0, LAYERS) as l:
                ln_pe(pe, LN, l * (2 * NCH), xT)
                phase_end(pe, "ln1", l)
                qkv_pe(pe, QKV, l, win, w_tok[:, 0, :], w_tok[:, 1, :], w_tok[:, 2, :])
                phase_end(pe, "qkv", l)
                attn_pe(pe, AT, l, win)
                phase_end(pe, "attn", l)
                out_pe(pe, OU, l, w_tok[:, 3, :])
                phase_end(pe, "out", l)
                ln_pe(pe, LN, l * (2 * NCH) + NCH, xT)
                phase_end(pe, "ln2", l)
                ffn_pe(pe, FT, l)
                phase_end(pe, "ffn", l)
            pe.wait_ge(s_w, 16 * 7)
            ln_pe(pe, LN, ln_at(4), xT)
            phase_end(pe, "ln3")
            phase_end(pe, "res")
            ln_pe(pe, LN, ln_at(5), hT)
            phase_end(pe, "ln4")
            qkv_pe(pe, QKV, 0, full, w_a0[:, 0, :], w_a0[:, 1, :], w_a0[:, 2, :], bv=bv_a0[:, :])
            phase_end(pe, "qkv0")
            attn_pe(pe, AT, 0, full)
            phase_end(pe, "attn0")
            out_pe(pe, OU, LAYERS, w_a0[:, 3, :])
            phase_end(pe, "out0")
            ln_pe(pe, LN, ln_at(6), xT)
            phase_end(pe, "ln5")
            gate_pe(pe, G0, E0, wr0[:, :])
            phase_end(pe, "gate0")
            pe.wait_ge(s_w, 16 * 8)
            moe_pe(pe, MO)
            phase_end(pe, "moe")
            ln_pe(pe, LN, ln_at(7), xT)
            phase_end(pe, "ln6")
            qkv_pe(pe, QKV, 0, causal, w_a1[:, 0, :], w_a1[:, 2, :], w_a1[:, 4, :],
                   wq2=w_a1[:, 1, :], wk2=w_a1[:, 3, :])
            phase_end(pe, "qkv1")
            attn_pe(pe, AT, 0, causal)
            phase_end(pe, "attn1")
            phase_end(pe, "out1")
            ln_pe(pe, LN, ln_at(8), xT)
            phase_end(pe, "ln7")
            gate_pe(pe, G1, E1, wr1[:, :])
            phase_end(pe, "gate1")
            swi_pe(pe, SW)
            phase_end(pe, "swi")
            fin_pe(pe)

        @block.vector
        def _(v):
            started(v, 3)
            em_dve(v)
            phase_end(v, "em")
            with v.Fori(0, LAYERS) as l:
                ln_dve(v, LN, l * (2 * NCH), xT, gained=True)
                phase_end(v, "ln1", l)
                qkv_dve(v, QKV, l, win)
                phase_end(v, "qkv", l)
                attn_dve(v, AT, l, win)
                phase_end(v, "attn", l)
                out_dve(v, OU, l, vt(4), parts=False)
                phase_end(v, "out", l)
                ln_dve(v, LN, l * (2 * NCH) + NCH, xT, gained=True)
                phase_end(v, "ln2", l)
                ffn_dve(v, FT, l)
                phase_end(v, "ffn", l)
            v.wait_ge(s_w, 16 * 7)
            ln_dve(v, LN, ln_at(4), xT)
            phase_end(v, "ln3")
            with v.Fori(0, NCH) as c:
                x = xT[:, bass.ds(c * CH, CH)]
                v.tensor_tensor(x, x, hT[:, bass.ds(c * CH, CH)], ALU.add).then_inc(RE["x"], 1)
            v.wait_ge(RE["x"], at(NCH))
            phase_end(v, "res")
            ln_dve(v, LN, ln_at(5), hT, gained=True)
            phase_end(v, "ln4")
            qkv_dve(v, QKV, 0, full)
            phase_end(v, "qkv0")
            attn_dve(v, AT, 0, full)
            phase_end(v, "attn0")
            out_dve(v, OU, LAYERS, va(4))
            phase_end(v, "out0")
            ln_dve(v, LN, ln_at(6), xT)
            phase_end(v, "ln5")
            gate_dve(v, G0, E0)
            phase_end(v, "gate0")
            moe_dve(v, MO)
            phase_end(v, "moe")
            ln_dve(v, LN, ln_at(7), xT)
            phase_end(v, "ln6")
            qkv_dve(v, QKV, 0, causal)
            phase_end(v, "qkv1")
            attn_dve(v, AT, 0, causal)
            phase_end(v, "attn1")
            out_dve(v, OU, LAYERS + 1, None, project=False)
            phase_end(v, "out1")
            ln_dve(v, LN, ln_at(8), xT)
            phase_end(v, "ln7")
            gate_dve(v, G1, E1, bias=br1[:, :])
            phase_end(v, "gate1")
            swi_dve(v, SW)
            phase_end(v, "swi")
            fin_dve(v)

        @block.scalar
        def _(act):
            started(act, 4)
            em_act(act)
            phase_end(act, "em")
            with act.Fori(0, LAYERS) as l:
                act.wait_ge(s_wl, (l + 1) * 5 * 16)
                ln_act(act, LN, l * (2 * NCH), (vt(0), vt(1)), weights=(l + 1) * 5 * 16)
                phase_end(act, "ln1", l)
                qkv_act(act, QKV, l, win)
                phase_end(act, "qkv", l)
                attn_act(act, AT, l, win)
                phase_end(act, "attn", l)
                out_act(act, OU, l, parts=False)
                phase_end(act, "out", l)
                ln_act(act, LN, l * (2 * NCH) + NCH, (vt(2), vt(3)))
                phase_end(act, "ln2", l)
                ffn_act(act, FT, l)
                phase_end(act, "ffn", l)
            act.wait_ge(s_w, 16 * 7)
            ln_act(act, LN, ln_at(4), None)
            phase_end(act, "ln3")
            phase_end(act, "res")
            ln_act(act, LN, ln_at(5), (va(0), va(1)))
            phase_end(act, "ln4")
            qkv_act(act, QKV, 0, full, bq=va(2), bk=va(3))
            phase_end(act, "qkv0")
            attn_act(act, AT, 0, full)
            phase_end(act, "attn0")
            out_act(act, OU, LAYERS)
            phase_end(act, "out0")
            ln_act(act, LN, ln_at(6), None)
            phase_end(act, "ln5")
            gate_act(act, G0, E0)
            phase_end(act, "gate0")
            moe_act(act, MO)
            phase_end(act, "moe")
            ln_act(act, LN, ln_at(7), None)
            phase_end(act, "ln6")
            qkv_act(act, QKV, 0, causal)
            phase_end(act, "qkv1")
            attn_act(act, AT, 0, causal)
            phase_end(act, "attn1")
            out_act(act, OU, LAYERS + 1)
            phase_end(act, "out1")
            ln_act(act, LN, ln_at(8), None)
            phase_end(act, "ln7")
            gate_act(act, G1, E1)
            phase_end(act, "gate1")
            swi_act(act, SW)
            phase_end(act, "swi")
            fin_act(act)


def rope_tables():
    t = np.arange(T, dtype=np.float64)
    out = []
    for d in (P, P // 2):
        i = np.arange(d // 2, dtype=np.float64)
        theta = 10000.0 ** (-(2.0 * (i - 1.0))) / d
        ang = t[:, None] * theta[None, :]
        cos, sin = np.cos(ang).astype(np.float32), np.sin(ang).astype(np.float32)
        c = np.repeat(cos, 2, axis=1).T
        s = np.stack([sin, -sin], axis=-1).reshape(T, d).T
        out.append((c, s))
    return out


def kernel(**inputs):
    import concourse.bacc as _bacc
    from concourse import mybir as _mybir
    from concourse.bass_utils import run_bass_kernel_spmd as _run

    x = {k: np.asarray(v) for k, v in inputs.items()}

    def pack(*arrays):
        return np.ascontiguousarray(np.stack(arrays, axis=-1))

    def blocks(rows):
        short = -len(rows) % P
        rows = np.concatenate([rows, np.zeros((short, rows.shape[1]), rows.dtype)])
        return rows.reshape(-1, P, rows.shape[1]).transpose(1, 0, 2)

    def columns(w, order):
        return w[:, order]

    swap = np.arange(P) ^ 1
    twice = np.concatenate([np.arange(HD) + HD * (h // 2) for h in range(H)])
    twice_swap = np.concatenate([(np.arange(HD) ^ 1) + HD * (h // 2) for h in range(H)])
    t = "L0_tok_"
    a, f, g, m = "L0_attn_", "L0_ffn_", "L1_attn_", "L1_ffn_"
    (cq, sq), (ck, sk) = rope_tables()
    wx, bx = x[a + "w_xyz"], x[a + "b_xyz"]
    w1 = np.concatenate([x[m + "expert_w1"], x[m + "shared_w1"][None]])
    acts = np.concatenate([x[m + "expert_act"], x[m + "shared_act"][None]])
    b1 = np.concatenate([x[m + "expert_b1"], x[m + "shared_b1"][None]])
    w2 = np.concatenate([x[m + "expert_w2"], x[m + "shared_w2"][None]])
    arrays = {
        "x": x["x"], "mask": x["mask_BS_i1_0"], "tok": x[t + "tok_emb"], "pos": x[t + "pos_emb"],
        "tok_w": np.stack([x[t + "Wq"], x[t + "Wk"], x[t + "Wv"], x[t + "Wo"]], axis=2),
        "tok_w1": x[t + "W1"],
        "tok_w2": x[t + "W2"].reshape(LAYERS, FB, P, P).transpose(0, 2, 1, 3),
        "tok_v": pack(x[t + "ln1_g"], x[t + "ln1_b"], x[t + "ln2_g"], x[t + "ln2_b"], x[t + "bo"], x[t + "b2"]),
        "tok_b1": x[t + "b1"].reshape(LAYERS, FB, P).transpose(0, 2, 1),
        "a0_w": np.stack([wx[:, 0:P], wx[:, P:2 * P], wx[:, 2 * P:], x[a + "w_end"]], axis=1),
        "a0_v": pack(x[a + "gamma"], x[a + "beta"], bx[0:P], bx[P:2 * P], x[a + "b_end"]),
        "a0_bv": bx[None, 2 * P:],
        "a1_w": np.stack([x[g + "Wq"], columns(x[g + "Wq"], swap), columns(x[g + "Wk"], twice),
                          columns(x[g + "Wk"], twice_swap), columns(x[g + "Wv"], twice)], axis=1),
        "cos": np.stack([cq, ck[twice]]), "sin": np.stack([sq, sk[twice]]),
        "wr0": x[f + "Wr"].T, "wr1": x[m + "gate_w"], "br1": x[m + "gate_b"][None],
        "e1": x[f + "W1"].transpose(2, 0, 1),
        "e2": x[f + "W2"].reshape(E0, P, FB, P).transpose(3, 0, 2, 1),
        "sw1g": w1[..., 0::2].transpose(1, 0, 2).reshape(P, -1),
        "sw1u": w1[..., 1::2].transpose(1, 0, 2).reshape(P, -1),
        "sw2": blocks(w2.reshape(-1, P)),
        "sact": blocks(np.concatenate([b1[:, 0::2].reshape(-1, 1), b1[:, 1::2].reshape(-1, 1),
                                       np.repeat(acts, I1, axis=0)], axis=1)).transpose(0, 2, 1),
        "sb2": np.concatenate([x[m + "expert_b2"], x[m + "shared_b2"][None]]),
    }
    nc = _bacc.Bacc("TRN2", target_bir_lowering=False, num_devices=1)
    sent, aps = {}, {}
    for name, v in arrays.items():
        v = np.ascontiguousarray(v)
        sent[f"in_{name}"] = v
        aps[name] = nc.dram_tensor(f"in_{name}", v.shape, _mybir.dt.from_np(v.dtype), kind="ExternalInput").ap()
    aps["out"] = nc.dram_tensor("out", (N, P), _mybir.dt.float32, kind="ExternalOutput").ap()
    build(nc, aps)
    r = _run(nc, [sent], core_ids=[0])
    return r.results[0]["out"].reshape(B, T, P)
```
